# Optimizing a Trainium2 kernel written in Bass

```python
import numpy as np
import jax
import jax.numpy as jnp

def _softmax(x, axis=-1):
    return jax.nn.softmax(x, axis=axis)

def _gelu(x):
    return jax.nn.gelu(x, approximate=True)

def _silu(x):
    return jax.nn.silu(x)

def _sigmoid(x):
    return jax.nn.sigmoid(x)

def _layernorm(x, axis=-1, eps=1e-05):
    m = jnp.mean(x, axis=axis, keepdims=True)
    v = jnp.var(x, axis=axis, keepdims=True)
    return (x - m) / jnp.sqrt(v + eps)

def _scatter_add(tgt, idx, src, axis=0):
    return tgt.at[idx].add(src)

def _segment_sum(src, seg, n):
    return jax.ops.segment_sum(src, seg, n)
kernel_name = 'mk_gnn_resnorm_d4_gnn_r16_2a0c18'

def setup_inputs(seed: int=0):
    np.random.seed(seed)
    _w = jnp.asarray

    def _rec_inputs():
        import jax
        import jax.numpy as jnp
        _gk = jax.random.key(seed)
        x = -0.0003713 + 1 * jax.random.normal(jax.random.fold_in(_gk, 1), (6250, 128), jnp.float32)
        src = jax.random.randint(jax.random.fold_in(_gk, 2), (100000,), 0, 6250, jnp.int32)
        dst = jax.random.randint(jax.random.fold_in(_gk, 3), (100000,), 0, 6250, jnp.int32)
        _o = jnp.argsort(dst, stable=True)
        src = src[_o]
        dst = dst[_o]
        edge_attr_16 = 0.000254156 + 0.999948 * jax.random.normal(jax.random.fold_in(_gk, 13), (100000, 16), jnp.float32)
        edge_type_8 = jax.random.randint(jax.random.fold_in(_gk, 15), (100000,), 0, 8, jnp.int32)
        edge_weight = jax.random.uniform(jax.random.fold_in(_gk, 16), (100000,), jnp.float32, 0.0, 1)
        return (x, src, dst, edge_attr_16, edge_type_8, edge_weight)
    x, src, dst, edge_attr_16, edge_type_8, edge_weight = _rec_inputs()

    def _L0_gnn_setup():
        import jax, jax.numpy as jnp
        import numpy as np
        N_NODES = 6250
        N_EDGES = 50000
        D_IN = 128
        D_OUT = 128
        E_DIM = 16
        key = jax.random.key(seed)
        k1, k2, k3, k4, k5 = jax.random.split(key, 5)
        x = jax.random.normal(k1, (N_NODES, D_IN), dtype=jnp.float32)
        edge_index = jax.random.randint(k2, (2, N_EDGES), 0, N_NODES, dtype=jnp.int64)
        edge_attr = jax.random.normal(k3, (N_EDGES, E_DIM), dtype=jnp.float32)
        W = jax.random.uniform(k4, (D_IN, D_OUT), dtype=jnp.float32, minval=-1.0, maxval=1.0) * float(np.sqrt(6.0 / (D_IN + D_OUT)))
        edge_w = jax.random.uniform(k5, (E_DIM, D_OUT), dtype=jnp.float32, minval=-1.0, maxval=1.0) * float(np.sqrt(6.0 / (E_DIM + D_OUT)))
        b = jnp.zeros((D_OUT,), dtype=jnp.float32)
        return {'x': x, 'edge_index': edge_index, 'edge_attr': edge_attr, 'W': W, 'edge_w': edge_w, 'b': b}
    _L0_gnn_all = _L0_gnn_setup()
    _L0_gnn_in = {k: v for k, v in _L0_gnn_all.items() if k in ('W', 'edge_w', 'b')}
    del _L0_gnn_all

    def _L1_gnn_setup():
        import jax, jax.numpy as jnp
        import numpy as np
        N_NODES = 3125
        N_EDGES = 50000
        N_RELS = 8
        IN_FEATS = 128
        OUT_FEATS = 128
        key = jax.random.key(seed)
        k = jax.random.split(key, 7)
        stdv = 1.0 / np.sqrt(IN_FEATS)
        return {'h': jax.random.normal(k[0], (N_NODES, IN_FEATS), dtype=jnp.float32), 'edge_norm': jax.random.uniform(k[1], (N_EDGES,), dtype=jnp.float32), 'edge_types': jax.random.randint(k[2], (N_EDGES,), 0, N_RELS, dtype=jnp.int32), 'src': jax.random.randint(k[3], (N_EDGES,), 0, N_NODES, dtype=jnp.int32), 'dst': jax.random.randint(k[4], (N_EDGES,), 0, N_NODES, dtype=jnp.int32), 'weight': jax.random.uniform(k[5], (N_RELS, IN_FEATS, OUT_FEATS), jnp.float32, -stdv, stdv), 'bias': jax.random.uniform(k[6], (OUT_FEATS,), jnp.float32, -stdv, stdv)}
    _L1_gnn_all = _L1_gnn_setup()
    _L1_gnn_in = {k: v for k, v in _L1_gnn_all.items() if k in ('weight', 'bias')}
    del _L1_gnn_all

    def _L2_gnn_setup():
        import jax, jax.numpy as jnp
        import numpy as np
        N_NODES = 3125
        N_EDGES = 50000
        IN_CH = 128
        OUT_CH = 128
        MLP_HID = 64
        key = jax.random.key(seed)
        ks = jax.random.split(key, 8)
        x = jax.random.normal(ks[0], (N_NODES, IN_CH), dtype=jnp.float32)
        edge_index = jax.random.randint(ks[1], (2, N_EDGES), 0, N_NODES, dtype=jnp.int64)
        s1 = 1.0 / np.sqrt(2 * IN_CH)
        mlp_w1 = jax.random.uniform(ks[2], (2 * IN_CH, MLP_HID), jnp.float32, -s1, s1)
        mlp_b1 = jax.random.uniform(ks[3], (MLP_HID,), jnp.float32, -s1, s1)
        s2 = 1.0 / np.sqrt(MLP_HID)
        mlp_w2 = jax.random.uniform(ks[4], (MLP_HID, 1), jnp.float32, -s2, s2)
        mlp_b2 = jax.random.uniform(ks[5], (1,), jnp.float32, -s2, s2)
        s3 = 1.0 / np.sqrt(IN_CH)
        conv_w = jax.random.uniform(ks[6], (IN_CH, OUT_CH), jnp.float32, -s3, s3)
        conv_b = jnp.zeros((OUT_CH,), jnp.float32)
        return {'x': x, 'edge_index': edge_index, 'mlp_w1': mlp_w1, 'mlp_b1': mlp_b1, 'mlp_w2': mlp_w2, 'mlp_b2': mlp_b2, 'conv_w': conv_w, 'conv_b': conv_b}
    _L2_gnn_all = _L2_gnn_setup()
    _L2_gnn_in = {k: v for k, v in _L2_gnn_all.items() if k in ('mlp_w1', 'mlp_b1', 'mlp_w2', 'mlp_b2', 'conv_w', 'conv_b')}
    del _L2_gnn_all

    def _L3_gnn_setup():
        import jax, jax.numpy as jnp
        import numpy as np
        N_NODES = 3125
        N_EDGES = 37500
        HIDDEN = 128
        N_LAYERS = 4
        key = jax.random.key(seed)
        ks = jax.random.split(key, 6)
        x = jax.random.normal(ks[0], (N_NODES, HIDDEN), dtype=jnp.float32)
        edge_index = jax.random.randint(ks[1], (2, N_EDGES), 0, N_NODES, dtype=jnp.int64)
        batch = jax.random.randint(ks[2], (N_NODES,), 0, 64, dtype=jnp.int64)
        scale = 1.0 / np.sqrt(HIDDEN)
        W1 = jax.random.normal(ks[3], (N_LAYERS, HIDDEN, HIDDEN), dtype=jnp.float32) * scale
        b1 = jnp.zeros((N_LAYERS, HIDDEN), dtype=jnp.float32)
        W2 = jax.random.normal(ks[4], (N_LAYERS, HIDDEN, HIDDEN), dtype=jnp.float32) * scale
        b2 = jnp.zeros((N_LAYERS, HIDDEN), dtype=jnp.float32)
        return {'x': x, 'edge_index': edge_index, 'batch': batch, 'W1': W1, 'b1': b1, 'W2': W2, 'b2': b2}
    _L3_gnn_all = _L3_gnn_setup()
    _L3_gnn_in = {k: v for k, v in _L3_gnn_all.items() if k in ('W1', 'b1', 'W2', 'b2')}
    del _L3_gnn_all
    return {'x': x, 'src': src, 'dst': dst, 'edge_attr_16': edge_attr_16, 'edge_type_8': edge_type_8, 'edge_weight': edge_weight, 'L0_gnn_W': _L0_gnn_in['W'], 'L0_gnn_edge_w': _L0_gnn_in['edge_w'], 'L0_gnn_b': _L0_gnn_in['b'], 'L1_gnn_weight': _L1_gnn_in['weight'], 'L1_gnn_bias': _L1_gnn_in['bias'], 'L2_gnn_mlp_w1': _L2_gnn_in['mlp_w1'], 'L2_gnn_mlp_b1': _L2_gnn_in['mlp_b1'], 'L2_gnn_mlp_w2': _L2_gnn_in['mlp_w2'], 'L2_gnn_mlp_b2': _L2_gnn_in['mlp_b2'], 'L2_gnn_conv_w': _L2_gnn_in['conv_w'], 'L2_gnn_conv_b': _L2_gnn_in['conv_b'], 'L3_gnn_W1': _L3_gnn_in['W1'], 'L3_gnn_b1': _L3_gnn_in['b1'], 'L3_gnn_W2': _L3_gnn_in['W2'], 'L3_gnn_b2': _L3_gnn_in['b2']}

def reference(x, src, dst, edge_attr_16, edge_type_8, edge_weight, L0_gnn_W, L0_gnn_edge_w, L0_gnn_b, L1_gnn_weight, L1_gnn_bias, L2_gnn_mlp_w1, L2_gnn_mlp_b1, L2_gnn_mlp_w2, L2_gnn_mlp_b2, L2_gnn_conv_w, L2_gnn_conv_b, L3_gnn_W1, L3_gnn_b1, L3_gnn_W2, L3_gnn_b2):
    import jax
    import jax.numpy as jnp

    def _L0_gnn_ref(x, edge_index, edge_attr, W, edge_w, b):
        import jax, jax.numpy as jnp
        import numpy as np
        N_NODES = 6250
        N_EDGES = 50000
        D_IN = 128
        D_OUT = 128
        E_DIM = 16
        src, dst = (edge_index[0], edge_index[1])
        xw = x @ W
        ew = edge_attr @ edge_w
        msg = xw[src] * ew
        out = jax.ops.segment_sum(msg, dst, num_segments=x.shape[0])
        out = out + b
        return out

    def _L1_gnn_ref(h, edge_norm, edge_types, src, dst, weight, bias):
        import jax, jax.numpy as jnp
        import numpy as np
        N_NODES = 3125
        N_EDGES = 50000
        N_RELS = 8
        IN_FEATS = 128
        OUT_FEATS = 128
        ht = jnp.einsum('ni,rio->nro', h, weight)
        msg = ht[src, edge_types] * edge_norm[:, None]
        out = jax.ops.segment_sum(msg, dst, num_segments=h.shape[0])
        out = out + bias
        return jax.nn.relu(out)

    def _L2_gnn_ref(x, edge_index, mlp_w1, mlp_b1, mlp_w2, mlp_b2, conv_w, conv_b):
        import jax, jax.numpy as jnp
        import numpy as np
        N_NODES = 3125
        N_EDGES = 50000
        IN_CH = 128
        OUT_CH = 128
        MLP_HID = 64
        n = x.shape[0]
        row, col = (edge_index[0], edge_index[1])
        edge_feat = jnp.concatenate([x[row], x[col]], axis=-1)
        h = jax.nn.gelu(edge_feat @ mlp_w1 + mlp_b1, approximate=False)
        edge_weight = jax.nn.sigmoid(h @ mlp_w2 + mlp_b2)[:, 0]
        loop = jnp.arange(n, dtype=row.dtype)
        row_f = jnp.concatenate([row, loop])
        col_f = jnp.concatenate([col, loop])
        ew_f = jnp.concatenate([edge_weight, jnp.ones((n,), x.dtype)])
        deg = jax.ops.segment_sum(ew_f, col_f, num_segments=n)
        dinv = jnp.where(deg > 0, jax.lax.rsqrt(deg), 0.0)
        norm = dinv[row_f] * ew_f * dinv[col_f]
        xt = x @ conv_w
        msg = xt[row_f] * norm[:, None]
        out = jax.ops.segment_sum(msg, col_f, num_segments=n)
        return out + conv_b

    def _L3_gnn_ref(x, edge_index, batch, W1, b1, W2, b2):
        import jax, jax.numpy as jnp
        import numpy as np
        N_NODES = 3125
        N_EDGES = 37500
        HIDDEN = 128
        N_LAYERS = 4
        src = edge_index[0]
        dst = edge_index[1]
        n = x.shape[0]
        for l in range(N_LAYERS):
            agg = jax.ops.segment_sum(x[src], dst, num_segments=n)
            h = x + agg
            h = jnp.maximum(h @ W1[l] + b1[l], 0.0)
            x = h @ W2[l] + b2[l]
        return x
    edge_index = jnp.stack([src, dst])
    batch0 = jnp.zeros((6250,), jnp.int32)
    x = _layernorm(x + _L0_gnn_ref(x, edge_index, edge_attr_16, L0_gnn_W, L0_gnn_edge_w, L0_gnn_b), axis=-1)
    x = _layernorm(x + _L1_gnn_ref(x, edge_weight, edge_type_8, src, dst, L1_gnn_weight, L1_gnn_bias), axis=-1)
    x = _layernorm(x + _L2_gnn_ref(x, edge_index, L2_gnn_mlp_w1, L2_gnn_mlp_b1, L2_gnn_mlp_w2, L2_gnn_mlp_b2, L2_gnn_conv_w, L2_gnn_conv_b), axis=-1)
    x = _layernorm(x + _L3_gnn_ref(x, edge_index, batch0, L3_gnn_W1, L3_gnn_b1, L3_gnn_W2, L3_gnn_b2), axis=-1)
    return x

_drawn_inputs = setup_inputs


def setup_inputs(seed=0):
    import zlib

    import numpy as np

    out = dict(_drawn_inputs(seed))
    spreads = {'L0_gnn_b': (0.0, 0.1),
     'L2_gnn_conv_b': (0.0, 0.1),
     'L3_gnn_b1': (0.0, 0.434),
     'L3_gnn_b2': (0.0, 0.312)}
    factors = {'edge_weight': 3.364,
     'L2_gnn_mlp_w1': 5.55,
     'L2_gnn_mlp_b1': 50.428,
     'L2_gnn_mlp_w2': 6.833}
    for name, (base, spread) in spreads.items():
        noise = np.random.default_rng([zlib.crc32(name.encode()), seed]).standard_normal(out[name].shape)
        drawn = base * np.exp(spread * noise) if base else spread * noise
        out[name] = jnp.asarray(drawn.astype(out[name].dtype))
    for name, factor in factors.items():
        out[name] = (out[name] * factor).astype(out[name].dtype)
    return out
```

```python
from contextlib import ExitStack

import concourse.bass as bass
from concourse import mybir

F32 = mybir.dt.float32
I32 = mybir.dt.int32
ALU = mybir.AluOpType
ACT = mybir.ActivationFunctionType
AXX = mybir.AxisListType.X

P = 128
D = 128
HID = 64
EDIM = 16
RELS = 8
LAYERS = 4
TPG = 8
GE = TPG * P
EPS = 1e-5


def gnn_program(nc, x, src, dst, edge_attr, edge_type, edge_weight, W0, edge_w, b0, W1r, bias1,
                mlp_w1, mlp_b1, mlp_w2, mlp_b2, conv_w, conv_b, L3W1, L3b1, L3W2, L3b2, out):
    N = x.shape[0]
    E = src.shape[0]
    NG = -(-E // GE)
    NIT = NG // 2
    FULL = E // GE
    TAIL = E - FULL * GE
    TAILP = TAIL // TPG
    NB = -(-N // P)
    NPAD = NB * P
    CB = 7
    NCH = NB // CB
    CW = CB * P
    LASTROWS = N - (NB - 1) * P
    MAXBASE = NPAD - P
    assert NG == 2 * NIT and NG == FULL + 1 and TAIL % TPG == 0 and NB == CB * NCH

    with ExitStack() as ctx:
        def sb(name, shape, dt=F32):
            return ctx.enter_context(nc.sbuf_tensor(name, shape, dt))

        def sem(name):
            return ctx.enter_context(nc.semaphore(name))

        def sem2(name):
            return [sem(f"{name}{b}") for b in range(2)]

        def scratch(name, shape):
            return nc.dram_tensor(name, shape, F32, kind="Internal").ap()

        xw_rows = scratch("xw_rows", (NPAD, D))
        ht_rows = scratch("ht_rows", (NPAD * RELS, D))
        a_rows = scratch("a_rows", (NPAD, HID))
        b_rows = scratch("b_rows", (NPAD, HID))
        xt_rows = scratch("xt_rows", (NPAD, D))
        x_rows = scratch("x_rows", (NPAD, D))

        iota = sb("iota", [P, NPAD])
        X = sb("X", [P, NPAD])
        XT2 = sb("XT2", [P, NPAD])
        acc = sb("acc", [P, NPAD])
        G = sb("G", [P, 2, GE])
        onehot = sb("onehot", [P, 2, GE])
        msg = sb("msg", [P, 2, GE])
        hid = sb("hid", [P, 2, TPG * HID])
        attr = sb("attr", [P, 2, TPG * EDIM])
        attrT = sb("attrT", [P, 2, P])
        bwin = sb("bwin", [P, 2, HID])
        srci = sb("srci", [P, NG * TPG + 2 * TPG], I32)
        reli = sb("reli", [P, NG * TPG], I32)
        dstf = sb("dstf", [P, NG * TPG])
        wedge = sb("wedge", [P, NG * TPG])
        ewt = sb("ewt", [P, NG * TPG])
        idx = sb("idx", [P, 2, TPG], I32)
        zed = sb("zed", [P, 2, TPG])
        tanhz = sb("tanhz", [P, 2, TPG])
        ews = sb("ews", [P, 2, TPG])
        stT = sb("stT", [P, CW])
        y = sb("y", [P, CW])
        sq = sb("sq", [P, CW])
        xn = sb("xn", [P, CW])
        xTs = sb("xTs", [P, CW])
        ident = sb("ident", [P, P])
        pcol = sb("pcol", [P, 1])
        stat = sb("stat", [P, 4, CB])
        dinv = sb("dinv", [P, NB])
        droot = sb("droot", [P, NB])
        onec = sb("onec", [P, 1])
        small = sb("small", [P, 8])
        rowf = sb("rowf", [1, 4, NG])
        basei = sb("basei", [1, NG], I32)
        nwini = sb("nwini", [1, 2], I32)
        one11 = sb("one11", [1, 1])
        W0s = sb("W0s", [P, D])
        EWb = sb("EWb", [P, TPG, D])
        W1s = sb("W1s", [P, RELS, D])
        W2s = sb("W2s", [P, 2 * HID + D])
        WA = sb("WA", [P, D])
        WB = sb("WB", [P, D])
        b0r = sb("b0r", [P, D])
        b1r = sb("b1r", [P, D])
        cbr = sb("cbr", [P, D])
        mb1r = sb("mb1r", [P, HID])
        w2r = sb("w2r", [P, HID])
        mb2r = sb("mb2r", [P, 1])
        l3b2r = sb("l3b2r", [P, D])
        l3b1c = sb("l3b1c", [P, 1])
        l3b2c = sb("l3b2c", [P, 1])

        raw = [XT2[:, k * GE:(k + 1) * GE] for k in range(4)]
        RSRC, RDST, RTYP, RWGT = range(4)
        xchunks = X[:, :].rearrange("p (b f) -> p b f", f=D)

        psS = [ctx.enter_context(nc.psum_tensor(f"psS{b}", [P, 512], F32)) for b in range(2)]
        psA = ctx.enter_context(nc.psum_tensor("psA", [P, 1024], F32))
        ps4 = ctx.enter_context(nc.psum_tensor("ps4", [P, 2048], F32))

        s_load = sem("s_load")
        s_wload = sem("s_wload")
        s_xload = sem("s_xload")
        s_fill = sem("s_fill")
        s_iota = sem("s_iota")
        s_ident = sem("s_ident")
        s_chain = sem("s_chain")
        s_prep = sem("s_prep")
        s_plan = sem("s_plan")
        s_pt = sem("s_pt")
        s_pe = sem("s_pe")
        s_zero = sem("s_zero")
        s_gate = sem("s_gate")

        r_idx = sem2("r_idx")
        r_ohraw = sem2("r_ohraw")
        r_oh = sem2("r_oh")
        r_seg = sem2("r_seg")
        r_acc = sem2("r_acc")

        class Round:
            def __init__(self, name, number, weighted=0):
                self.g0 = number * NIT
                self.w0 = weighted * NIT
                self.gathered = sem2(name + "_gath")

        R0, R1, R2b, R3 = Round("r0", 0), Round("r1", 1, 0), Round("r2b", 2, 1), Round("r3", 3)
        s_attr = sem2("s_attr")
        s_attrp = sem2("s_attrp")
        s_attrT = sem2("s_attrT")
        s_ew = sem2("s_ew")
        s_msg = sem2("s_msg")
        m_idx = sem2("m_idx")
        m_gath = sem2("m_gath")
        m_oh = sem2("m_oh")
        m_tp = sem2("m_tp")
        m_ohT = sem2("m_ohT")
        m_bwin = sem2("m_bwin")
        m_exp = sem2("m_exp")
        m_h = sem2("m_h")
        m_gelu = sem2("m_gelu")
        m_dot = sem2("m_dot")
        m_tanh = sem2("m_tanh")
        m_ew = sem2("m_ew")
        m_ewt = sem("m_ewt")
        s_half = sem("s_half")
        m_oh2 = sem2("m_oh2")
        m_deg = sem2("m_deg")
        m_dacc = sem2("m_dacc")
        d_t = sem("d_t")
        d_sq = sem("d_sq")
        d_v = sem("d_v")
        d_out = sem("d_out")

        def phase(name, steps, kinds):
            p = {kind: sem(f"{name}_{kind}") for kind in kinds.split()}
            return {**p, "steps": steps, "centred": steps - 3, "varied": steps - 1}

        norm = "dv sq xn xs "
        N0 = phase("n0", 0, "xn t2 xT tb ev dma stored")
        N1 = phase("n1", 8, norm + "st t1 t2 xT tb ev eva dma dmb stored storedb")
        N2 = phase("n2", 8, norm + "st t1 t2 xT tb ev eva eva2 dma dmb stored")
        N3 = phase("n3", 10, norm + "st t1 t2 eva dma stored")
        NF = phase("nf", 7, norm + "dma dmb")
        l_x2 = sem("l_x2")
        l_w = sem("l_w")
        l_h = sem("l_h")
        l_relu = sem("l_relu")
        l_o = sem("l_o")
        l_acc = sem("l_acc")
        l_xo = sem("l_xo")
        l_dma = sem("l_dma")
        l_stored = sem("l_stored")

        def pass_waits(eng):
            eng.sem_inc(s_gate, 1)

        def as_row(v):
            return v.rearrange("(a n) -> a n", a=1)

        def window(base, w):
            if isinstance(w, int) and w == 0:
                return bass.ds(base, P)
            at = nc.s_assert_within(base + w * P, 0, MAXBASE, skip_runtime_bounds_check_because=
                                    "more than one window only from base 0")
            return bass.ds(at, P)

        def window_count(eng):
            return (eng.value_load(nwini[0:1, 0:1], min_val=1, max_val=NB),
                    eng.value_load(nwini[0:1, 1:2], min_val=0, max_val=NB - 1))

        def blocks(ap):
            return ap.rearrange("p (b f) -> p b f", f=D)

        ALLW = 16 * (TPG + 11)

        block = ctx.enter_context(nc.Block())


        @block.sync
        def _(sp):
            sp.wait_ge(s_fill, 1)
            for r, a in ((RSRC, src), (RDST, dst), (RTYP, edge_type), (RWGT, edge_weight)):
                v = raw[r] if r == RWGT else raw[r].bitcast(I32)
                sp.dma_start(v[0:FULL, :], a[0:FULL * GE].rearrange("(g e) -> g e", e=GE)).then_inc(s_load, 16)
                sp.dma_start(v[FULL:FULL + 1, 0:TAIL], as_row(a[FULL * GE:E])).then_inc(s_load, 16)
            sp.dma_start(blocks(X[:, 0:(NB - 1) * P]), x[0:(NB - 1) * P, :].rearrange("(b p) f -> p b f", p=P)).then_inc(s_xload, 16)
            sp.dma_start(X[0:LASTROWS, (NB - 1) * P:NPAD], x[(NB - 1) * P:N, :]).then_inc(s_xload, 16)
            for j in range(TPG):
                sp.dma_start(EWb[j * EDIM:(j + 1) * EDIM, j, :], edge_w[:, :]).then_inc(s_wload, 16)
            loads = [(W0s[:, :], W0[:, :]), (W1s[:, :, :], W1r.rearrange("r i o -> i r o")),
                     (W2s[:, 0:HID], mlp_w1[0:D, :]), (W2s[:, HID:2 * HID], mlp_w1[D:2 * D, :]),
                     (W2s[:, 2 * HID:], conv_w[:, :]),
                     (b0r[:, :], as_row(b0).broadcast_to([P, D])), (b1r[:, :], as_row(bias1).broadcast_to([P, D])),
                     (cbr[:, :], as_row(conv_b).broadcast_to([P, D])), (mb1r[:, :], as_row(mlp_b1).broadcast_to([P, HID])),
                     (w2r[:, :], mlp_w2.rearrange("h a -> a h").broadcast_to([P, HID])),
                     (mb2r[:, :], as_row(mlp_b2).broadcast_to([P, 1]))]
            for o, i in loads:
                sp.dma_start(o, i).then_inc(s_wload, 16)

            def rows_of(table, c):
                return table.rearrange("(b p) f -> p b f", p=P)[:, bass.ds(c * CB, CB), :]

            for s in (N0["stored"], N1["stored"], N1["storedb"], N2["stored"], N3["stored"], l_stored):
                sp.sem_inc(s, 1)

            with sp.Fori(0, NCH) as c:
                sp.wait_ge(N0["ev"], c + 2)
                pass_waits(sp)
                sp.dma_start(rows_of(xw_rows, c), blocks(msg[:, 0, 0:CW])).then_inc(N0["dma"], 16)
                sp.wait_ge(N0["dma"], 16 * c + 16)
                sp.sem_inc(N0["stored"], 1)

            def load_attr(b, it, g, parts):
                sp.wait_ge(s_attrp[b], it + 1)
                pass_waits(sp)
                sp.dma_start(attr[0:parts, b, :],
                             edge_attr[bass.ds(g * GE, parts * TPG), :].rearrange("(p j) k -> p (j k)", j=TPG)
                             ).then_inc(s_attr[b], 16)
            with sp.Fori(0, NIT - 1) as it:
                for b in range(2):
                    load_attr(b, it, it * 2 + b, P)
            load_attr(0, NIT - 1, NG - 2, P)
            load_attr(1, NIT - 1, NG - 1, TAILP)

            ht = ht_rows.rearrange("(b p r) f -> b p (r f)", p=P, r=RELS)
            with sp.Fori(0, NCH) as c:
                def stored(k):
                    if k % 2:
                        sp.wait_ge(N1["dmb"], 16 * (c * 3 + k // 2) + 16)
                        sp.sem_inc(N1["storedb"], 1)
                    else:
                        sp.wait_ge(N1["dma"], 16 * (c * 4 + k // 2) + 16)
                        sp.sem_inc(N1["stored"], 1)
                for k in range(CB):
                    ready, done, per = ((N1["ev"], N1["dma"], 4), (N1["eva"], N1["dmb"], 3))[k % 2]
                    sp.wait_ge(ready, c * per + k // 2 + 2)
                    pass_waits(sp)
                    sp.dma_start(ht[bass.ds(c * CB + k, 1)].rearrange("a p n -> (a p) n"), msg[:, k % 2, :]).then_inc(done, 16)
                    if k:
                        stored(k - 1)
                stored(CB - 1)

            with sp.Fori(0, NCH) as c:
                sp.wait_ge(N2["ev"], c + 2)
                pass_waits(sp)
                sp.dma_start(rows_of(a_rows, c), msg[:, 0, 0:CB * HID].rearrange("p (b f) -> p b f", f=HID)).then_inc(N2["dma"], 16)
                sp.wait_ge(N2["eva"], c + 1)
                pass_waits(sp)
                sp.dma_start(rows_of(b_rows, c), msg[:, 1, 0:CB * HID].rearrange("p (b f) -> p b f", f=HID)).then_inc(N2["dmb"], 16)
                sp.wait_ge(N2["dma"], 16 * c + 16)
                sp.wait_ge(N2["dmb"], 16 * c + 16)
                sp.sem_inc(N2["stored"], 1)

            nwin, more = window_count(sp)

            def load_window(b, base, w, q):
                sp.wait_ge(m_exp[b], q + 1)
                pass_waits(sp)
                sp.dma_start(bwin[:, b, :], b_rows[window(base, w), :]).then_inc(m_bwin[b], 16)
            with sp.Fori(0, NIT) as it:
                bases = [sp.value_load(basei[0:1, bass.ds(it * 2 + b, 1)], min_val=0, max_val=MAXBASE) for b in range(2)]
                for b in range(2):
                    load_window(b, bases[b], 0, it * nwin)
                for b in range(2):
                    with sp.If(more > 0):
                        with sp.Fori(1, more + 1) as w:
                            load_window(b, bases[b], w, it * nwin + w)

            sp.wait_ge(d_v, 2)
            sp.dma_start(xt_rows.rearrange("(b p) f -> p b f", p=P), blocks(XT2[:, :])).then_inc(d_out, 16)

            with sp.Fori(0, NCH) as c:
                sp.wait_ge(N3["xn"], c + 1)
                pass_waits(sp)
                sp.dma_start(rows_of(x_rows, c), blocks(xn[:, :])).then_inc(N3["dma"], 16)
                sp.wait_ge(N3["dma"], 16 * c + 16)
                sp.sem_inc(N3["stored"], 1)

            with sp.Fori(0, LAYERS) as l:
                sp.dma_start(WA[:, :], L3W1[bass.ds(l, 1)].rearrange("a i o -> (a i) o")).then_inc(l_w, 16)
                sp.dma_start(WB[:, :], L3W2[bass.ds(l, 1)].rearrange("a i o -> (a i) o")).then_inc(l_w, 16)
                sp.dma_start(l3b2r[:, :], L3b2[bass.ds(l, 1), :].broadcast_to([P, D])).then_inc(l_w, 16)
                sp.dma_start(l3b1c[:, :], L3b1[bass.ds(l, 1), :].rearrange("a f -> f a")).then_inc(l_w, 16)
                sp.dma_start(l3b2c[:, :], L3b2[bass.ds(l, 1), :].rearrange("a f -> f a")).then_inc(l_w, 16)
                with sp.Fori(0, NCH) as c:
                    sp.wait_ge(l_xo, l * NCH + c + 1)
                    pass_waits(sp)
                    sp.dma_start(rows_of(x_rows, c), blocks(y[:, :])).then_inc(l_dma, 16)
                    sp.wait_ge(l_dma, (l * NCH + c) * 16 + 16)
                    sp.sem_inc(l_stored, 1)
                sp.wait_ge(l_acc, l * NCH + NCH)
                pass_waits(sp)

            sp.wait_ge(NF["xs"], NCH)
            sp.dma_start(out[0:(NB - 1) * P, :].rearrange("(b p) f -> p b f", p=P), blocks(X[:, 0:(NB - 1) * P])).then_inc(NF["dma"], 16)
            sp.dma_start(out[(NB - 1) * P:N, :], X[0:LASTROWS, (NB - 1) * P:NPAD]).then_inc(NF["dmb"], 16)
            sp.wait_ge(NF["dma"], 16)
            sp.wait_ge(NF["dmb"], 16)

        @block.gpsimd
        def _(pool):
            pool.iota(iota[:, :], [[1, NPAD]], base=0, channel_multiplier=0,
                      allow_small_or_imprecise_dtypes=True).then_inc(s_iota, 1)
            pool.iota(pcol[:, :], [[0, 1]], base=0, channel_multiplier=1,
                      allow_small_or_imprecise_dtypes=True).then_inc(s_iota, 1)
            pool.memset(acc[:, :], 0.0).then_inc(s_zero, 1)

            def gathers(it, idx_ready, gathered, table, width):
                for b in range(2):
                    pool.wait_ge(idx_ready[b], it + 1)
                    pass_waits(pool)
                    for j in range(TPG):
                        pool.indirect_dma_start(G[:, b, j * width:(j + 1) * width], None, table[:, :],
                                                bass.IndirectOffsetOnAxis(ap=idx[:, b, j:j + 1], axis=0)
                                                ).then_inc(gathered[b], 16)

            def zero_acc(read, count):
                pool.wait_ge(read, count)
                pool.memset(acc[:, :], 0.0).then_inc(s_zero, 1)

            pool.wait_ge(N0["stored"], NCH + 1)
            with pool.Fori(0, NIT) as it:
                gathers(it, r_idx, R0.gathered, xw_rows, D)
            zero_acc(N1["st"], NCH)
            pool.wait_ge(N1["stored"], NCH * 4 + 1)
            pool.wait_ge(N1["storedb"], NCH * 3 + 1)
            with pool.Fori(0, NIT) as it:
                gathers(it + R1.g0, r_idx, R1.gathered, ht_rows, D)
            zero_acc(N2["st"], NCH)
            pool.wait_ge(N2["stored"], NCH + 1)
            with pool.Fori(0, NIT) as it:
                gathers(it, m_idx, m_gath, a_rows, HID)
            zero_acc(d_t, 1)
            pool.wait_ge(d_out, 16)
            with pool.Fori(0, NIT) as it:
                gathers(it + R2b.g0, r_idx, R2b.gathered, xt_rows, D)
            pool.wait_ge(N3["stored"], NCH + 1)
            with pool.Fori(0, LAYERS) as l:
                with pool.Fori(0, NIT) as it:
                    gathers(l * NIT + it + R3.g0, r_idx, R3.gathered, x_rows, D)
                pool.wait_ge(l_stored, l * NCH + NCH + 1)
                pass_waits(pool)

        @block.scalar
        def _(act):
            act.wait_ge(s_plan, 1)
            nwin, more = window_count(act)

            act.sem_inc(N1["eva"], 1)

            def stage_idx(b, it, free, count, idx_ready, lists):
                act.wait_ge(free[b], count + 1)
                pass_waits(act)
                act.copy(idx[:, b, :], lists[:, bass.ds(it * (2 * TPG) + b * TPG, TPG)]).then_inc(idx_ready[b], 1)

            def index_round(R, lists, l=0):
                with act.Fori(0, NIT) as it:
                    for b in range(2):
                        stage_idx(b, it, r_seg, (l * NIT + it + R.g0) * nwin, r_idx, lists)

            def norm_steps(p, c):
                act.wait_ge(p["dv"], c * p["steps"] + p["centred"])
                act.activation(sq[:, :], y[:, :], ACT.Square).then_inc(p["sq"], 1)
                act.wait_ge(p["dv"], c * p["steps"] + p["varied"])
                act.activation(stat[:, 2, :], stat[:, 1, :], ACT.Sqrt).then_inc(p["sq"], 1)
                act.wait_ge(p["xn"], c + 1)
                pass_waits(act)
                act.copy(X[:, bass.ds(c * CW, CW)], xn[:, :]).then_inc(p["xs"], 1)

            def stage_acc(p, c):
                act.copy(stT[:, :], acc[:, bass.ds(c * CW, CW)]).then_inc(p["st"], 1)

            def transposed(p, c):
                act.wait_ge(p["t2"], c + 1)
                act.copy(xTs[:, :], psA[:, 0:CW]).then_inc(p["xT"], 1)

            def summed(R):
                for b in range(2):
                    act.wait_ge(r_acc[b], (R.g0 + NIT) * nwin + 1)

            with act.Fori(0, NCH) as c:
                transposed(N0, c)

            with act.Fori(0, NIT) as it:
                for b in range(2):
                    stage_idx(b, it, r_seg, it * nwin, r_idx, srci)
                for b in range(2):
                    act.wait_ge(s_attrp[b], it + 2)
                    act.copy(attrT[:, b, :], psA[:, b * 512:b * 512 + P]).then_inc(s_attrT[b], 1)

            summed(R0)
            with act.Fori(0, NCH) as c:
                stage_acc(N1, c)
                norm_steps(N1, c)
                transposed(N1, c)
                for k in range(1, CB, 2):
                    act.wait_ge(N1["tb"], c * CB + k + 1)
                    act.wait_ge(N1["storedb"], c * 3 + k // 2 + 1)
                    act.copy(msg[:, 1, :], ps4[:, 1024:2048]).then_inc(N1["eva"], 1)

            index_round(R1, reli)

            summed(R1)
            with act.Fori(0, NCH) as c:
                stage_acc(N2, c)
                norm_steps(N2, c)
                transposed(N2, c)
                act.wait_ge(N2["tb"], c + 1)
                act.wait_ge(N2["ev"], c + 2)
                act.wait_ge(N2["stored"], c + 1)
                rows = ps4[:, 0:CB * 256].rearrange("p (b n) -> p b n", n=256)
                act.copy(msg[:, 1, 0:CB * HID].rearrange("p (b n) -> p b n", n=HID), rows[:, :, HID:2 * HID]).then_inc(N2["eva"], 1)
                act.copy(blocks(XT2[:, bass.ds(c * CW, CW)]), rows[:, :, 2 * HID:]).then_inc(N2["eva2"], 1)

            def turned_onehots(b, q):
                act.wait_ge(m_tp[b], q + 2)
                act.copy(msg[:, b, :], ps4[:, b * GE:(b + 1) * GE]).then_inc(m_ohT[b], 1)
            act.wait_ge(N2["stored"], NCH + 1)
            act.wait_ge(s_half, 1)
            for b in range(2):
                act.copy(idx[:, b, :], srci[:, b * TPG:(b + 1) * TPG]).then_inc(m_idx[b], 1)
            with act.Fori(0, NIT) as it:
                for b in range(2):
                    turned_onehots(b, it * nwin)
                for b in range(2):
                    with act.If(more > 0):
                        with act.Fori(1, more + 1) as w:
                            turned_onehots(b, it * nwin + w)
                    act.wait_ge(m_h[b], it * nwin + nwin + 1)
                    act.activation(hid[:, b, :], G[:, b, 0:TPG * HID], ACT.Gelu).then_inc(m_gelu[b], 1)
                    stage_idx(b, it + 1, m_gelu, it, m_idx, srci)
                    act.wait_ge(m_dot[b], it * 2 + 2)
                    act.activation(tanhz[:, b, :], zed[:, b, :], ACT.Tanh, bias=mb2r[:, :], scale=0.5).then_inc(m_tanh[b], 1)
            act.wait_ge(d_t, 1)
            act.activation(droot[:, :], ps4[:, 0:NB], ACT.Sqrt, bias=onec[:, :]).then_inc(d_sq, 1)

            index_round(R2b, srci)

            summed(R2b)
            with act.Fori(0, NCH) as c:
                stage_acc(N3, c)
                norm_steps(N3, c)
                act.wait_ge(N3["t2"], c + 1)
                pass_waits(act)
                act.copy(acc[:, bass.ds(c * CW, CW)], psA[:, 0:CW]).then_inc(N3["eva"], 1)

            with act.Fori(0, LAYERS) as l:
                index_round(R3, srci, l)
                with act.Fori(0, NCH) as c:
                    act.wait_ge(l_h, l * NCH + c + 1)
                    act.activation(xTs[:, :], psA[:, 0:CW], ACT.Relu, bias=l3b1c[:, :]).then_inc(l_relu, 1)
                    act.wait_ge(l_o, l * NCH + c + 1)
                    pass_waits(act)
                    act.activation(acc[:, bass.ds(c * CW, CW)], ps4[:, 1024:1024 + CW], ACT.Identity,
                                   bias=l3b2c[:, :]).then_inc(l_acc, 1)

            with act.Fori(0, NCH) as c:
                norm_steps(NF, c)

        @block.tensor
        def _(pe):
            pe.wait_ge(s_ident, 1)
            for r in range(4):
                pe.wait_ge(s_prep, r + 1)
                if r >= 1:
                    pe.wait_ge(s_pe, r)
                v = raw[r].rearrange("g (p j) -> g j p", j=TPG)
                for j in range(TPG):
                    m = pe.transpose(ps4[:, j * P:j * P + NG], v[0:NG, j, :], ident[0:NG, 0:NG])
                m.then_inc(s_pt, 1)
            pe.wait_ge(s_prep, 5)
            pe.transpose(psA[0:1, 0:NG], small[0:NG, 0:1], ident[0:NG, 0:NG])
            pe.transpose(psA[0:1, P:P + NG], small[0:NG, 1:2], ident[0:NG, 0:NG]).then_inc(s_pt, 1)
            pe.wait_ge(s_plan, 1)
            nwin, more = window_count(pe)
            pe.wait_ge(s_wload, ALLW)

            def turn_chunk(source, done):
                for k in range(CB):
                    m = pe.transpose(psA[:, k * P:(k + 1) * P], source[:, k * P:(k + 1) * P], ident[:, :])
                m.then_inc(done, 1)

            def window_sums(rows, b, q):
                pe.wait_ge(r_oh[b], q + 1)
                pe.wait_ge(r_acc[b], q + 1)
                for j in range(TPG):
                    m = pe.matmul(psS[b][:, 0:P], rows[:, b, j * P:(j + 1) * P], onehot[:, b, j * P:(j + 1) * P],
                                  start=(j == 0), stop=(j == TPG - 1))
                m.then_inc(r_seg[b], 1)

            def segment_sums(rows, b, q0):
                window_sums(rows, b, q0)
                with pe.If(more > 0):
                    with pe.Fori(1, more + 1) as w:
                        window_sums(rows, b, q0 + w)

            def plain_round(R, l=0):
                with pe.Fori(0, NIT) as it:
                    for b in range(2):
                        pe.wait_ge(R.gathered[b], (l * NIT + it) * (16 * TPG) + 16 * TPG)
                        segment_sums(G, b, (l * NIT + it + R.g0) * nwin)

            for b in range(2):
                pe.sem_inc(r_seg[b], 1)
                pe.sem_inc(s_attrp[b], 1)
                pe.sem_inc(m_tp[b], 1)
                pe.sem_inc(m_exp[b], 1)

            with pe.Fori(0, NCH) as c:
                pe.wait_ge(N0["xn"], c + 1)
                turn_chunk(xn, N0["t2"])
                pe.wait_ge(N0["xT"], c + 1)
                pe.wait_ge(N0["ev"], c + 1)
                for k in range(CB):
                    m = pe.matmul(ps4[:, k * P:(k + 1) * P], xTs[:, k * P:(k + 1) * P], W0s[:, :], start=True, stop=True)
                m.then_inc(N0["tb"], 1)

            pe.wait_ge(N0["ev"], NCH + 1)
            with pe.Fori(0, NIT) as it:
                for b in range(2):
                    pe.wait_ge(s_attr[b], 16 * it + 16)
                    pe.transpose(psA[:, b * 512:b * 512 + P], attr[:, b, :], ident[:, :]).then_inc(s_attrp[b], 1)
                for b in range(2):
                    pe.wait_ge(s_attrT[b], it + 1)
                    pe.wait_ge(s_msg[b], it + 1)
                    for h in range(2):
                        m = pe.matmul(ps4[:, b * GE + h * 512:b * GE + (h + 1) * 512], attrT[:, b, :],
                                      EWb[:, 4 * h:4 * h + 4, :].rearrange("p j f -> p (j f)"), start=True, stop=True)
                    m.then_inc(s_ew[b], 1)
                for b in range(2):
                    pe.wait_ge(s_msg[b], it + 2)
                    segment_sums(msg, b, it * nwin)

            with pe.Fori(0, NCH) as c:
                pe.wait_ge(N1["st"], c + 1)
                turn_chunk(stT, N1["t1"])
                pe.wait_ge(N1["xn"], c + 1)
                turn_chunk(xn, N1["t2"])
                pe.wait_ge(N1["xT"], c + 1)
                for k in range(CB):
                    if k % 2:
                        pe.wait_ge(N1["eva"], c * 3 + k // 2 + 1)
                    else:
                        pe.wait_ge(N1["ev"], c * 4 + k // 2 + 1)
                    for h in range(2):
                        m = pe.matmul(ps4[:, (k % 2) * 1024 + h * 512:(k % 2) * 1024 + (h + 1) * 512], xTs[:, k * P:(k + 1) * P],
                                      W1s[:, 4 * h:4 * h + 4, :].rearrange("p r f -> p (r f)"), start=True, stop=True)
                    m.then_inc(N1["tb"], 1)

            plain_round(R1)

            with pe.Fori(0, NCH) as c:
                pe.wait_ge(N2["st"], c + 1)
                turn_chunk(stT, N2["t1"])
                pe.wait_ge(N2["xn"], c + 1)
                turn_chunk(xn, N2["t2"])
                pe.wait_ge(N2["xT"], c + 1)
                pe.wait_ge(N2["ev"], c + 1)
                for k in range(CB):
                    m = pe.matmul(ps4[:, k * 256:(k + 1) * 256], xTs[:, k * P:(k + 1) * P], W2s[:, :], start=True, stop=True)
                m.then_inc(N2["tb"], 1)

            pe.wait_ge(N2["ev"], NCH + 1)
            pe.wait_ge(N2["eva2"], NCH)

            def expand(b, q):
                pe.wait_ge(m_oh[b], q + 1)
                for j in range(TPG):
                    m = pe.transpose(ps4[:, b * GE + j * P:b * GE + (j + 1) * P], onehot[:, b, j * P:(j + 1) * P], ident[:, :])
                m.then_inc(m_tp[b], 1)
                pe.wait_ge(m_ohT[b], q + 1)
                pe.wait_ge(m_bwin[b], 16 * q + 16)
                pe.wait_ge(m_h[b], q + 1)
                for j in range(TPG):
                    m = pe.matmul(psA[:, b * 512 + j * HID:b * 512 + (j + 1) * HID], msg[:, b, j * P:(j + 1) * P],
                                  bwin[:, b, :], start=True, stop=True)
                m.then_inc(m_exp[b], 1)

            def degrees(b, q):
                pe.wait_ge(m_dacc[b], q + 1)
                for j in range(TPG):
                    m = pe.matmul(psS[b][0:1, 0:P], ews[:, b, j:j + 1], onehot[:, b, j * P:(j + 1) * P],
                                  start=(j == 0), stop=(j == TPG - 1))
                m.then_inc(m_deg[b], 1)
            with pe.Fori(0, NIT) as it:
                for b in range(2):
                    expand(b, it * nwin)
                for b in range(2):
                    with pe.If(more > 0):
                        with pe.Fori(1, more + 1) as w:
                            expand(b, it * nwin + w)
                    pe.wait_ge(m_ew[b], it + 1)
                    degrees(b, it * nwin)
                    with pe.If(more > 0):
                        with pe.Fori(0, more) as w:
                            pe.wait_ge(m_oh2[b], it * more + w + 1)
                            degrees(b, it * nwin + w + 1)
            for b in range(2):
                pe.wait_ge(m_dacc[b], NIT * nwin + 1)
            for k in range(NB):
                m = pe.matmul(ps4[:, k:k + 1], acc[0:1, k * P:(k + 1) * P], one11[:, :], start=True, stop=True)
            m.then_inc(d_t, 1)

            plain_round(R2b)

            with pe.Fori(0, NCH) as c:
                pe.wait_ge(N3["st"], c + 1)
                turn_chunk(stT, N3["t1"])
                pe.wait_ge(N3["xn"], c + 1)
                turn_chunk(xn, N3["t2"])

            pe.wait_ge(N3["eva"], NCH)
            with pe.Fori(0, LAYERS) as l:
                plain_round(R3, l)
                pe.wait_ge(l_w, l * 80 + 80)
                for b in range(2):
                    pe.wait_ge(r_acc[b], (l * NIT + NIT + R3.g0) * nwin + 1)
                pass_waits(pe)
                with pe.Fori(0, NCH) as c:
                    for lo, hi in ((0, 512), (512, CW)):
                        m = pe.matmul(psA[:, lo:hi], WA[:, :], acc[:, bass.ds(c * CW + lo, hi - lo)], start=True, stop=True)
                    m.then_inc(l_h, 1)
                    pe.wait_ge(l_relu, l * NCH + c + 1)
                    for k in range(CB):
                        pe.matmul(ps4[:, k * P:(k + 1) * P], xTs[:, k * P:(k + 1) * P], WB[:, :], start=True, stop=True)
                    for lo, hi in ((0, 512), (512, CW)):
                        m = pe.matmul(ps4[:, 1024 + lo:1024 + hi], WB[:, :], xTs[:, lo:hi], start=True, stop=True)
                    m.then_inc(l_o, 1)
                    pe.wait_ge(l_acc, l * NCH + c + 1)
                    pe.wait_ge(l_xo, l * NCH + c + 1)

        @block.vector
        def _(dve):
            chain = [0]

            def link(ins):
                chain[0] += 1
                ins.then_inc(s_chain, 1)
                dve.wait_ge(s_chain, chain[0])

            for r in range(4):
                if r == RDST:
                    dve.memset(raw[r].bitcast(I32), -1)
                else:
                    dve.memset(raw[r], 0.0)
            dve.memset(EWb[:, :, :], 0.0)
            dve.memset(attr[:, :, :], 0.0)
            dve.memset(srci[:, NG * TPG:], 0)
            dve.memset(one11[:, :], 1.0)
            dve.memset(onec[:, :], 1.0)
            dve.memset(X[:, (NB - 1) * P:NPAD], 0.0).then_inc(s_fill, 1)
            for b in range(2):
                dve.sem_inc(r_acc[b], 1)
                dve.sem_inc(s_msg[b], 1)
                dve.sem_inc(m_h[b], 1)
                dve.sem_inc(m_dacc[b], 1)
            for p in (N0, N1, N2):
                dve.sem_inc(p["ev"], 1)
            dve.wait_ge(s_iota, 2)
            dve.tensor_scalar(ident[:, :], iota[:, 0:P], pcol[:, 0:1], None, ALU.is_equal).then_inc(s_ident, 1)
            dve.wait_ge(s_load, 16 * 8)
            link(dve.tensor_copy(raw[RSRC], raw[RSRC].bitcast(I32)))
            dve.sem_inc(s_prep, 1)
            link(dve.tensor_copy(raw[RDST], raw[RDST].bitcast(I32)))
            dve.sem_inc(s_prep, 1)
            link(dve.tensor_copy(raw[RTYP], raw[RTYP].bitcast(I32)))
            link(dve.scalar_tensor_tensor(raw[RTYP], raw[RSRC], float(RELS), raw[RTYP], ALU.mult, ALU.add))
            dve.sem_inc(s_prep, 2)
            link(dve.tensor_scalar(msg[0:NG, 0, :], raw[RDST][0:NG, :], 0.0, float(NPAD), ALU.is_lt, ALU.mult))
            link(dve.tensor_tensor(msg[0:NG, 0, :], msg[0:NG, 0, :], raw[RDST][0:NG, :], ALU.add))
            link(dve.tensor_reduce(small[0:NG, 0:1], msg[0:NG, 0, :], AXX, ALU.min))
            link(dve.tensor_reduce(small[0:NG, 1:2], raw[RDST][0:NG, :], AXX, ALU.max))
            dve.sem_inc(s_prep, 1)
            lists = ((RSRC, srci), (RDST, dstf), (RTYP, reli), (RWGT, wedge))
            for r, to in lists:
                dve.wait_ge(s_pt, r + 1)
                link(dve.tensor_copy(to[:, 0:NG * TPG].rearrange("p (g j) -> p j g", j=TPG),
                                     ps4[:, 0:GE].rearrange("p (j g) -> p j g", j=TPG)[:, :, 0:NG]))
                dve.sem_inc(s_pe, 1)
            dve.wait_ge(s_pt, 5)
            lo, hi, span, base = (rowf[:, k, :] for k in range(4))
            link(dve.tensor_copy(lo, psA[0:1, 0:NG]))
            link(dve.tensor_tensor(span, psA[0:1, P:P + NG], lo, ALU.subtract))
            link(dve.tensor_reduce(hi[:, 0:1], span, AXX, ALU.max))
            link(dve.tensor_scalar(hi[:, 1:2], hi[:, 0:1], float(P), None, ALU.is_lt))
            link(dve.tensor_scalar(base, lo, float(MAXBASE), hi[:, 1:2], ALU.min, ALU.mult))
            link(dve.tensor_copy(basei[:, :], base))
            link(dve.tensor_scalar(hi[:, 2:3], hi[:, 1:2], float(1 - NB), float(NB), ALU.mult, ALU.add))
            link(dve.tensor_scalar(hi[:, 3:4], hi[:, 2:3], -1.0, None, ALU.add))
            link(dve.tensor_copy(nwini[:, :], hi[:, 2:4]))
            dve.sem_inc(s_plan, 1)
            nwin, more = window_count(dve)
            dve.wait_ge(s_wload, ALLW)
            dve.tensor_scalar(mb2r[:, :], mb2r[:, :], 0.5, None, ALU.mult).then_inc(s_half, 1)

            def load_base(it, b):
                return dve.value_load(basei[0:1, bass.ds(it * 2 + b, 1)], min_val=0, max_val=MAXBASE)

            def tiles(ap):
                return ap.rearrange("p (j n) -> p j n", j=TPG)

            def columns(table, it, b):
                return table[:, bass.ds(it * (2 * TPG) + b * TPG, TPG)].unsqueeze(2).broadcast_to([P, TPG, P])

            def compare(b, base, w, it):
                return dve.tensor_tensor(tiles(onehot[:, b, :]), iota[:, window(base, w)].unsqueeze(1).broadcast_to([P, TPG, P]),
                                         columns(dstf, it, b), ALU.is_equal)

            def make_onehots(b, base, w, it, raw_count, weights):
                if weights is None:
                    compare(b, base, w, it).then_inc(r_oh[b], 1)
                else:
                    compare(b, base, w, it).then_inc(r_ohraw[b], 1)
                    dve.wait_ge(r_ohraw[b], raw_count + 1)
                    dve.tensor_tensor(tiles(onehot[:, b, :]), tiles(onehot[:, b, :]), columns(weights, it, b),
                                      ALU.mult).then_inc(r_oh[b], 1)

            def last_add(done, b, w, q, steps):
                if not isinstance(w, int):
                    dve.wait_ge(done[b], q + 1)
                elif b:
                    dve.wait_ge(done[0], steps + nwin + 1)
                else:
                    dve.wait_ge(done[1], steps + 1)

            def add_sums(b, base, w, q, q0):
                last_add(r_acc, b, w, q, q0)
                dve.wait_ge(r_seg[b], q + 2)
                at = acc[:, window(base, w)]
                dve.tensor_tensor(at, at, psS[b][:, 0:P], ALU.add).then_inc(r_acc[b], 1)

            def round_(R, weights, l=0, messages=False):
                with dve.Fori(0, NIT) as it:
                    bases = []
                    q = (l * NIT + it + R.g0) * nwin
                    qw = (it + R.w0) * nwin
                    for b in range(2):
                        bases.append(load_base(it, b))
                        make_onehots(b, bases[b], 0, it, qw, weights)
                    for b in range(2):
                        if messages:
                            dve.wait_ge(R.gathered[b], it * (16 * TPG) + 16 * TPG)
                            dve.wait_ge(s_ew[b], it + 1)
                            dve.tensor_tensor(msg[:, b, :], G[:, b, :], ps4[:, b * GE:(b + 1) * GE], ALU.mult).then_inc(s_msg[b], 1)
                        add_sums(b, bases[b], 0, q, q)
                        with dve.If(more > 0):
                            with dve.Fori(1, more + 1) as w:
                                make_onehots(b, bases[b], w, it, qw + w, weights)
                                add_sums(b, bases[b], w, q + w, q)

            def spread(ap):
                return ap.unsqueeze(1).broadcast_to([P, CB, D])

            def per_node(ap):
                return ap.unsqueeze(2).broadcast_to([P, CB, D])

            def stepper(p, c):
                k = [0]

                def step(ins):
                    k[0] += 1
                    ins.then_inc(p["dv"], 1)
                    dve.wait_ge(p["dv"], c * p["steps"] + k[0])
                return step, k

            def normalise(p, c, step, k):
                y3 = blocks(y[:, :])
                step(dve.tensor_reduce(stat[:, 0, :], y3, AXX, ALU.add))
                step(dve.tensor_scalar(stat[:, 0, :], stat[:, 0, :], -1.0 / D, None, ALU.mult))
                step(dve.tensor_tensor(y3, y3, per_node(stat[:, 0, :]), ALU.add))
                assert k[0] == p["centred"]
                dve.wait_ge(p["sq"], c * 2 + 1)
                step(dve.tensor_reduce(stat[:, 1, :], blocks(sq[:, :]), AXX, ALU.add))
                step(dve.tensor_scalar(stat[:, 1, :], stat[:, 1, :], 1.0 / D, EPS, ALU.mult, ALU.add))
                assert k[0] == p["varied"]
                dve.wait_ge(p["sq"], c * 2 + 2)
                step(dve.reciprocal(stat[:, 3, :], stat[:, 2, :]))
                assert k[0] == p["steps"]
                if p is N3:
                    dve.wait_ge(N3["stored"], c + 1)
                dve.tensor_tensor(blocks(xn[:, :]), y3, per_node(stat[:, 3, :]), ALU.mult).then_inc(p["xn"], 1)

            def chunk(table, c):
                return table[:, bass.ds(c * CW, CW)]

            dve.wait_ge(s_xload, 32)
            with dve.Fori(0, NCH) as c:
                dve.tensor_copy(xn[:, :], chunk(X, c)).then_inc(N0["xn"], 1)
                dve.wait_ge(N0["tb"], c + 1)
                dve.wait_ge(N0["stored"], c + 1)
                dve.tensor_copy(msg[:, 0, 0:CW], ps4[:, 0:CW]).then_inc(N0["ev"], 1)

            dve.wait_ge(N0["stored"], NCH + 1)
            dve.wait_ge(s_zero, 1)
            round_(R0, None, messages=True)

            with dve.Fori(0, NCH) as c:
                step, k = stepper(N1, c)
                dve.wait_ge(N1["t1"], c + 1)
                step(dve.tensor_tensor(y[:, :], psA[:, 0:CW], chunk(X, c), ALU.add))
                step(dve.tensor_tensor(blocks(y[:, :]), blocks(y[:, :]), spread(b0r[:, :]), ALU.add))
                normalise(N1, c, step, k)
                for k in range(0, CB, 2):
                    dve.wait_ge(N1["tb"], c * CB + k + 1)
                    dve.wait_ge(N1["stored"], c * 4 + k // 2 + 1)
                    dve.tensor_copy(msg[:, 0, :], ps4[:, 0:1024]).then_inc(N1["ev"], 1)

            dve.wait_ge(s_zero, 2)
            round_(R1, wedge)

            with dve.Fori(0, NCH) as c:
                step, k = stepper(N2, c)
                dve.wait_ge(N2["t1"], c + 1)
                step(dve.tensor_tensor(blocks(y[:, :]), blocks(psA[:, 0:CW]), spread(b1r[:, :]), ALU.add))
                step(dve.scalar_tensor_tensor(y[:, :], y[:, :], 0.0, chunk(X, c), ALU.max, ALU.add))
                normalise(N2, c, step, k)
                dve.wait_ge(N2["tb"], c + 1)
                dve.wait_ge(N2["stored"], c + 1)
                dve.tensor_tensor(msg[:, 0, 0:CB * HID].rearrange("p (b n) -> p b n", n=HID),
                                  ps4[:, 0:CB * 256].rearrange("p (b n) -> p b n", n=256)[:, :, 0:HID],
                                  mb1r[:, :].unsqueeze(1).broadcast_to([P, CB, HID]), ALU.add).then_inc(N2["ev"], 1)

            dve.wait_ge(s_zero, 3)

            def add_expanded(b, q):
                dve.wait_ge(m_exp[b], q + 2)
                h = G[:, b, 0:TPG * HID]
                dve.tensor_tensor(h, h, psA[:, b * 512:b * 512 + TPG * HID], ALU.add).then_inc(m_h[b], 1)

            def add_degrees(b, base, w, q, q0, first):
                last_add(m_dacc, b, 0 if first else w, q, q0)
                dve.wait_ge(m_deg[b], q + 1)
                at = acc[0:1, window(base, w)]
                dve.tensor_tensor(at, at, psS[b][0:1, 0:P], ALU.add).then_inc(m_dacc[b], 1)

            with dve.Fori(0, NIT) as it:
                bases = []
                q = it * nwin
                for b in range(2):
                    bases.append(load_base(it, b))
                    compare(b, bases[b], 0, it).then_inc(m_oh[b], 1)
                for b in range(2):
                    dve.wait_ge(m_gath[b], it * (16 * TPG) + 16 * TPG)
                    add_expanded(b, q)
                    with dve.If(more > 0):
                        with dve.Fori(1, more + 1) as w:
                            compare(b, bases[b], w, it).then_inc(m_oh[b], 1)
                            dve.wait_ge(m_h[b], q + w + 1)
                            add_expanded(b, q + w)
                    dve.wait_ge(m_gelu[b], it + 1)
                    e3 = tiles(hid[:, b, :])
                    dve.tensor_tensor(e3, e3, w2r[:, :].unsqueeze(1).broadcast_to([P, TPG, HID]), ALU.mult).then_inc(m_dot[b], 1)
                    dve.wait_ge(m_dot[b], it * 2 + 1)
                    dve.tensor_reduce(zed[:, b, :], e3, AXX, ALU.add).then_inc(m_dot[b], 1)
                    dve.wait_ge(m_tanh[b], it + 1)
                    dve.tensor_scalar(ews[:, b, :], tanhz[:, b, :], 0.5, 0.5, ALU.mult, ALU.add).then_inc(m_ew[b], 1)
                    dve.tensor_scalar(ewt[:, bass.ds(it * (2 * TPG) + b * TPG, TPG)], tanhz[:, b, :], 0.5, 0.5,
                                      ALU.mult, ALU.add).then_inc(m_ewt, 1)
                    add_degrees(b, bases[b], more, q, q, True)
                    with dve.If(more > 0):
                        with dve.Fori(0, more) as w:
                            compare(b, bases[b], w, it).then_inc(m_oh2[b], 1)
                            add_degrees(b, bases[b], w, q + w + 1, q, False)

            dve.wait_ge(d_sq, 1)
            dve.reciprocal(dinv[:, :], droot[:, :]).then_inc(d_v, 1)
            dve.wait_ge(d_v, 1)
            dve.tensor_tensor(blocks(XT2[:, :]), blocks(XT2[:, :]), dinv[:, :].unsqueeze(2).broadcast_to([P, NB, D]),
                              ALU.mult).then_inc(d_v, 1)
            dve.wait_ge(m_ewt, NG)
            dve.wait_ge(s_zero, 4)
            round_(R2b, ewt)

            dve.wait_ge(d_v, 2)
            with dve.Fori(0, NCH) as c:
                step, k = stepper(N3, c)
                dve.wait_ge(N3["t1"], c + 1)
                step(dve.tensor_tensor(y[:, :], psA[:, 0:CW], chunk(XT2, c), ALU.add))
                step(dve.tensor_tensor(blocks(y[:, :]), blocks(y[:, :]), per_node(dinv[:, bass.ds(c * CB, CB)]), ALU.mult))
                step(dve.tensor_tensor(blocks(y[:, :]), blocks(y[:, :]), spread(cbr[:, :]), ALU.add))
                step(dve.tensor_tensor(y[:, :], y[:, :], chunk(X, c), ALU.add))
                normalise(N3, c, step, k)

            dve.wait_ge(N3["eva"], NCH)
            with dve.Fori(0, LAYERS) as l:
                round_(R3, None, l=l)
                dve.wait_ge(l_w, l * 80 + 80)
                pass_waits(dve)
                with dve.Fori(0, NCH) as c:
                    dve.wait_ge(l_o, l * NCH + c + 1)
                    new = blocks(ps4[:, 0:CW])
                    dve.tensor_tensor(blocks(chunk(XT2, c)), new, spread(l3b2r[:, :]), ALU.add).then_inc(l_x2, 1)
                    dve.wait_ge(l_stored, l * NCH + c + 1)
                    dve.tensor_tensor(blocks(y[:, :]), new, spread(l3b2r[:, :]), ALU.add).then_inc(l_xo, 1)
                dve.wait_ge(l_acc, l * NCH + NCH)
                pass_waits(dve)

            dve.wait_ge(l_x2, LAYERS * NCH)
            dve.wait_ge(l_stored, LAYERS * NCH + 1)
            with dve.Fori(0, NCH) as c:
                step, k = stepper(NF, c)
                step(dve.tensor_tensor(y[:, :], chunk(XT2, c), chunk(X, c), ALU.add))
                normalise(NF, c, step, k)
                dve.wait_ge(NF["xn"], c + 1)
                pass_waits(dve)


_INS = ['x', 'src', 'dst', 'edge_attr_16', 'edge_type_8', 'edge_weight', 'L0_gnn_W', 'L0_gnn_edge_w', 'L0_gnn_b',
        'L1_gnn_weight', 'L1_gnn_bias', 'L2_gnn_mlp_w1', 'L2_gnn_mlp_b1', 'L2_gnn_mlp_w2', 'L2_gnn_mlp_b2',
        'L2_gnn_conv_w', 'L2_gnn_conv_b', 'L3_gnn_W1', 'L3_gnn_b1', 'L3_gnn_W2', 'L3_gnn_b2']
_OUTS = [((6250, 128), 'float32')]


def kernel(**inputs):
    import numpy as _np
    import concourse.bacc as _bacc
    from concourse import mybir as _mybir
    from concourse.bass_utils import run_bass_kernel_spmd as _run

    nc = _bacc.Bacc("TRN2", target_bir_lowering=False, num_devices=1)
    arrays, args = {}, []
    for name in _INS:
        a = _np.ascontiguousarray(inputs[name])
        arrays[f"in_{name}_dram"] = a
        args.append(nc.dram_tensor(f"in_{name}_dram", a.shape, _mybir.dt.from_np(a.dtype), kind="ExternalInput").ap())
    for i, (shape, dtype) in enumerate(_OUTS):
        dt = _mybir.dt.from_np(_np.dtype(dtype))
        args.append(nc.dram_tensor(f"out_{i}_dram", shape, dt, kind="ExternalOutput").ap())
    gnn_program(nc, *args)
    r = _run(nc, [arrays], core_ids=[0])
    got = tuple(r.results[0][f"out_{i}_dram"] for i in range(len(_OUTS)))
    return got[0]
```

```python
from contextlib import ExitStack

import concourse.bass as bass
from concourse import mybir

F32 = mybir.dt.float32
I32 = mybir.dt.int32
F16 = mybir.dt.float16
BF16 = mybir.dt.bfloat16
ALU = mybir.AluOpType
ACT = mybir.ActivationFunctionType
AXX = mybir.AxisListType.X

P = 128
D = 128
HID = 64
EDIM = 16
RELS = 8
LAYERS = 4
TPG = 8
GE = TPG * P
EPS = 1e-5
TB = 32
KS = 4
BT = 5
BE = BT * P
EXACT = 256


def gnn_program(nc, x, src, dst, edge_attr, edge_type, edge_weight, W0, edge_w, b0, W1r, bias1,
                mlp_w1, mlp_b1, mlp_w2, mlp_b2, conv_w, conv_b, L3W1, L3b1, L3W2, L3b2, out):
    N = x.shape[0]
    E = src.shape[0]
    NG = -(-E // GE)
    NIT = NG // 2
    FULL = E // GE
    TAIL = E - FULL * GE
    TAILP = TAIL // TPG
    NB = -(-N // P)
    NPAD = NB * P
    CB = 7
    NCH = NB // CB
    CW = CB * P
    LASTROWS = N - (NB - 1) * P
    MAXBASE = NPAD - P
    NT = NPAD // TB
    SG = -(-NB // KS)
    BN = SG * TB
    TS = KS * BN
    NCB = 14
    CC = NCB * TB
    NCI = NT // (2 * NCB)
    PADDED = NG * GE - E
    assert NG == 2 * NIT and NG == FULL + 1 and TAIL % TPG == 0 and NB == CB * NCH
    assert NT == 4 * NIT and NT == 2 * NCB * NCI and TAIL > EXACT and E >= BE

    with ExitStack() as ctx:
        def sb(name, shape, dt=F32):
            return ctx.enter_context(nc.sbuf_tensor(name, shape, dt))

        def sem(name):
            return ctx.enter_context(nc.semaphore(name))

        def sem2(name):
            return [sem(f"{name}{b}") for b in range(2)]

        def scratch(name, shape, dt=F32):
            return nc.dram_tensor(name, shape, dt, kind="Internal").ap()

        xw_rows = scratch("xw_rows", (NPAD, D))
        ht_rows = scratch("ht_rows", (NPAD * RELS, D))
        a_rows = scratch("a_rows", (NPAD, HID))
        b_rows = scratch("b_rows", (NPAD, HID))
        xt_rows = scratch("xt_rows", (NPAD, D))
        x_rows = scratch("x_rows", (NPAD, D))
        x_keep = scratch("x_keep", (NPAD, D))
        key_rows = scratch("key_rows", (E, 3))
        A_rows = scratch("A_rows", (NT, P, TS), BF16)

        big = sb("big", [P, 3 * NPAD + 6 * GE])
        iota = big[:, 0:NPAD]
        XT2 = big[:, NPAD:2 * NPAD]
        X = big[:, 2 * NPAD:3 * NPAD]
        G, onehot, msg = (big[:, 3 * NPAD + k * 2 * GE:3 * NPAD + (k + 1) * 2 * GE].rearrange("p (b n) -> p b n", b=2)
                          for k in range(3))
        Aring = big[:, 0:NCB * TS].bitcast(BF16).rearrange("p (r m t n) -> p r m t n", r=2, m=NCB, n=TB)
        acc = sb("acc", [P, NPAD])
        xsb = sb("xsb", [P, NB * 3 * D // 2])
        xs = xsb[:, :].bitcast(BF16).rearrange("p (t k f) -> p t k f", k=3, f=D)
        taken = [0]

        def part(words):
            taken[0] += words
            return xsb[:, taken[0] - words:taken[0]]
        ohS = part(BT * KS * P).bitcast(BF16).rearrange("p (u n) -> p u n", u=2)
        ohB = part(BT * BN).bitcast(BF16).rearrange("p (u n) -> p u n", u=2)
        Astage = part(TS).bitcast(BF16).rearrange("p (u s k n) -> p u s k n", u=2, s=SG, k=KS)
        hid = part(2 * TPG * HID).rearrange("p (b n) -> p b n", b=2)
        EWb = part(TPG * D).rearrange("p (j f) -> p j f", j=TPG)
        W1s = part(RELS * D).rearrange("p (r f) -> p r f", r=RELS)
        iotaS = sb("iotaS", [P, KS * P], F16)
        iotaB = sb("iotaB", [P, BN], F16)
        keys = sb("keys", [P, 2, BT, 3])
        kk = sb("kk", [P, 2, BT])
        starts = sb("starts", [1, 2, NT + 4])
        starti = sb("starti", [1, NT + 4], I32)
        densei = sb("densei", [1, 1], I32)
        attr = sb("attr", [P, 2, TPG * EDIM])
        attrT = sb("attrT", [P, 2, P])
        bwin = sb("bwin", [P, 2, HID])
        srci = sb("srci", [P, NG * TPG + 2 * TPG], I32)
        reli = sb("reli", [P, NG * TPG], I32)
        dstf = sb("dstf", [P, NG * TPG])
        wedge = sb("wedge", [P, NG * TPG])
        ewt = wedge
        idx = sb("idx", [P, 2, TPG], I32)
        zed = sb("zed", [P, 2, TPG])
        tanhz = sb("tanhz", [P, 2, TPG])
        ews = sb("ews", [P, 2, TPG])
        stT = sb("stT", [P, CW])
        y = sb("y", [P, CW])
        sq = sb("sq", [P, CW])
        xn = sb("xn", [P, CW])
        xTs = sb("xTs", [P, CW])
        ident = sb("ident", [P, P])
        pcol = sb("pcol", [P, 1])
        stat = sb("stat", [P, 4, CB])
        dinv = sb("dinv", [P, NB])
        droot = sb("droot", [P, NB])
        onec = sb("onec", [P, 1])
        small = sb("small", [P, 8])
        rowf = sb("rowf", [1, 4, NG])
        badrow = sb("badrow", [1, 4])
        basei = sb("basei", [1, NG], I32)
        nwini = sb("nwini", [1, 2], I32)
        one11 = sb("one11", [1, 1])
        W0s = sb("W0s", [P, D])
        W2s = sb("W2s", [P, 2 * HID + D])
        WA = sb("WA", [P, D])
        WB = sb("WB", [P, D])
        b0r = sb("b0r", [P, D])
        b1r = sb("b1r", [P, D])
        cbr = sb("cbr", [P, D])
        mb1r = sb("mb1r", [P, HID])
        w2r = sb("w2r", [P, HID])
        mb2r = sb("mb2r", [P, 1])
        l3b2r = sb("l3b2r", [P, D])
        l3b1c = sb("l3b1c", [P, 1])
        l3b2c = sb("l3b2c", [P, 1])

        raw = [XT2[:, k * GE:(k + 1) * GE] for k in range(4)]
        RSRC, RDST, RTYP, RWGT = range(4)
        atmost = XT2[:, 4 * GE:5 * GE]
        counts = XT2[:, 5 * GE:5 * GE + NT]
        keyraw = acc[:, 0:3 * GE].rearrange("p (e k) -> p e k", k=3)
        next1 = acc[:, 3 * GE:4 * GE]
        nextx = acc[:, 4 * GE:5 * GE]
        xchunks = X[:, :].rearrange("p (b f) -> p b f", f=D)

        psS = [ctx.enter_context(nc.psum_tensor(f"psS{b}", [P, 512], F32)) for b in range(2)]
        psA = ctx.enter_context(nc.psum_tensor("psA", [P, 1024], F32))
        ps4 = ctx.enter_context(nc.psum_tensor("ps4", [P, 2048], F32))

        s_load = sem("s_load")
        s_wload = sem("s_wload")
        s_xload = sem("s_xload")
        s_fill = sem("s_fill")
        s_iota = sem("s_iota")
        s_ident = sem("s_ident")
        s_chain = sem("s_chain")
        s_prep = sem("s_prep")
        s_plan = sem("s_plan")
        s_pt = sem("s_pt")
        s_pe = sem("s_pe")
        s_zero = sem("s_zero")
        c_keys = sem("c_keys")
        c_list = sem("c_list")
        c_ge = sem("c_ge")
        c_cnt = sem("c_cnt")
        c_start = sem("c_start")
        b_keys = sem2("b_keys")
        b_kk = sem("b_kk")
        b_oh = sem2("b_oh")
        b_bank = sem("b_bank")
        b_ev = sem("b_ev")
        b_dma = sem2("b_dma")
        b_free = sem2("b_free")
        a_ready = sem2("a_ready")
        a_done = sem2("a_done")
        a_add = sem2("a_add")
        x_s = sem("x_s")
        s_gate = sem("s_gate")

        r_idx = sem2("r_idx")
        r_ohraw = sem2("r_ohraw")
        r_oh = sem2("r_oh")
        r_seg = sem2("r_seg")
        r_acc = sem2("r_acc")

        class Round:
            def __init__(self, number, weighted, gathered, first):
                self.g0 = number * NIT
                self.w0 = weighted * NIT
                self.gathered = gathered
                self.d0 = first * NIT

        r_gath = sem2("r_gath")
        l_gath = sem2("l_gath")
        R0, R1, R2b, R3 = Round(0, 0, r_gath, 0), Round(1, 0, r_gath, 1), Round(2, 1, r_gath, 2), Round(3, 0, l_gath, 0)
        s_attr = sem2("s_attr")
        s_attrp = sem2("s_attrp")
        s_attrT = sem2("s_attrT")
        s_ew = sem2("s_ew")
        s_msg = sem2("s_msg")
        m_idx = sem2("m_idx")
        m_gath = sem2("m_gath")
        m_oh = sem2("m_oh")
        m_tp = sem2("m_tp")
        m_ohT = sem2("m_ohT")
        m_bwin = sem2("m_bwin")
        m_exp = sem2("m_exp")
        m_h = sem2("m_h")
        m_gelu = sem2("m_gelu")
        m_dot = sem2("m_dot")
        m_tanh = sem2("m_tanh")
        m_ew = sem2("m_ew")
        m_ewt = sem("m_ewt")
        s_half = sem("s_half")
        m_oh2 = sem2("m_oh2")
        m_deg = sem2("m_deg")
        m_dacc = sem2("m_dacc")
        d_t = sem("d_t")
        d_sq = sem("d_sq")
        d_v = sem("d_v")
        d_out = sem("d_out")

        def phase(name, steps, kinds):
            p = {kind: sem(f"{name}_{kind}") for kind in kinds.split()}
            return {**p, "steps": steps, "centred": steps - 3, "varied": steps - 1}

        norm = "dv sq xn xs "
        N0 = phase("n0", 0, "xn t2 xT tb ev dma stored")
        N1 = phase("n1", 8, norm + "st t1 t2 xT tb ev eva dma dmb stored storedb")
        N2 = phase("n2", 8, norm + "st t1 t2 xT tb ev eva eva2 dma dmb stored")
        N3 = phase("n3", 10, norm + "st t1 t2 eva dma stored")
        NF = phase("nf", 7, norm + "dma")
        l_w = sem("l_w")
        l_h = sem("l_h")
        l_relu = sem("l_relu")
        l_o = sem("l_o")
        l_acc = sem("l_acc")
        l_xo = sem("l_xo")
        l_dma = sem("l_dma")
        l_stored = sem("l_stored")

        def pass_waits(eng):
            eng.sem_inc(s_gate, 1)

        def as_row(v):
            return v.rearrange("(a n) -> a n", a=1)

        def window(base, w):
            if isinstance(w, int) and w == 0:
                return bass.ds(base, P)
            at = nc.s_assert_within(base + w * P, 0, MAXBASE, skip_runtime_bounds_check_because=
                                    "more than one window only from base 0")
            return bass.ds(at, P)

        def window_count(eng):
            return (eng.value_load(nwini[0:1, 0:1], min_val=1, max_val=NB),
                    eng.value_load(nwini[0:1, 1:2], min_val=0, max_val=NB - 1))

        def blocks(ap):
            return ap.rearrange("p (b f) -> p b f", f=D)

        def dense_flag(eng):
            return eng.value_load(densei[0:1, 0:1], min_val=0, max_val=1)

        R1N, R2N = 0, NIT
        NSTEP = 2 * NIT

        ALLW = 16 * (TPG + 11)

        block = ctx.enter_context(nc.Block())


        @block.sync
        def _(sp):
            sp.wait_ge(s_fill, 1)
            for r, a in ((RSRC, src), (RDST, dst), (RTYP, edge_type), (RWGT, edge_weight)):
                v = raw[r] if r == RWGT else raw[r].bitcast(I32)
                sp.dma_start(v[0:FULL, :], a[0:FULL * GE].rearrange("(g e) -> g e", e=GE)).then_inc(s_load, 16)
                sp.dma_start(v[FULL:FULL + 1, 0:TAIL], as_row(a[FULL * GE:E])).then_inc(s_load, 16)
            for v, shift in ((next1.bitcast(I32), 1), (nextx.bitcast(I32), EXACT)):
                sp.dma_start(v[0:FULL, :], dst[shift:FULL * GE + shift].rearrange("(g e) -> g e", e=GE)).then_inc(s_load, 16)
                sp.dma_start(v[FULL:FULL + 1, 0:TAIL - shift], as_row(dst[FULL * GE + shift:E])).then_inc(s_load, 16)
            sp.dma_start(blocks(X[:, 0:(NB - 1) * P]), x[0:(NB - 1) * P, :].rearrange("(b p) f -> p b f", p=P)).then_inc(s_xload, 16)
            sp.dma_start(X[0:LASTROWS, (NB - 1) * P:NPAD], x[(NB - 1) * P:N, :]).then_inc(s_xload, 16)
            for j in range(TPG):
                sp.dma_start(EWb[j * EDIM:(j + 1) * EDIM, j, :], edge_w[:, :]).then_inc(s_wload, 16)
            loads = [(W0s[:, :], W0[:, :]), (W1s[:, :, :], W1r.rearrange("r i o -> i r o")),
                     (W2s[:, 0:HID], mlp_w1[0:D, :]), (W2s[:, HID:2 * HID], mlp_w1[D:2 * D, :]),
                     (W2s[:, 2 * HID:], conv_w[:, :]),
                     (b0r[:, :], as_row(b0).broadcast_to([P, D])), (b1r[:, :], as_row(bias1).broadcast_to([P, D])),
                     (cbr[:, :], as_row(conv_b).broadcast_to([P, D])), (mb1r[:, :], as_row(mlp_b1).broadcast_to([P, HID])),
                     (w2r[:, :], mlp_w2.rearrange("h a -> a h").broadcast_to([P, HID])),
                     (mb2r[:, :], as_row(mlp_b2).broadcast_to([P, 1]))]
            for o, i in loads:
                sp.dma_start(o, i).then_inc(s_wload, 16)

            def rows_of(table, c):
                return table.rearrange("(b p) f -> p b f", p=P)[:, bass.ds(c * CB, CB), :]

            for s in (N0["stored"], N1["stored"], N1["storedb"], N2["stored"], N3["stored"], l_stored, *b_free):
                sp.sem_inc(s, 1)

            sp.wait_ge(c_keys, 1)
            sp.dma_start(key_rows[0:FULL * GE, :].rearrange("(g e) k -> g (e k)", e=GE), acc[0:FULL, 0:3 * GE]).then_inc(c_list, 16)
            sp.dma_start(key_rows[FULL * GE:E, :].rearrange("(a e) k -> a (e k)", a=1), acc[FULL:FULL + 1, 0:3 * TAIL]).then_inc(c_list, 16)

            with sp.Fori(0, NCH) as c:
                sp.wait_ge(N0["ev"], c + 2)
                pass_waits(sp)
                sp.dma_start(rows_of(xw_rows, c), blocks(msg[:, 0, 0:CW])).then_inc(N0["dma"], 16)
                sp.wait_ge(N0["dma"], 16 * c + 16)
                sp.sem_inc(N0["stored"], 1)

            def load_attr(b, it, g, parts):
                sp.wait_ge(s_attrp[b], it + 1)
                pass_waits(sp)
                sp.dma_start(attr[0:parts, b, :],
                             edge_attr[bass.ds(g * GE, parts * TPG), :].rearrange("(p j) k -> p (j k)", j=TPG)
                             ).then_inc(s_attr[b], 16)
            with sp.Fori(0, NIT - 1) as it:
                for b in range(2):
                    load_attr(b, it, it * 2 + b, P)
            load_attr(0, NIT - 1, NG - 2, P)
            load_attr(1, NIT - 1, NG - 1, TAILP)

            def load_keys(u, m):
                start = sp.value_load(starti[0:1, bass.ds(m, 1)], min_val=0, max_val=E - BE)
                sp.dma_start(keys[:, u, :, :], key_rows[bass.ds(start, BE), :].rearrange("(p j) k -> p j k", j=BT)
                             ).then_inc(b_keys[u], 16)

            def block_traffic(n0):
                with sp.Fori(0, NIT) as it:
                    n = it + n0
                    for u in range(2):
                        sp.wait_ge(b_oh[u], n + 2)
                        pass_waits(sp)
                        load_keys(u, n * 2 + 2 + u)
                    for u in range(2):
                        sp.wait_ge(b_dma[u], n * 16 + 16)
                        sp.sem_inc(b_free[u], 1)
            sp.wait_ge(c_start, 1)
            for u in range(2):
                load_keys(u, u)

            ht = ht_rows.rearrange("(b p r) f -> b p (r f)", p=P, r=RELS)
            with sp.Fori(0, NCH) as c:
                def stored(k):
                    if k % 2:
                        sp.wait_ge(N1["dmb"], 16 * (c * 3 + k // 2) + 16)
                        sp.sem_inc(N1["storedb"], 1)
                    else:
                        sp.wait_ge(N1["dma"], 16 * (c * 4 + k // 2) + 16)
                        sp.sem_inc(N1["stored"], 1)
                for k in range(CB):
                    ready, done, per = ((N1["ev"], N1["dma"], 4), (N1["eva"], N1["dmb"], 3))[k % 2]
                    sp.wait_ge(ready, c * per + k // 2 + 2)
                    pass_waits(sp)
                    sp.dma_start(ht[bass.ds(c * CB + k, 1)].rearrange("a p n -> (a p) n"), msg[:, k % 2, :]).then_inc(done, 16)
                    if k:
                        stored(k - 1)
                stored(CB - 1)

            block_traffic(R1N)

            with sp.Fori(0, NCH) as c:
                sp.wait_ge(N2["ev"], c + 2)
                pass_waits(sp)
                sp.dma_start(rows_of(a_rows, c), msg[:, 0, 0:CB * HID].rearrange("p (b f) -> p b f", f=HID)).then_inc(N2["dma"], 16)
                sp.wait_ge(N2["eva"], c + 1)
                pass_waits(sp)
                sp.dma_start(rows_of(b_rows, c), msg[:, 1, 0:CB * HID].rearrange("p (b f) -> p b f", f=HID)).then_inc(N2["dmb"], 16)
                sp.wait_ge(N2["dma"], 16 * c + 16)
                sp.wait_ge(N2["dmb"], 16 * c + 16)
                sp.sem_inc(N2["stored"], 1)

            nwin, more = window_count(sp)

            def load_window(b, base, w, q):
                sp.wait_ge(m_exp[b], q + 1)
                pass_waits(sp)
                sp.dma_start(bwin[:, b, :], b_rows[window(base, w), :]).then_inc(m_bwin[b], 16)
            with sp.Fori(0, NIT) as it:
                bases = [sp.value_load(basei[0:1, bass.ds(it * 2 + b, 1)], min_val=0, max_val=MAXBASE) for b in range(2)]
                for b in range(2):
                    load_window(b, bases[b], 0, it * nwin)
                for b in range(2):
                    with sp.If(more > 0):
                        with sp.Fori(1, more + 1) as w:
                            load_window(b, bases[b], w, it * nwin + w)

            sp.wait_ge(d_v, 2)
            sp.dma_start(xt_rows.rearrange("(b p) f -> p b f", p=P), blocks(XT2[:, :])).then_inc(d_out, 16)

            block_traffic(R2N)

            with sp.Fori(0, NCH) as c:
                sp.wait_ge(N3["xn"], c + 1)
                pass_waits(sp)
                for table in (x_rows, x_keep):
                    sp.dma_start(rows_of(table, c), blocks(xn[:, :])).then_inc(N3["dma"], 16)
                sp.wait_ge(N3["dma"], 32 * c + 32)
                sp.sem_inc(N3["stored"], 1)

            sp.wait_ge(N3["xs"], NCH)
            for u in range(2):
                sp.wait_ge(b_dma[u], 16 * NSTEP)
            dense = dense_flag(sp)
            with sp.If(dense > 0):
                with sp.Fori(0, LAYERS) as l:
                    with sp.Fori(0, NCI) as i:
                        for r in range(2):
                            sp.wait_ge(a_done[r], l * NCI + i + 1)
                            pass_waits(sp)
                            for h in range(2):
                                half = NCB // 2
                                sp.dma_start(Aring[:, r, h * half:(h + 1) * half, :, :].rearrange("p m t n -> p m (t n)"),
                                             A_rows[bass.ds(i * (2 * NCB) + r * NCB + h * half, half), :, :].rearrange("m p c -> p m c")
                                             ).then_inc(a_ready[r], 16)

            sp.wait_ge(l_stored, LAYERS * NCH + 1)
            sp.dma_start(blocks(X[:, :]), x_keep.rearrange("(b p) f -> p b f", p=P)).then_inc(s_xload, 16)
            sp.dma_start(blocks(XT2[:, :]), x_rows.rearrange("(b p) f -> p b f", p=P)).then_inc(s_xload, 16)

            sp.wait_ge(NF["xs"], NCH)
            sp.dma_start(out[0:(NB - 1) * P, :].rearrange("(b p) f -> p b f", p=P), blocks(X[:, 0:(NB - 1) * P])).then_inc(NF["dma"], 16)
            sp.dma_start(out[(NB - 1) * P:N, :], X[0:LASTROWS, (NB - 1) * P:NPAD]).then_inc(NF["dma"], 16)
            sp.wait_ge(NF["dma"], 32)

        @block.gpsimd
        def _(pool):
            pool.iota(iota[:, :], [[1, NPAD]], base=0, channel_multiplier=0,
                      allow_small_or_imprecise_dtypes=True).then_inc(s_iota, 1)
            pool.iota(pcol[:, :], [[0, 1]], base=0, channel_multiplier=1,
                      allow_small_or_imprecise_dtypes=True).then_inc(s_iota, 1)
            pool.wait_ge(c_list, 32)
            pool.wait_ge(s_prep, 1)
            pool.memset(acc[:, :], 0.0).then_inc(s_zero, 1)

            def gathers(it, idx_ready, gathered, table, width):
                for b in range(2):
                    pool.wait_ge(idx_ready[b], it + 1)
                    pass_waits(pool)
                    for j in range(TPG):
                        pool.indirect_dma_start(G[:, b, j * width:(j + 1) * width], None, table[:, :],
                                                bass.IndirectOffsetOnAxis(ap=idx[:, b, j:j + 1], axis=0)
                                                ).then_inc(gathered[b], 16)

            def zero_acc(read, count):
                pool.wait_ge(read, count)
                pool.memset(acc[:, :], 0.0).then_inc(s_zero, 1)

            pool.wait_ge(N0["stored"], NCH + 1)
            with pool.Fori(0, NIT) as it:
                gathers(it, r_idx, R0.gathered, xw_rows, D)
            zero_acc(N1["st"], NCH)
            pool.wait_ge(N1["stored"], NCH * 4 + 1)
            pool.wait_ge(N1["storedb"], NCH * 3 + 1)
            with pool.Fori(0, NIT) as it:
                gathers(it + R1.g0, r_idx, R1.gathered, ht_rows, D)
            zero_acc(N2["st"], NCH)
            pool.wait_ge(N2["stored"], NCH + 1)
            with pool.Fori(0, NIT) as it:
                gathers(it, m_idx, m_gath, a_rows, HID)
            zero_acc(d_t, 1)
            pool.wait_ge(d_out, 16)
            with pool.Fori(0, NIT) as it:
                gathers(it + R2b.g0, r_idx, R2b.gathered, xt_rows, D)
            pool.wait_ge(N3["stored"], NCH + 1)
            dense = dense_flag(pool)
            with pool.Fori(0, LAYERS) as l:
                with pool.If(dense < 1):
                    with pool.Fori(0, NIT) as it:
                        gathers(l * NIT + it + R3.g0, r_idx, R3.gathered, x_rows, D)
                with pool.Fori(0, NCH) as c:
                    pool.wait_ge(l_xo, l * NCH + c + 1)
                    pass_waits(pool)
                    pool.dma_start(x_rows.rearrange("(b p) f -> p b f", p=P)[:, bass.ds(c * CB, CB), :],
                                   blocks(y[:, :])).then_inc(l_dma, 16)
                    pool.wait_ge(l_dma, (l * NCH + c) * 16 + 16)
                    pool.sem_inc(l_stored, 1)

        @block.scalar
        def _(act):
            act.wait_ge(s_plan, 1)
            nwin, more = window_count(act)

            act.sem_inc(N1["eva"], 1)
            act.sem_inc(b_ev, KS)

            def stage_idx(b, it, free, count, idx_ready, lists):
                act.wait_ge(free[b], count + 1)
                pass_waits(act)
                act.copy(idx[:, b, :], lists[:, bass.ds(it * (2 * TPG) + b * TPG, TPG)]).then_inc(idx_ready[b], 1)

            def index_round(R, lists, l=0):
                with act.Fori(0, NIT) as it:
                    for b in range(2):
                        stage_idx(b, it, r_seg, (l * NIT + it + R.g0) * nwin, r_idx, lists)

            def block_stage(u, n):
                m = n * 2 + u
                act.wait_ge(b_free[u], n + 1)
                for k in range(KS):
                    act.wait_ge(b_bank, m * KS + 2 * KS + k + 1)
                    act.copy(Astage[:, u, :, k, :], ps4[:, k * 512:k * 512 + BN].rearrange("p (s n) -> p s n", n=TB)).then_inc(b_ev, 1)
                act.wait_ge(b_ev, m * KS + 2 * KS)
                pass_waits(act)
                act.dma_start(A_rows[bass.ds(m, 1), :, :].rearrange("a p c -> (a p) c"),
                              Astage[:, u, :, :, :].rearrange("p s k n -> p (s k n)")).then_inc(b_dma[u], 16)

            def index_and_stage_round(R, lists, n0):
                for b in range(2):
                    stage_idx(b, 0, r_seg, R.g0 * nwin, r_idx, lists)
                with act.Fori(0, NIT - 1) as it:
                    for b in range(2):
                        block_stage(b, it + n0)
                        stage_idx(b, it + 1, r_seg, (it + 1 + R.g0) * nwin, r_idx, lists)
                for b in range(2):
                    block_stage(b, NIT - 1 + n0)

            def norm_steps(p, c):
                act.wait_ge(p["dv"], c * p["steps"] + p["centred"])
                act.activation(sq[:, :], y[:, :], ACT.Square).then_inc(p["sq"], 1)
                act.wait_ge(p["dv"], c * p["steps"] + p["varied"])
                act.activation(stat[:, 2, :], stat[:, 1, :], ACT.Sqrt).then_inc(p["sq"], 1)
                act.wait_ge(p["xn"], c + 1)
                pass_waits(act)
                act.copy(X[:, bass.ds(c * CW, CW)], xn[:, :]).then_inc(p["xs"], 1)

            def stage_acc(p, c):
                act.copy(stT[:, :], acc[:, bass.ds(c * CW, CW)]).then_inc(p["st"], 1)

            def transposed(p, c):
                act.wait_ge(p["t2"], c + 1)
                act.copy(xTs[:, :], psA[:, 0:CW]).then_inc(p["xT"], 1)

            def summed(R):
                for b in range(2):
                    act.wait_ge(r_acc[b], (R.g0 + NIT) * nwin + 1)

            with act.Fori(0, NCH) as c:
                transposed(N0, c)

            with act.Fori(0, NIT) as it:
                for b in range(2):
                    stage_idx(b, it, r_seg, it * nwin, r_idx, srci)
                for b in range(2):
                    act.wait_ge(s_attrp[b], it + 2)
                    act.copy(attrT[:, b, :], psA[:, b * 512:b * 512 + P]).then_inc(s_attrT[b], 1)

            summed(R0)
            with act.Fori(0, NCH) as c:
                stage_acc(N1, c)
                norm_steps(N1, c)
                transposed(N1, c)
                for k in range(1, CB, 2):
                    act.wait_ge(N1["tb"], c * CB + k + 1)
                    act.wait_ge(N1["storedb"], c * 3 + k // 2 + 1)
                    act.copy(msg[:, 1, :], ps4[:, 1024:2048]).then_inc(N1["eva"], 1)

            index_and_stage_round(R1, reli, R1N)

            summed(R1)
            with act.Fori(0, NCH) as c:
                stage_acc(N2, c)
                norm_steps(N2, c)
                transposed(N2, c)
                act.wait_ge(N2["tb"], c + 1)
                act.wait_ge(N2["ev"], c + 2)
                act.wait_ge(N2["stored"], c + 1)
                rows = ps4[:, 0:CB * 256].rearrange("p (b n) -> p b n", n=256)
                act.copy(msg[:, 1, 0:CB * HID].rearrange("p (b n) -> p b n", n=HID), rows[:, :, HID:2 * HID]).then_inc(N2["eva"], 1)
                act.copy(blocks(XT2[:, bass.ds(c * CW, CW)]), rows[:, :, 2 * HID:]).then_inc(N2["eva2"], 1)

            def turned_onehots(b, q):
                act.wait_ge(m_tp[b], q + 2)
                act.copy(msg[:, b, :], ps4[:, b * GE:(b + 1) * GE]).then_inc(m_ohT[b], 1)
            act.wait_ge(N2["stored"], NCH + 1)
            act.wait_ge(s_half, 1)
            for b in range(2):
                act.copy(idx[:, b, :], srci[:, b * TPG:(b + 1) * TPG]).then_inc(m_idx[b], 1)
            with act.Fori(0, NIT) as it:
                for b in range(2):
                    turned_onehots(b, it * nwin)
                for b in range(2):
                    with act.If(more > 0):
                        with act.Fori(1, more + 1) as w:
                            turned_onehots(b, it * nwin + w)
                    act.wait_ge(m_h[b], it * nwin + nwin + 1)
                    act.activation(hid[:, b, :], G[:, b, 0:TPG * HID], ACT.Gelu).then_inc(m_gelu[b], 1)
                    stage_idx(b, it + 1, m_gelu, it, m_idx, srci)
                    act.wait_ge(m_dot[b], it * 2 + 2)
                    act.activation(tanhz[:, b, :], zed[:, b, :], ACT.Tanh, bias=mb2r[:, :], scale=0.5).then_inc(m_tanh[b], 1)
            act.wait_ge(d_t, 1)
            act.activation(droot[:, :], ps4[:, 0:NB], ACT.Sqrt, bias=onec[:, :]).then_inc(d_sq, 1)

            index_and_stage_round(R2b, srci, R2N)

            summed(R2b)
            with act.Fori(0, NCH) as c:
                stage_acc(N3, c)
                norm_steps(N3, c)
                act.wait_ge(N3["t2"], c + 1)
                pass_waits(act)
                act.copy(acc[:, bass.ds(c * CW, CW)], psA[:, 0:CW]).then_inc(N3["eva"], 1)

            dense = dense_flag(act)
            with act.Fori(0, LAYERS) as l:
                act.dma_start(WA[:, :], L3W1[bass.ds(l, 1)].rearrange("a i o -> (a i) o")).then_inc(l_w, 16)
                act.dma_start(WB[:, :], L3W2[bass.ds(l, 1)].rearrange("a i o -> (a i) o")).then_inc(l_w, 16)
                act.dma_start(l3b2r[:, :], L3b2[bass.ds(l, 1), :].broadcast_to([P, D])).then_inc(l_w, 16)
                act.dma_start(l3b1c[:, :], L3b1[bass.ds(l, 1), :].rearrange("a f -> f a")).then_inc(l_w, 16)
                act.dma_start(l3b2c[:, :], L3b2[bass.ds(l, 1), :].rearrange("a f -> f a")).then_inc(l_w, 16)
                with act.If(dense < 1):
                    index_round(R3, srci, l)
                with act.Fori(0, NCH) as c:
                    act.wait_ge(l_h, l * NCH + c + 1)
                    act.activation(xTs[:, :], psA[:, 0:CW], ACT.Relu, bias=l3b1c[:, :]).then_inc(l_relu, 1)
                    act.wait_ge(l_o, l * NCH + c + 1)
                    pass_waits(act)
                    act.activation(acc[:, bass.ds(c * CW, CW)], ps4[:, 1024:1024 + CW], ACT.Identity,
                                   bias=l3b2c[:, :]).then_inc(l_acc, 1)
                act.wait_ge(l_acc, l * NCH + NCH)
                act.wait_ge(l_xo, l * NCH + NCH)
                pass_waits(act)

            act.wait_ge(s_xload, 64)
            with act.Fori(0, NCH) as c:
                norm_steps(NF, c)

        @block.tensor
        def _(pe):
            pe.wait_ge(s_ident, 1)
            for r in range(4):
                pe.wait_ge(s_prep, r + 1)
                if r >= 1:
                    pe.wait_ge(s_pe, r)
                v = raw[r].rearrange("g (p j) -> g j p", j=TPG)
                for j in range(TPG):
                    m = pe.transpose(ps4[:, j * P:j * P + NG], v[0:NG, j, :], ident[0:NG, 0:NG])
                m.then_inc(s_pt, 1)
            pe.wait_ge(s_prep, 5)
            pe.transpose(psA[0:1, 0:NG], small[0:NG, 0:1], ident[0:NG, 0:NG])
            pe.transpose(psA[0:1, P:P + NG], small[0:NG, 1:2], ident[0:NG, 0:NG])
            pe.transpose(psA[0:1, 2 * P:2 * P + NG], small[0:NG, 2:3], ident[0:NG, 0:NG]).then_inc(s_pt, 1)
            pe.wait_ge(s_plan, 1)
            nwin, more = window_count(pe)
            pe.wait_ge(s_wload, ALLW)

            def turn_chunk(source, done):
                for k in range(CB):
                    m = pe.transpose(psA[:, k * P:(k + 1) * P], source[:, k * P:(k + 1) * P], ident[:, :])
                m.then_inc(done, 1)

            def window_sums(rows, b, q):
                pe.wait_ge(r_oh[b], q + 1)
                pe.wait_ge(r_acc[b], q + 1)
                for j in range(TPG):
                    m = pe.matmul(psS[b][:, 0:P], rows[:, b, j * P:(j + 1) * P], onehot[:, b, j * P:(j + 1) * P],
                                  start=(j == 0), stop=(j == TPG - 1))
                m.then_inc(r_seg[b], 1)

            def segment_sums(rows, b, q0):
                window_sums(rows, b, q0)
                with pe.If(more > 0):
                    with pe.Fori(1, more + 1) as w:
                        window_sums(rows, b, q0 + w)

            def plain_round(R, l=0):
                with pe.Fori(0, NIT) as it:
                    for b in range(2):
                        pe.wait_ge(R.gathered[b], (l * NIT + it + R.d0) * (16 * TPG) + 16 * TPG)
                        segment_sums(G, b, (l * NIT + it + R.g0) * nwin)

            def block_counts(u, n):
                m = n * 2 + u
                pe.wait_ge(b_oh[u], n + 2)
                for k in range(KS):
                    pe.wait_ge(b_ev, m * KS + k + 1)
                    for j in range(BT):
                        mm = pe.matmul(ps4[:, k * 512:k * 512 + BN], ohS[:, u, (j * KS + k) * P:(j * KS + k + 1) * P],
                                       ohB[:, u, j * BN:(j + 1) * BN], start=(j == 0), stop=(j == BT - 1))
                    mm.then_inc(b_bank, 1)

            def counting_round(R, n0):
                with pe.Fori(0, NIT) as it:
                    for b in range(2):
                        block_counts(b, it + n0)
                        pe.wait_ge(R.gathered[b], (it + R.d0) * (16 * TPG) + 16 * TPG)
                        segment_sums(G, b, (it + R.g0) * nwin)

            pe.sem_inc(b_bank, 2 * KS)
            for b in range(2):
                pe.sem_inc(a_done[b], 1)
                pe.sem_inc(r_seg[b], 1)
                pe.sem_inc(s_attrp[b], 1)
                pe.sem_inc(m_tp[b], 1)
                pe.sem_inc(m_exp[b], 1)

            with pe.Fori(0, NCH) as c:
                pe.wait_ge(N0["xn"], c + 1)
                turn_chunk(xn, N0["t2"])
                pe.wait_ge(N0["xT"], c + 1)
                pe.wait_ge(N0["ev"], c + 1)
                for k in range(CB):
                    m = pe.matmul(ps4[:, k * P:(k + 1) * P], xTs[:, k * P:(k + 1) * P], W0s[:, :], start=True, stop=True)
                m.then_inc(N0["tb"], 1)

            pe.wait_ge(N0["ev"], NCH + 1)
            with pe.Fori(0, NIT) as it:
                for b in range(2):
                    pe.wait_ge(s_attr[b], 16 * it + 16)
                    pe.transpose(psA[:, b * 512:b * 512 + P], attr[:, b, :], ident[:, :]).then_inc(s_attrp[b], 1)
                for b in range(2):
                    pe.wait_ge(s_attrT[b], it + 1)
                    pe.wait_ge(s_msg[b], it + 1)
                    for h in range(2):
                        m = pe.matmul(ps4[:, b * GE + h * 512:b * GE + (h + 1) * 512], attrT[:, b, :],
                                      EWb[:, 4 * h:4 * h + 4, :].rearrange("p j f -> p (j f)"), start=True, stop=True)
                    m.then_inc(s_ew[b], 1)
                for b in range(2):
                    pe.wait_ge(s_msg[b], it + 2)
                    segment_sums(msg, b, it * nwin)

            pe.wait_ge(c_cnt, NT + 1)
            pe.wait_ge(r_acc[0], NIT * nwin + 1)
            pe.matmul(psS[0][0:1, 0:NT], onec[0:NG, :], counts[0:NG, :], start=True, stop=True).then_inc(s_pt, 1)

            with pe.Fori(0, NCH) as c:
                pe.wait_ge(N1["st"], c + 1)
                turn_chunk(stT, N1["t1"])
                pe.wait_ge(N1["xn"], c + 1)
                turn_chunk(xn, N1["t2"])
                pe.wait_ge(N1["xT"], c + 1)
                for k in range(CB):
                    if k % 2:
                        pe.wait_ge(N1["eva"], c * 3 + k // 2 + 1)
                    else:
                        pe.wait_ge(N1["ev"], c * 4 + k // 2 + 1)
                    for h in range(2):
                        m = pe.matmul(ps4[:, (k % 2) * 1024 + h * 512:(k % 2) * 1024 + (h + 1) * 512], xTs[:, k * P:(k + 1) * P],
                                      W1s[:, 4 * h:4 * h + 4, :].rearrange("p r f -> p (r f)"), start=True, stop=True)
                    m.then_inc(N1["tb"], 1)

            pe.wait_ge(N1["ev"], NCH * 4 + 1)
            pe.wait_ge(N1["eva"], NCH * 3 + 1)
            pe.wait_ge(c_start, 1)
            counting_round(R1, R1N)
            pe.wait_ge(b_ev, 2 * NIT * KS + KS)

            with pe.Fori(0, NCH) as c:
                pe.wait_ge(N2["st"], c + 1)
                turn_chunk(stT, N2["t1"])
                pe.wait_ge(N2["xn"], c + 1)
                turn_chunk(xn, N2["t2"])
                pe.wait_ge(N2["xT"], c + 1)
                pe.wait_ge(N2["ev"], c + 1)
                for k in range(CB):
                    m = pe.matmul(ps4[:, k * 256:(k + 1) * 256], xTs[:, k * P:(k + 1) * P], W2s[:, :], start=True, stop=True)
                m.then_inc(N2["tb"], 1)

            pe.wait_ge(N2["ev"], NCH + 1)
            pe.wait_ge(N2["eva2"], NCH)

            def expand(b, q):
                pe.wait_ge(m_oh[b], q + 1)
                for j in range(TPG):
                    m = pe.transpose(ps4[:, b * GE + j * P:b * GE + (j + 1) * P], onehot[:, b, j * P:(j + 1) * P], ident[:, :])
                m.then_inc(m_tp[b], 1)
                pe.wait_ge(m_ohT[b], q + 1)
                pe.wait_ge(m_bwin[b], 16 * q + 16)
                pe.wait_ge(m_h[b], q + 1)
                for j in range(TPG):
                    m = pe.matmul(psA[:, b * 512 + j * HID:b * 512 + (j + 1) * HID], msg[:, b, j * P:(j + 1) * P],
                                  bwin[:, b, :], start=True, stop=True)
                m.then_inc(m_exp[b], 1)

            def degrees(b, q):
                pe.wait_ge(m_dacc[b], q + 1)
                for j in range(TPG):
                    m = pe.matmul(psS[b][0:1, 0:P], ews[:, b, j:j + 1], onehot[:, b, j * P:(j + 1) * P],
                                  start=(j == 0), stop=(j == TPG - 1))
                m.then_inc(m_deg[b], 1)
            with pe.Fori(0, NIT) as it:
                for b in range(2):
                    expand(b, it * nwin)
                for b in range(2):
                    with pe.If(more > 0):
                        with pe.Fori(1, more + 1) as w:
                            expand(b, it * nwin + w)
                    pe.wait_ge(m_ew[b], it + 1)
                    degrees(b, it * nwin)
                    with pe.If(more > 0):
                        with pe.Fori(0, more) as w:
                            pe.wait_ge(m_oh2[b], it * more + w + 1)
                            degrees(b, it * nwin + w + 1)
            for b in range(2):
                pe.wait_ge(m_dacc[b], NIT * nwin + 1)
            for k in range(NB):
                m = pe.matmul(ps4[:, k:k + 1], acc[0:1, k * P:(k + 1) * P], one11[:, :], start=True, stop=True)
            m.then_inc(d_t, 1)

            pe.wait_ge(d_sq, 1)
            counting_round(R2b, R2N)

            with pe.Fori(0, NCH) as c:
                pe.wait_ge(N3["st"], c + 1)
                turn_chunk(stT, N3["t1"])
                pe.wait_ge(N3["xn"], c + 1)
                turn_chunk(xn, N3["t2"])

            pe.wait_ge(N3["eva"], NCH)
            pe.wait_ge(b_ev, 4 * NIT * KS + KS)
            dense = dense_flag(pe)
            with pe.Fori(0, LAYERS) as l:
                with pe.If(dense < 1):
                    plain_round(R3, l)
                    for b in range(2):
                        pe.wait_ge(r_acc[b], (l * NIT + NIT + R3.g0) * nwin + 1)
                    pass_waits(pe)
                with pe.If(dense > 0):
                    pe.wait_ge(x_s, l * (4 * NCH) + 4 * NCH)
                    pass_waits(pe)
                    with pe.Fori(0, NCI) as i:
                        for r in range(2):
                            pe.wait_ge(a_ready[r], (l * NCI + i) * 32 + 32)
                            pe.wait_ge(a_add[r], l * NCI + i + 1)
                            for t in range(NB):
                                for k in range(3):
                                    m = pe.matmul(psS[r][:, 0:CC], xs[:, t, k, :], Aring[:, r, :, t, :],
                                                  start=(t == 0 and k == 0), stop=(t == NB - 1 and k == 2))
                            m.then_inc(a_done[r], 1)
                    for r in range(2):
                        pe.wait_ge(a_add[r], l * NCI + NCI + 1)
                    pass_waits(pe)
                pe.wait_ge(l_w, l * 80 + 80)
                pass_waits(pe)
                with pe.Fori(0, NCH) as c:
                    for lo, hi in ((0, 512), (512, CW)):
                        m = pe.matmul(psA[:, lo:hi], WA[:, :], acc[:, bass.ds(c * CW + lo, hi - lo)], start=True, stop=True)
                    m.then_inc(l_h, 1)
                    pe.wait_ge(l_relu, l * NCH + c + 1)
                    for k in range(CB):
                        pe.matmul(ps4[:, k * P:(k + 1) * P], xTs[:, k * P:(k + 1) * P], WB[:, :], start=True, stop=True)
                    for lo, hi in ((0, 512), (512, CW)):
                        m = pe.matmul(ps4[:, 1024 + lo:1024 + hi], WB[:, :], xTs[:, lo:hi], start=True, stop=True)
                    m.then_inc(l_o, 1)
                    pe.wait_ge(l_acc, l * NCH + c + 1)
                    pe.wait_ge(l_xo, l * NCH + c + 1)

        @block.vector
        def _(dve):
            chain = [0]

            def link(ins):
                chain[0] += 1
                ins.then_inc(s_chain, 1)
                dve.wait_ge(s_chain, chain[0])

            for r in range(4):
                if r == RDST:
                    dve.memset(raw[r].bitcast(I32), -1)
                else:
                    dve.memset(raw[r], 0.0)
            for v in (next1, nextx):
                dve.memset(v.bitcast(I32), 2 * NPAD)
            dve.memset(starts[:, :, :], 0.0)
            dve.memset(starti[:, :], 0)
            dve.memset(EWb[:, :, :], 0.0)
            dve.memset(attr[:, :, :], 0.0)
            dve.memset(srci[:, NG * TPG:], 0)
            dve.memset(one11[:, :], 1.0)
            dve.memset(onec[:, :], 1.0)
            dve.memset(X[:, (NB - 1) * P:NPAD], 0.0).then_inc(s_fill, 1)
            for b in range(2):
                dve.sem_inc(r_acc[b], 1)
                dve.sem_inc(s_msg[b], 1)
                dve.sem_inc(m_h[b], 1)
                dve.sem_inc(m_dacc[b], 1)
                dve.sem_inc(b_oh[b], 1)
                dve.sem_inc(a_add[b], 1)
            dve.sem_inc(c_cnt, 1)
            for p in (N0, N1, N2):
                dve.sem_inc(p["ev"], 1)
            dve.wait_ge(s_iota, 2)
            dve.tensor_scalar(ident[:, :], iota[:, 0:P], pcol[:, 0:1], None, ALU.is_equal).then_inc(s_ident, 1)
            dve.tensor_copy(iotaS[:, :], iota[:, 0:KS * P])
            dve.tensor_copy(iotaB[:, :], iota[:, 1:BN + 1])
            dve.wait_ge(s_load, 16 * 12)
            srcn, dstn = raw[RSRC].bitcast(I32), raw[RDST].bitcast(I32)
            ka, kb = G[:, 0, :].bitcast(I32), G[:, 1, :].bitcast(I32)
            shift_s, shift_t = (KS * P).bit_length() - 1, TB.bit_length() - 1
            link(dve.tensor_scalar(ka, srcn, KS * P - 1, None, ALU.bitwise_and))
            link(dve.tensor_copy(keyraw[:, :, 0], ka))
            link(dve.tensor_scalar(ka, srcn, shift_s - shift_t, 15 * TB, ALU.logical_shift_right, ALU.bitwise_and))
            link(dve.tensor_scalar(kb, dstn, TB - 1, None, ALU.bitwise_and))
            link(dve.scalar_tensor_tensor(keyraw[:, :, 1], ka, 1.0, kb, ALU.add, ALU.add))
            link(dve.tensor_scalar(ka, dstn, shift_t, None, ALU.logical_shift_right))
            link(dve.tensor_copy(keyraw[:, :, 2], ka))
            dve.sem_inc(c_keys, 1)
            unsorted, many = G[:, 0, :], G[:, 1, :]
            link(dve.tensor_tensor(unsorted, dstn, next1.bitcast(I32), ALU.is_gt))
            link(dve.tensor_tensor(many, dstn, nextx.bitcast(I32), ALU.is_equal))
            link(dve.tensor_tensor(many, many, unsorted, ALU.max))
            link(dve.tensor_reduce(small[:, 2:3], many, AXX, ALU.max))
            link(dve.tensor_copy(raw[RSRC], raw[RSRC].bitcast(I32)))
            dve.sem_inc(s_prep, 1)
            link(dve.tensor_copy(raw[RDST], raw[RDST].bitcast(I32)))
            dve.sem_inc(s_prep, 1)
            link(dve.tensor_copy(raw[RTYP], raw[RTYP].bitcast(I32)))
            link(dve.scalar_tensor_tensor(raw[RTYP], raw[RSRC], float(RELS), raw[RTYP], ALU.mult, ALU.add))
            dve.sem_inc(s_prep, 2)
            link(dve.tensor_scalar(msg[0:NG, 0, :], raw[RDST][0:NG, :], 0.0, float(NPAD), ALU.is_lt, ALU.mult))
            link(dve.tensor_tensor(msg[0:NG, 0, :], msg[0:NG, 0, :], raw[RDST][0:NG, :], ALU.add))
            link(dve.tensor_reduce(small[0:NG, 0:1], msg[0:NG, 0, :], AXX, ALU.min))
            link(dve.tensor_reduce(small[0:NG, 1:2], raw[RDST][0:NG, :], AXX, ALU.max))
            dve.sem_inc(s_prep, 1)
            lists = ((RSRC, srci), (RDST, dstf), (RTYP, reli), (RWGT, wedge))
            for r, to in lists:
                dve.wait_ge(s_pt, r + 1)
                link(dve.tensor_copy(to[:, 0:NG * TPG].rearrange("p (g j) -> p j g", j=TPG),
                                     ps4[:, 0:GE].rearrange("p (j g) -> p j g", j=TPG)[:, :, 0:NG]))
                dve.sem_inc(s_pe, 1)
            dve.wait_ge(s_pt, 5)
            lo, hi, span, base = (rowf[:, k, :] for k in range(4))
            link(dve.tensor_copy(lo, psA[0:1, 0:NG]))
            link(dve.tensor_tensor(span, psA[0:1, P:P + NG], lo, ALU.subtract))
            link(dve.tensor_reduce(badrow[:, 0:1], psA[0:1, 2 * P:2 * P + NG], AXX, ALU.max))
            link(dve.tensor_reduce(hi[:, 0:1], span, AXX, ALU.max))
            link(dve.tensor_scalar(hi[:, 1:2], hi[:, 0:1], float(P), None, ALU.is_lt))
            link(dve.tensor_scalar(base, lo, float(MAXBASE), hi[:, 1:2], ALU.min, ALU.mult))
            link(dve.tensor_copy(basei[:, :], base))
            link(dve.tensor_scalar(hi[:, 2:3], hi[:, 1:2], float(1 - NB), float(NB), ALU.mult, ALU.add))
            link(dve.tensor_scalar(hi[:, 3:4], hi[:, 2:3], -1.0, None, ALU.add))
            link(dve.tensor_copy(nwini[:, :], hi[:, 2:4]))
            dve.sem_inc(s_plan, 1)
            nwin, more = window_count(dve)
            dve.wait_ge(s_wload, ALLW)
            dve.tensor_scalar(mb2r[:, :], mb2r[:, :], 0.5, None, ALU.mult).then_inc(s_half, 1)

            def load_base(it, b):
                return dve.value_load(basei[0:1, bass.ds(it * 2 + b, 1)], min_val=0, max_val=MAXBASE)

            def tiles(ap):
                return ap.rearrange("p (j n) -> p j n", j=TPG)

            def columns(table, it, b):
                return table[:, bass.ds(it * (2 * TPG) + b * TPG, TPG)].unsqueeze(2).broadcast_to([P, TPG, P])

            def compare(b, base, w, it):
                return dve.tensor_tensor(tiles(onehot[:, b, :]), iota[:, window(base, w)].unsqueeze(1).broadcast_to([P, TPG, P]),
                                         columns(dstf, it, b), ALU.is_equal)

            def make_onehots(b, base, w, it, raw_count, weights):
                if weights is None:
                    compare(b, base, w, it).then_inc(r_oh[b], 1)
                else:
                    compare(b, base, w, it).then_inc(r_ohraw[b], 1)
                    dve.wait_ge(r_ohraw[b], raw_count + 1)
                    dve.tensor_tensor(tiles(onehot[:, b, :]), tiles(onehot[:, b, :]), columns(weights, it, b),
                                      ALU.mult).then_inc(r_oh[b], 1)

            def last_add(done, b, w, q, steps):
                if not isinstance(w, int):
                    dve.wait_ge(done[b], q + 1)
                elif b:
                    dve.wait_ge(done[0], steps + nwin + 1)
                else:
                    dve.wait_ge(done[1], steps + 1)

            def add_sums(b, base, w, q, q0):
                last_add(r_acc, b, w, q, q0)
                dve.wait_ge(r_seg[b], q + 2)
                at = acc[:, window(base, w)]
                dve.tensor_tensor(at, at, psS[b][:, 0:P], ALU.add).then_inc(r_acc[b], 1)

            def block_onehots(u, n):
                dve.wait_ge(b_keys[u], n * 16 + 16)
                dve.scalar_tensor_tensor(kk[:, u, :], keys[:, u, :, 2], iota[:, bass.ds(n * 2 + u, 1)], keys[:, u, :, 1],
                                         ALU.is_equal, ALU.mult).then_inc(b_kk, 1)
                dve.wait_ge(b_bank, n * (2 * KS) + (u + 1) * KS)
                for j in range(BT):
                    dve.tensor_scalar(ohS[:, u, j * KS * P:(j + 1) * KS * P], iotaS[:, :], keys[:, u, j, 0:1], None, ALU.is_equal)
                dve.wait_ge(b_kk, n * 2 + u + 1)
                for j in range(BT):
                    last = dve.tensor_scalar(ohB[:, u, j * BN:(j + 1) * BN], iotaB[:, :], kk[:, u, j:j + 1], None, ALU.is_equal)
                last.then_inc(b_oh[u], 1)

            def count_edges(it):
                for k in range(4):
                    m = it * 4 + k
                    dve.wait_ge(c_cnt, m + 1)
                    dve.tensor_tensor(atmost, iota[:, bass.ds(m * TB + (TB - 1), 1)].broadcast_to([P, GE]), raw[RDST],
                                      ALU.is_ge).then_inc(c_ge, 1)
                    dve.wait_ge(c_ge, m + 1)
                    dve.tensor_reduce(counts[:, bass.ds(m, 1)], atmost, AXX, ALU.add).then_inc(c_cnt, 1)

            def round_(R, weights, l=0, messages=False, n0=None):
                with dve.Fori(0, NIT) as it:
                    bases = []
                    q = (l * NIT + it + R.g0) * nwin
                    qw = (it + R.w0) * nwin
                    if messages:
                        count_edges(it)
                    for b in range(2):
                        if n0 is not None:
                            block_onehots(b, it + n0)
                        bases.append(load_base(it, b))
                        make_onehots(b, bases[b], 0, it, qw, weights)
                    for b in range(2):
                        if messages:
                            dve.wait_ge(R.gathered[b], it * (16 * TPG) + 16 * TPG)
                            dve.wait_ge(s_ew[b], it + 1)
                            dve.tensor_tensor(msg[:, b, :], G[:, b, :], ps4[:, b * GE:(b + 1) * GE], ALU.mult).then_inc(s_msg[b], 1)
                        add_sums(b, bases[b], 0, q, q)
                        with dve.If(more > 0):
                            with dve.Fori(1, more + 1) as w:
                                make_onehots(b, bases[b], w, it, qw + w, weights)
                                add_sums(b, bases[b], w, q + w, q)

            def spread(ap):
                return ap.unsqueeze(1).broadcast_to([P, CB, D])

            def per_node(ap):
                return ap.unsqueeze(2).broadcast_to([P, CB, D])

            def stepper(p, c):
                k = [0]

                def step(ins):
                    k[0] += 1
                    ins.then_inc(p["dv"], 1)
                    dve.wait_ge(p["dv"], c * p["steps"] + k[0])
                return step, k

            def normalise(p, c, step, k):
                y3 = blocks(y[:, :])
                step(dve.tensor_reduce(stat[:, 0, :], y3, AXX, ALU.add))
                step(dve.tensor_scalar(stat[:, 0, :], stat[:, 0, :], -1.0 / D, None, ALU.mult))
                step(dve.tensor_tensor(y3, y3, per_node(stat[:, 0, :]), ALU.add))
                assert k[0] == p["centred"]
                dve.wait_ge(p["sq"], c * 2 + 1)
                step(dve.tensor_reduce(stat[:, 1, :], blocks(sq[:, :]), AXX, ALU.add))
                step(dve.tensor_scalar(stat[:, 1, :], stat[:, 1, :], 1.0 / D, EPS, ALU.mult, ALU.add))
                assert k[0] == p["varied"]
                dve.wait_ge(p["sq"], c * 2 + 2)
                step(dve.reciprocal(stat[:, 3, :], stat[:, 2, :]))
                assert k[0] == p["steps"]
                if p is N3:
                    dve.wait_ge(N3["stored"], c + 1)
                dve.tensor_tensor(blocks(xn[:, :]), y3, per_node(stat[:, 3, :]), ALU.mult).then_inc(p["xn"], 1)

            def chunk(table, c):
                return table[:, bass.ds(c * CW, CW)]

            dve.wait_ge(s_xload, 32)
            with dve.Fori(0, NCH) as c:
                dve.tensor_copy(xn[:, :], chunk(X, c)).then_inc(N0["xn"], 1)
                dve.wait_ge(N0["tb"], c + 1)
                dve.wait_ge(N0["stored"], c + 1)
                dve.tensor_copy(msg[:, 0, 0:CW], ps4[:, 0:CW]).then_inc(N0["ev"], 1)

            dve.wait_ge(N0["stored"], NCH + 1)
            dve.wait_ge(s_zero, 1)
            round_(R0, None, messages=True)

            dve.wait_ge(s_pt, 6)
            first, size = starts[:, 0, :], starts[:, 1, :]
            link(dve.tensor_scalar(first[:, 1:NT + 1], psS[0][0:1, 0:NT], -float(PADDED), None, ALU.add))
            link(dve.tensor_tensor(size[:, 0:NT], first[:, 1:NT + 1], first[:, 0:NT], ALU.subtract))
            link(dve.tensor_reduce(badrow[:, 1:2], size[:, 0:NT], AXX, ALU.max))
            link(dve.tensor_scalar(badrow[:, 1:2], badrow[:, 1:2], float(BE), None, ALU.is_gt))
            link(dve.tensor_tensor(badrow[:, 0:1], badrow[:, 0:1], badrow[:, 1:2], ALU.max))
            link(dve.tensor_scalar(badrow[:, 0:1], badrow[:, 0:1], 0.0, None, ALU.is_equal))
            link(dve.tensor_copy(densei[:, :], badrow[:, 0:1]))
            link(dve.tensor_scalar(first[:, 0:NT], first[:, 0:NT], float(E - BE), None, ALU.min))
            link(dve.tensor_copy(starti[:, 0:NT], first[:, 0:NT]))
            dve.sem_inc(c_start, 1)

            with dve.Fori(0, NCH) as c:
                step, k = stepper(N1, c)
                dve.wait_ge(N1["t1"], c + 1)
                step(dve.tensor_tensor(y[:, :], psA[:, 0:CW], chunk(X, c), ALU.add))
                step(dve.tensor_tensor(blocks(y[:, :]), blocks(y[:, :]), spread(b0r[:, :]), ALU.add))
                normalise(N1, c, step, k)
                for k in range(0, CB, 2):
                    dve.wait_ge(N1["tb"], c * CB + k + 1)
                    dve.wait_ge(N1["stored"], c * 4 + k // 2 + 1)
                    dve.tensor_copy(msg[:, 0, :], ps4[:, 0:1024]).then_inc(N1["ev"], 1)

            dve.wait_ge(s_zero, 2)
            round_(R1, wedge, n0=R1N)

            with dve.Fori(0, NCH) as c:
                step, k = stepper(N2, c)
                dve.wait_ge(N2["t1"], c + 1)
                step(dve.tensor_tensor(blocks(y[:, :]), blocks(psA[:, 0:CW]), spread(b1r[:, :]), ALU.add))
                step(dve.scalar_tensor_tensor(y[:, :], y[:, :], 0.0, chunk(X, c), ALU.max, ALU.add))
                normalise(N2, c, step, k)
                dve.wait_ge(N2["tb"], c + 1)
                dve.wait_ge(N2["stored"], c + 1)
                dve.tensor_tensor(msg[:, 0, 0:CB * HID].rearrange("p (b n) -> p b n", n=HID),
                                  ps4[:, 0:CB * 256].rearrange("p (b n) -> p b n", n=256)[:, :, 0:HID],
                                  mb1r[:, :].unsqueeze(1).broadcast_to([P, CB, HID]), ALU.add).then_inc(N2["ev"], 1)

            dve.wait_ge(s_zero, 3)

            def add_expanded(b, q):
                dve.wait_ge(m_exp[b], q + 2)
                h = G[:, b, 0:TPG * HID]
                dve.tensor_tensor(h, h, psA[:, b * 512:b * 512 + TPG * HID], ALU.add).then_inc(m_h[b], 1)

            def add_degrees(b, base, w, q, q0, first):
                last_add(m_dacc, b, 0 if first else w, q, q0)
                dve.wait_ge(m_deg[b], q + 1)
                at = acc[0:1, window(base, w)]
                dve.tensor_tensor(at, at, psS[b][0:1, 0:P], ALU.add).then_inc(m_dacc[b], 1)

            with dve.Fori(0, NIT) as it:
                bases = []
                q = it * nwin
                for b in range(2):
                    bases.append(load_base(it, b))
                    compare(b, bases[b], 0, it).then_inc(m_oh[b], 1)
                for b in range(2):
                    dve.wait_ge(m_gath[b], it * (16 * TPG) + 16 * TPG)
                    add_expanded(b, q)
                    with dve.If(more > 0):
                        with dve.Fori(1, more + 1) as w:
                            compare(b, bases[b], w, it).then_inc(m_oh[b], 1)
                            dve.wait_ge(m_h[b], q + w + 1)
                            add_expanded(b, q + w)
                    dve.wait_ge(m_gelu[b], it + 1)
                    e3 = tiles(hid[:, b, :])
                    dve.tensor_tensor(e3, e3, w2r[:, :].unsqueeze(1).broadcast_to([P, TPG, HID]), ALU.mult).then_inc(m_dot[b], 1)
                    dve.wait_ge(m_dot[b], it * 2 + 1)
                    dve.tensor_reduce(zed[:, b, :], e3, AXX, ALU.add).then_inc(m_dot[b], 1)
                    dve.wait_ge(m_tanh[b], it + 1)
                    dve.tensor_scalar(ews[:, b, :], tanhz[:, b, :], 0.5, 0.5, ALU.mult, ALU.add).then_inc(m_ew[b], 1)
                    dve.tensor_scalar(ewt[:, bass.ds(it * (2 * TPG) + b * TPG, TPG)], tanhz[:, b, :], 0.5, 0.5,
                                      ALU.mult, ALU.add).then_inc(m_ewt, 1)
                    add_degrees(b, bases[b], more, q, q, True)
                    with dve.If(more > 0):
                        with dve.Fori(0, more) as w:
                            compare(b, bases[b], w, it).then_inc(m_oh2[b], 1)
                            add_degrees(b, bases[b], w, q + w + 1, q, False)

            dve.wait_ge(d_sq, 1)
            dve.reciprocal(dinv[:, :], droot[:, :]).then_inc(d_v, 1)
            dve.wait_ge(d_v, 1)
            dve.tensor_tensor(blocks(XT2[:, :]), blocks(XT2[:, :]), dinv[:, :].unsqueeze(2).broadcast_to([P, NB, D]),
                              ALU.mult).then_inc(d_v, 1)
            dve.wait_ge(m_ewt, NG)
            dve.wait_ge(s_zero, 4)
            round_(R2b, ewt, n0=R2N)

            def split(v, c, count):
                hi, mid, lo = (xs[:, bass.ds(c * CB, CB), k, :] for k in range(3))
                rest = blocks(sq[:, :])
                for s, ins in enumerate((lambda: dve.tensor_copy(hi, v),
                                         lambda: dve.tensor_tensor(rest, v, hi, ALU.subtract),
                                         lambda: dve.tensor_copy(mid, rest),
                                         lambda: dve.tensor_tensor(lo, rest, mid, ALU.subtract))):
                    ins().then_inc(x_s, 1)
                    dve.wait_ge(x_s, count * 4 + s + 1)

            dve.wait_ge(d_v, 2)
            for u in range(2):
                dve.wait_ge(b_free[u], NSTEP + 1)
            with dve.Fori(0, NCH) as c:
                step, k = stepper(N3, c)
                dve.wait_ge(N3["t1"], c + 1)
                step(dve.tensor_tensor(y[:, :], psA[:, 0:CW], chunk(XT2, c), ALU.add))
                step(dve.tensor_tensor(blocks(y[:, :]), blocks(y[:, :]), per_node(dinv[:, bass.ds(c * CB, CB)]), ALU.mult))
                step(dve.tensor_tensor(blocks(y[:, :]), blocks(y[:, :]), spread(cbr[:, :]), ALU.add))
                step(dve.tensor_tensor(y[:, :], y[:, :], chunk(X, c), ALU.add))
                normalise(N3, c, step, k)
                dve.wait_ge(N3["xn"], c + 1)
                split(blocks(xn[:, :]), c, c)

            dve.wait_ge(N3["eva"], NCH)
            dense = dense_flag(dve)
            with dve.Fori(0, LAYERS) as l:
                with dve.If(dense < 1):
                    round_(R3, None, l=l)
                with dve.If(dense > 0):
                    with dve.Fori(0, NCI) as i:
                        for r in range(2):
                            dve.wait_ge(a_done[r], l * NCI + i + 2)
                            at = acc[:, bass.ds(i * (2 * CC) + r * CC, CC)]
                            dve.tensor_tensor(at, at, psS[r][:, 0:CC], ALU.add).then_inc(a_add[r], 1)
                dve.wait_ge(l_w, l * 80 + 80)
                pass_waits(dve)
                with dve.Fori(0, NCH) as c:
                    lc = l * NCH + c
                    dve.wait_ge(l_o, lc + 1)
                    dve.wait_ge(l_stored, lc + 1)
                    dve.tensor_tensor(blocks(y[:, :]), blocks(ps4[:, 0:CW]), spread(l3b2r[:, :]), ALU.add).then_inc(l_xo, 1)
                    dve.wait_ge(l_xo, lc + 1)
                    split(blocks(y[:, :]), c, lc + NCH)
                dve.wait_ge(l_acc, l * NCH + NCH)
                pass_waits(dve)

            dve.wait_ge(l_stored, LAYERS * NCH + 1)
            dve.wait_ge(s_xload, 64)
            with dve.Fori(0, NCH) as c:
                step, k = stepper(NF, c)
                step(dve.tensor_tensor(y[:, :], chunk(XT2, c), chunk(X, c), ALU.add))
                normalise(NF, c, step, k)
                dve.wait_ge(NF["xn"], c + 1)
                pass_waits(dve)


_INS = ['x', 'src', 'dst', 'edge_attr_16', 'edge_type_8', 'edge_weight', 'L0_gnn_W', 'L0_gnn_edge_w', 'L0_gnn_b',
        'L1_gnn_weight', 'L1_gnn_bias', 'L2_gnn_mlp_w1', 'L2_gnn_mlp_b1', 'L2_gnn_mlp_w2', 'L2_gnn_mlp_b2',
        'L2_gnn_conv_w', 'L2_gnn_conv_b', 'L3_gnn_W1', 'L3_gnn_b1', 'L3_gnn_W2', 'L3_gnn_b2']
_OUTS = [((6250, 128), 'float32')]


def kernel(**inputs):
    import numpy as _np
    import concourse.bacc as _bacc
    from concourse import mybir as _mybir
    from concourse.bass_utils import run_bass_kernel_spmd as _run

    nc = _bacc.Bacc("TRN2", target_bir_lowering=False, num_devices=1)
    arrays, args = {}, []
    for name in _INS:
        a = _np.ascontiguousarray(inputs[name])
        arrays[f"in_{name}_dram"] = a
        args.append(nc.dram_tensor(f"in_{name}_dram", a.shape, _mybir.dt.from_np(a.dtype), kind="ExternalInput").ap())
    for i, (shape, dtype) in enumerate(_OUTS):
        dt = _mybir.dt.from_np(_np.dtype(dtype))
        args.append(nc.dram_tensor(f"out_{i}_dram", shape, dt, kind="ExternalOutput").ap())
    gnn_program(nc, *args)
    r = _run(nc, [arrays], core_ids=[0])
    got = tuple(r.results[0][f"out_{i}_dram"] for i in range(len(_OUTS)))
    return got[0]
```

```python
from contextlib import ExitStack

import concourse.bass as bass
from concourse import mybir

F32 = mybir.dt.float32
I32 = mybir.dt.int32
F16 = mybir.dt.float16
BF16 = mybir.dt.bfloat16
ALU = mybir.AluOpType
ACT = mybir.ActivationFunctionType
AXX = mybir.AxisListType.X

P = 128
D = 128
HID = 64
EDIM = 16
RELS = 8
LAYERS = 4
TPG = 8
GE = TPG * P
EPS = 1e-5
TB = 32
KS = 4
BT = 5
BE = BT * P
EXACT = 256


def gnn_program(nc, x, src, dst, edge_attr, edge_type, edge_weight, W0, edge_w, b0, W1r, bias1,
                mlp_w1, mlp_b1, mlp_w2, mlp_b2, conv_w, conv_b, L3W1, L3b1, L3W2, L3b2, out):
    N = x.shape[0]
    E = src.shape[0]
    NG = -(-E // GE)
    NIT = NG // 2
    FULL = E // GE
    TAIL = E - FULL * GE
    TAILP = TAIL // TPG
    NB = -(-N // P)
    NPAD = NB * P
    CB = 7
    NCH = NB // CB
    CW = CB * P
    LASTROWS = N - (NB - 1) * P
    MAXBASE = NPAD - P
    NT = NPAD // TB
    SG = -(-NB // KS)
    BN = SG * TB
    TS = KS * BN
    NCB = 14
    CC = NCB * TB
    NCI = NT // (2 * NCB)
    PADDED = NG * GE - E
    assert NG == 2 * NIT and NG == FULL + 1 and TAIL % TPG == 0 and NB == CB * NCH
    assert NT == 4 * NIT and NT == 2 * NCB * NCI and TAIL > EXACT and E >= BE

    with ExitStack() as ctx:
        def sb(name, shape, dt=F32):
            return ctx.enter_context(nc.sbuf_tensor(name, shape, dt))

        def sem(name):
            return ctx.enter_context(nc.semaphore(name))

        def sem2(name):
            return [sem(f"{name}{b}") for b in range(2)]

        def scratch(name, shape, dt=F32):
            return nc.dram_tensor(name, shape, dt, kind="Internal").ap()

        xw_rows = scratch("xw_rows", (NPAD, D))
        ht_rows = scratch("ht_rows", (NPAD * RELS, D))
        ab_rows = scratch("ab_rows", (NPAD, 2 * HID))
        xt_rows = scratch("xt_rows", (NPAD, D))
        x_rows = scratch("x_rows", (NPAD, D))
        x_keep = scratch("x_keep", (NPAD, D))
        key_rows = scratch("key_rows", (E, 3))
        A_rows = scratch("A_rows", (NT, P, TS), BF16)

        big = sb("big", [P, 3 * NPAD + 6 * GE])
        iota = big[:, 0:NPAD]
        XT2 = big[:, NPAD:2 * NPAD]
        X = big[:, 2 * NPAD:3 * NPAD]
        G, onehot, msg = (big[:, 3 * NPAD + k * 2 * GE:3 * NPAD + (k + 1) * 2 * GE].rearrange("p (b n) -> p b n", b=2)
                          for k in range(3))
        Aring = big[:, 0:NCB * TS].bitcast(BF16).rearrange("p (r m t n) -> p r m t n", r=2, m=NCB, n=TB)
        acc = sb("acc", [P, NPAD])
        xsb = sb("xsb", [P, NB * 3 * D // 2])
        xs = xsb[:, :].bitcast(BF16).rearrange("p (t k f) -> p t k f", k=3, f=D)
        taken = [0]

        def part(words):
            taken[0] += words
            return xsb[:, taken[0] - words:taken[0]]
        ohS = part(BT * KS * P).bitcast(BF16).rearrange("p (u n) -> p u n", u=2)
        ohB = part(BT * BN).bitcast(BF16).rearrange("p (u n) -> p u n", u=2)
        Astage = part(TS).bitcast(BF16).rearrange("p (u s k n) -> p u s k n", u=2, s=SG, k=KS)
        hid = part(2 * TPG * HID).rearrange("p (b n) -> p b n", b=2)
        EWb = part(TPG * D).rearrange("p (j f) -> p j f", j=TPG)
        W1s = part(RELS * D).rearrange("p (r f) -> p r f", r=RELS)
        iotaS = sb("iotaS", [P, KS * P], F16)
        iotaB = sb("iotaB", [P, BN], F16)
        keys = sb("keys", [P, 2, BT, 3])
        kk = sb("kk", [P, 2, BT])
        starts = sb("starts", [1, 2, NT + 4])
        starti = sb("starti", [1, NT + 4], I32)
        densei = sb("densei", [1, 1], I32)
        attr = sb("attr", [P, 2, TPG * EDIM])
        attrT = sb("attrT", [P, 2, P])
        bwin = sb("bwin", [P, 2, HID])
        srci = sb("srci", [P, NG * TPG + 2 * TPG], I32)
        reli = sb("reli", [P, NG * TPG], I32)
        dstf = sb("dstf", [P, NG * TPG])
        wedge = sb("wedge", [P, NG * TPG])
        ewt = wedge
        idx = sb("idx", [P, 2, TPG], I32)
        zed = sb("zed", [P, 2, TPG])
        tanhz = sb("tanhz", [P, 2, TPG])
        ews = sb("ews", [P, 2, TPG])
        stT = sb("stT", [P, CW])
        y = sb("y", [P, CW])
        sq = sb("sq", [P, CW])
        xn = sb("xn", [P, CW])
        xTs = sb("xTs", [P, CW])
        n1stage = [buf[:, b, :] for buf in (msg, onehot) for b in range(2)]
        l3stage = (y, xn)
        ident = sb("ident", [P, P])
        pcol = sb("pcol", [P, 1])
        stat = sb("stat", [P, 4, CB])
        dinv = sb("dinv", [P, NB])
        droot = sb("droot", [P, NB])
        onec = sb("onec", [P, 1])
        small = sb("small", [P, 8])
        rowf = sb("rowf", [1, 4, NG])
        badrow = sb("badrow", [1, 4])
        basei = sb("basei", [1, NG], I32)
        nwini = sb("nwini", [1, 2], I32)
        one11 = sb("one11", [1, 1])
        W0s = sb("W0s", [P, D])
        W2s = sb("W2s", [P, 2 * HID + D])
        WA = sb("WA", [P, D])
        WB = sb("WB", [P, D])
        b0r = sb("b0r", [P, D])
        b1r = sb("b1r", [P, D])
        cbr = sb("cbr", [P, D])
        mb1r = sb("mb1r", [P, HID])
        w2r = sb("w2r", [P, HID])
        mb2r = sb("mb2r", [P, 1])
        l3b2r = sb("l3b2r", [P, D])
        l3b1c = sb("l3b1c", [P, 1])
        l3b2c = sb("l3b2c", [P, 1])

        raw = [XT2[:, k * GE:(k + 1) * GE] for k in range(4)]
        RSRC, RDST, RTYP, RWGT = range(4)
        atmost = XT2[:, 4 * GE:5 * GE]
        counts = XT2[:, 5 * GE:5 * GE + NT]
        keyraw = acc[:, 0:3 * GE].rearrange("p (e k) -> p e k", k=3)
        next1 = acc[:, 3 * GE:4 * GE]
        nextx = acc[:, 4 * GE:5 * GE]
        xchunks = X[:, :].rearrange("p (b f) -> p b f", f=D)

        psS = [ctx.enter_context(nc.psum_tensor(f"psS{b}", [P, 512], F32)) for b in range(2)]
        psA = ctx.enter_context(nc.psum_tensor("psA", [P, 1024], F32))
        ps4 = ctx.enter_context(nc.psum_tensor("ps4", [P, 2048], F32))

        s_load = sem("s_load")
        s_wload = sem("s_wload")
        s_xload = sem("s_xload")
        s_fill = sem("s_fill")
        s_iota = sem("s_iota")
        s_ident = sem("s_ident")
        s_chain = sem("s_chain")
        s_prep = sem("s_prep")
        s_plan = sem("s_plan")
        s_pt = sem("s_pt")
        s_pe = sem("s_pe")
        s_zero = sem("s_zero")
        c_keys = sem("c_keys")
        c_list = sem("c_list")
        c_ge = sem("c_ge")
        c_cnt = sem("c_cnt")
        c_start = sem("c_start")
        b_keys = sem2("b_keys")
        b_kk = sem("b_kk")
        b_oh = sem2("b_oh")
        b_bank = sem("b_bank")
        b_ev = sem("b_ev")
        b_dma = sem2("b_dma")
        b_free = sem2("b_free")
        a_ready = sem2("a_ready")
        a_done = sem2("a_done")
        a_add = sem2("a_add")
        x_s = sem("x_s")
        f_part = sem("f_part")
        s_gate = sem("s_gate")

        r_idx = sem2("r_idx")
        r_ohraw = sem2("r_ohraw")
        r_oh = sem2("r_oh")
        r_seg = sem2("r_seg")
        r_acc = sem2("r_acc")

        class Round:
            def __init__(self, number, weighted, gathered, first):
                self.g0 = number * NIT
                self.w0 = weighted * NIT
                self.gathered = gathered
                self.d0 = first * NIT

        r_gath = sem2("r_gath")
        l_gath = sem2("l_gath")
        R0, R1, R2b, R3 = Round(0, 0, r_gath, 0), Round(1, 0, r_gath, 1), Round(2, 1, r_gath, 2), Round(3, 0, l_gath, 0)
        s_attr = sem2("s_attr")
        s_attrp = sem2("s_attrp")
        s_attrT = sem2("s_attrT")
        s_ew = sem2("s_ew")
        s_msg = sem2("s_msg")
        m_idx = sem2("m_idx")
        m_gath = sem2("m_gath")
        m_oh = sem2("m_oh")
        m_tp = sem2("m_tp")
        m_ohT = sem2("m_ohT")
        m_bwin = sem2("m_bwin")
        m_exp = sem2("m_exp")
        m_h = sem2("m_h")
        m_gelu = sem2("m_gelu")
        m_dot = sem2("m_dot")
        m_tanh = sem2("m_tanh")
        m_ew = sem2("m_ew")
        m_ewt = sem("m_ewt")
        s_half = sem("s_half")
        m_oh2 = sem2("m_oh2")
        m_deg = sem2("m_deg")
        m_dacc = sem2("m_dacc")
        d_t = sem("d_t")
        d_sq = sem("d_sq")
        d_v = sem("d_v")
        d_out = sem("d_out")

        def phase(name, steps, kinds):
            p = {kind: sem(f"{name}_{kind}") for kind in kinds.split()}
            return {**p, "steps": steps, "centred": steps - 3, "varied": steps - 1}

        norm = "dv sq xn xs "
        N0 = phase("n0", 0, "xn t2 xT tb ev dma stored")
        N1 = phase("n1", 8, norm + "st t1 t2 xT tb eva dma dmb stored")
        N2 = phase("n2", 8, norm + "st t1 t2 xT tb ev eva eva2 dma stored")
        N3 = phase("n3", 10, norm + "st t1 t2 eva dma stored")
        NF = phase("nf", 7, norm + "dma")
        l_w = sem("l_w")
        l_h = sem("l_h")
        l_relu = sem("l_relu")
        l_o = sem("l_o")
        l_acc = sem("l_acc")
        l_xo = sem("l_xo")
        l_dma = sem("l_dma")
        l_stored = sem("l_stored")

        def pass_waits(eng):
            eng.sem_inc(s_gate, 1)

        def as_row(v):
            return v.rearrange("(a n) -> a n", a=1)

        def window(base, w):
            if isinstance(w, int) and w == 0:
                return bass.ds(base, P)
            at = nc.s_assert_within(base + w * P, 0, MAXBASE, skip_runtime_bounds_check_because=
                                    "more than one window only from base 0")
            return bass.ds(at, P)

        def window_count(eng):
            return (eng.value_load(nwini[0:1, 0:1], min_val=1, max_val=NB),
                    eng.value_load(nwini[0:1, 1:2], min_val=0, max_val=NB - 1))

        def blocks(ap):
            return ap.rearrange("p (b f) -> p b f", f=D)

        def dense_flag(eng):
            return eng.value_load(densei[0:1, 0:1], min_val=0, max_val=1)

        R1N, R2N = 0, NIT
        NSTEP = 2 * NIT

        ALLW = 16 * (TPG + 11)

        block = ctx.enter_context(nc.Block())


        @block.sync
        def _(sp):
            sp.wait_ge(s_fill, 1)
            for r, a in ((RSRC, src), (RDST, dst), (RTYP, edge_type), (RWGT, edge_weight)):
                v = raw[r] if r == RWGT else raw[r].bitcast(I32)
                sp.dma_start(v[0:FULL, :], a[0:FULL * GE].rearrange("(g e) -> g e", e=GE)).then_inc(s_load, 16)
                sp.dma_start(v[FULL:FULL + 1, 0:TAIL], as_row(a[FULL * GE:E])).then_inc(s_load, 16)
            for v, shift in ((next1.bitcast(I32), 1), (nextx.bitcast(I32), EXACT)):
                sp.dma_start(v[0:FULL, :], dst[shift:FULL * GE + shift].rearrange("(g e) -> g e", e=GE)).then_inc(s_load, 16)
                sp.dma_start(v[FULL:FULL + 1, 0:TAIL - shift], as_row(dst[FULL * GE + shift:E])).then_inc(s_load, 16)
            sp.dma_start(blocks(X[:, 0:(NB - 1) * P]), x[0:(NB - 1) * P, :].rearrange("(b p) f -> p b f", p=P)).then_inc(s_xload, 16)
            sp.dma_start(X[0:LASTROWS, (NB - 1) * P:NPAD], x[(NB - 1) * P:N, :]).then_inc(s_xload, 16)
            for j in range(TPG):
                sp.dma_start(EWb[j * EDIM:(j + 1) * EDIM, j, :], edge_w[:, :]).then_inc(s_wload, 16)
            loads = [(W0s[:, :], W0[:, :]), (W1s[:, :, :], W1r.rearrange("r i o -> i r o")),
                     (W2s[:, 0:HID], mlp_w1[0:D, :]), (W2s[:, HID:2 * HID], mlp_w1[D:2 * D, :]),
                     (W2s[:, 2 * HID:], conv_w[:, :]),
                     (b0r[:, :], as_row(b0).broadcast_to([P, D])), (b1r[:, :], as_row(bias1).broadcast_to([P, D])),
                     (cbr[:, :], as_row(conv_b).broadcast_to([P, D])), (mb1r[:, :], as_row(mlp_b1).broadcast_to([P, HID])),
                     (w2r[:, :], mlp_w2.rearrange("h a -> a h").broadcast_to([P, HID])),
                     (mb2r[:, :], as_row(mlp_b2).broadcast_to([P, 1]))]
            for o, i in loads:
                sp.dma_start(o, i).then_inc(s_wload, 16)

            def rows_of(table, c):
                return table.rearrange("(b p) f -> p b f", p=P)[:, bass.ds(c * CB, CB), :]

            sp.sem_inc(N1["stored"], 3)
            for s in (N0["stored"], N2["stored"], N3["stored"], l_stored, *b_free):
                sp.sem_inc(s, 1)

            sp.wait_ge(c_keys, 1)
            sp.dma_start(key_rows[0:FULL * GE, :].rearrange("(g e) k -> g (e k)", e=GE), acc[0:FULL, 0:3 * GE]).then_inc(c_list, 16)
            sp.dma_start(key_rows[FULL * GE:E, :].rearrange("(a e) k -> a (e k)", a=1), acc[FULL:FULL + 1, 0:3 * TAIL]).then_inc(c_list, 16)

            with sp.Fori(0, NCH) as c:
                sp.wait_ge(N0["ev"], c + 2)
                pass_waits(sp)
                sp.dma_start(rows_of(xw_rows, c), blocks(msg[:, 0, 0:CW])).then_inc(N0["dma"], 16)
                sp.wait_ge(N0["dma"], 16 * c + 16)
                sp.sem_inc(N0["stored"], 1)

            def load_attr(b, it, g, parts):
                sp.wait_ge(s_attrp[b], it + 1)
                pass_waits(sp)
                sp.dma_start(attr[0:parts, b, :],
                             edge_attr[bass.ds(g * GE, parts * TPG), :].rearrange("(p j) k -> p (j k)", j=TPG)
                             ).then_inc(s_attr[b], 16)
            with sp.Fori(0, NIT - 1) as it:
                for b in range(2):
                    load_attr(b, it, it * 2 + b, P)
            load_attr(0, NIT - 1, NG - 2, P)
            load_attr(1, NIT - 1, NG - 1, TAILP)

            def load_keys(u, m):
                start = sp.value_load(starti[0:1, bass.ds(m, 1)], min_val=0, max_val=E - BE)
                sp.dma_start(keys[:, u, :, :], key_rows[bass.ds(start, BE), :].rearrange("(p j) k -> p j k", j=BT)
                             ).then_inc(b_keys[u], 16)

            def block_traffic(n0):
                with sp.Fori(0, NIT) as it:
                    n = it + n0
                    for u in range(2):
                        sp.wait_ge(b_oh[u], n + 2)
                        pass_waits(sp)
                        load_keys(u, n * 2 + 2 + u)
                    for u in range(2):
                        sp.wait_ge(b_dma[u], n * 16 + 16)
                        sp.sem_inc(b_free[u], 1)
            sp.wait_ge(c_start, 1)
            for u in range(2):
                load_keys(u, u)

            ht = ht_rows.rearrange("(b p r) f -> b p (r f)", p=P, r=RELS)
            with sp.Fori(0, NCH) as c:
                def stored(k):
                    done, per = ((N1["dma"], 4), (N1["dmb"], 3))[k % 2]
                    sp.wait_ge(done, 16 * (c * per + k // 2) + 16)
                    sp.sem_inc(N1["stored"], 1)
                for k in range(CB):
                    done = (N1["dma"], N1["dmb"])[k % 2]
                    sp.wait_ge(N1["eva"], c * CB + k + 2)
                    pass_waits(sp)
                    sp.dma_start(ht[bass.ds(c * CB + k, 1)].rearrange("a p n -> (a p) n"), n1stage[k % 4]).then_inc(done, 16)
                    if k:
                        stored(k - 1)
                stored(CB - 1)

            block_traffic(R1N)

            with sp.Fori(0, NCH) as c:
                sp.wait_ge(N2["ev"], c + 2)
                pass_waits(sp)
                sp.wait_ge(N2["eva"], c + 1)
                pass_waits(sp)
                sp.dma_start(rows_of(ab_rows, c), blocks(msg[:, 0, 0:CW])).then_inc(N2["dma"], 16)
                sp.wait_ge(N2["dma"], 16 * c + 16)
                sp.sem_inc(N2["stored"], 1)

            nwin, more = window_count(sp)

            def load_window(b, base, w, q):
                sp.wait_ge(m_exp[b], q + 1)
                pass_waits(sp)
                sp.dma_start(bwin[:, b, :], ab_rows[window(base, w), HID:2 * HID]).then_inc(m_bwin[b], 16)
            def window_base(it, b):
                return sp.value_load(basei[0:1, bass.ds(it * 2 + b, 1)], min_val=0, max_val=MAXBASE)

            def windows_step(it, last):
                for b in range(2):
                    if not (last and b):
                        load_window(1 - b, window_base(it + b, 1 - b), 0, (it + b) * nwin)
                    with sp.If(more > 0):
                        base = window_base(it, b)
                        with sp.Fori(1, more + 1) as w:
                            load_window(b, base, w, it * nwin + w)
            load_window(0, window_base(0, 0), 0, 0)
            with sp.Fori(0, NIT - 1) as it:
                windows_step(it, False)
            windows_step(NIT - 1, True)

            sp.wait_ge(d_v, 2)
            sp.dma_start(xt_rows.rearrange("(b p) f -> p b f", p=P), blocks(XT2[:, :])).then_inc(d_out, 16)

            block_traffic(R2N)

            with sp.Fori(0, NCH) as c:
                sp.wait_ge(N3["xn"], c + 1)
                pass_waits(sp)
                for table in (x_rows, x_keep):
                    sp.dma_start(rows_of(table, c), blocks(xn[:, :])).then_inc(N3["dma"], 16)
                sp.wait_ge(N3["dma"], 32 * c + 32)
                sp.sem_inc(N3["stored"], 1)

            sp.wait_ge(N3["xs"], NCH)
            for u in range(2):
                sp.wait_ge(b_dma[u], 16 * NSTEP)
            dense = dense_flag(sp)
            with sp.If(dense > 0):
                with sp.Fori(0, LAYERS) as l:
                    with sp.Fori(0, NCI) as i:
                        for r in range(2):
                            sp.wait_ge(a_done[r], l * NCI + i + 1)
                            pass_waits(sp)
                            for h in range(2):
                                half = NCB // 2
                                sp.dma_start(Aring[:, r, h * half:(h + 1) * half, :, :].rearrange("p m t n -> p m (t n)"),
                                             A_rows[bass.ds(i * (2 * NCB) + r * NCB + h * half, half), :, :].rearrange("m p c -> p m c")
                                             ).then_inc(a_ready[r], 16)

                for r in range(2):
                    sp.wait_ge(a_done[r], LAYERS * NCI + 1)

            sp.dma_start(blocks(X[:, :]), x_keep.rearrange("(b p) f -> p b f", p=P)).then_inc(s_xload, 16)
            sp.wait_ge(s_xload, 48)
            for c in range(NCH):
                sp.wait_ge(l_stored, (LAYERS - 1) * NCH + c + 2)
                sp.dma_start(blocks(XT2[:, c * CW:(c + 1) * CW]),
                             x_rows.rearrange("(b p) f -> p b f", p=P)[:, c * CB:(c + 1) * CB, :]).then_inc(s_xload, 16)
                sp.wait_ge(s_xload, c * 16 + 64)
                sp.sem_inc(f_part, 1)

            for c in range(NCH):
                sp.wait_ge(NF["xs"], c + 1)
                whole = CB if c < NCH - 1 else CB - 1
                lo = c * CW
                sp.dma_start(out[lo:lo + whole * P, :].rearrange("(b p) f -> p b f", p=P), blocks(X[:, lo:lo + whole * P])
                             ).then_inc(NF["dma"], 16)
            sp.dma_start(out[(NB - 1) * P:N, :], X[0:LASTROWS, (NB - 1) * P:NPAD]).then_inc(NF["dma"], 16)
            sp.wait_ge(NF["dma"], 16 * NCH + 16)

        @block.gpsimd
        def _(pool):
            pool.iota(iota[:, :], [[1, NPAD]], base=0, channel_multiplier=0,
                      allow_small_or_imprecise_dtypes=True).then_inc(s_iota, 1)
            pool.iota(pcol[:, :], [[0, 1]], base=0, channel_multiplier=1,
                      allow_small_or_imprecise_dtypes=True).then_inc(s_iota, 1)
            pool.wait_ge(c_list, 32)
            pool.wait_ge(s_prep, 1)
            pool.memset(acc[:, :], 0.0).then_inc(s_zero, 1)

            def gathers(it, idx_ready, gathered, table):
                for b in range(2):
                    pool.wait_ge(idx_ready[b], it + 1)
                    pass_waits(pool)
                    for j in range(TPG):
                        pool.indirect_dma_start(G[:, b, j * D:(j + 1) * D], None, table[:, :],
                                                bass.IndirectOffsetOnAxis(ap=idx[:, b, j:j + 1], axis=0)
                                                ).then_inc(gathered[b], 16)

            def zero_acc(read, count):
                pool.wait_ge(read, count)
                pool.memset(acc[:, :], 0.0).then_inc(s_zero, 1)

            pool.wait_ge(N0["stored"], NCH + 1)
            with pool.Fori(0, NIT) as it:
                gathers(it, r_idx, R0.gathered, xw_rows)
            zero_acc(N1["st"], NCH)
            pool.wait_ge(N1["stored"], NCH * CB + 3)
            with pool.Fori(0, NIT) as it:
                gathers(it + R1.g0, r_idx, R1.gathered, ht_rows)
            zero_acc(N2["st"], NCH)
            pool.wait_ge(N2["stored"], NCH + 1)
            with pool.Fori(0, NIT) as it:
                gathers(it, m_idx, m_gath, ab_rows)
            zero_acc(d_t, 1)
            pool.wait_ge(d_out, 16)
            with pool.Fori(0, NIT) as it:
                gathers(it + R2b.g0, r_idx, R2b.gathered, xt_rows)
            pool.wait_ge(N3["stored"], NCH + 1)
            dense = dense_flag(pool)
            with pool.Fori(0, LAYERS) as l:
                with pool.If(dense < 1):
                    with pool.Fori(0, NIT) as it:
                        gathers(l * NIT + it + R3.g0, r_idx, R3.gathered, x_rows)
                for c in range(NCH):
                    pool.wait_ge(l_xo, l * NCH + c + 1)
                    pass_waits(pool)
                    pool.dma_start(x_rows.rearrange("(b p) f -> p b f", p=P)[:, c * CB:(c + 1) * CB, :],
                                   blocks(l3stage[c % 2][:, :])).then_inc(l_dma, 16)
                    pool.wait_ge(l_dma, (l * NCH + c) * 16 + 16)
                    pool.sem_inc(l_stored, 1)

        @block.scalar
        def _(act):
            act.wait_ge(s_plan, 1)
            nwin, more = window_count(act)

            act.sem_inc(N1["eva"], 1)
            act.sem_inc(N2["eva2"], 1)
            act.sem_inc(b_ev, KS)

            def stage_idx(b, it, free, count, idx_ready, lists):
                act.wait_ge(free[b], count + 1)
                pass_waits(act)
                act.copy(idx[:, b, :], lists[:, bass.ds(it * (2 * TPG) + b * TPG, TPG)]).then_inc(idx_ready[b], 1)

            def index_round(R, lists, l=0):
                with act.Fori(0, NIT) as it:
                    for b in range(2):
                        stage_idx(b, it, r_seg, (l * NIT + it + R.g0) * nwin, r_idx, lists)

            def block_stage(u, n):
                m = n * 2 + u
                act.wait_ge(b_free[u], n + 1)
                for k in range(KS):
                    act.wait_ge(b_bank, m * KS + 2 * KS + k + 1)
                    act.copy(Astage[:, u, :, k, :], ps4[:, k * 512:k * 512 + BN].rearrange("p (s n) -> p s n", n=TB)).then_inc(b_ev, 1)
                act.wait_ge(b_ev, m * KS + 2 * KS)
                pass_waits(act)
                act.dma_start(A_rows[bass.ds(m, 1), :, :].rearrange("a p c -> (a p) c"),
                              Astage[:, u, :, :, :].rearrange("p s k n -> p (s k n)")).then_inc(b_dma[u], 16)

            def index_and_stage_round(R, lists, n0):
                for b in range(2):
                    stage_idx(b, 0, r_seg, R.g0 * nwin, r_idx, lists)
                with act.Fori(0, NIT - 1) as it:
                    for b in range(2):
                        block_stage(b, it + n0)
                        stage_idx(b, it + 1, r_seg, (it + 1 + R.g0) * nwin, r_idx, lists)
                for b in range(2):
                    block_stage(b, NIT - 1 + n0)

            def squares(p, c):
                act.wait_ge(p["dv"], c * p["steps"] + p["centred"])
                act.activation(sq[:, :], y[:, :], ACT.Square).then_inc(p["sq"], 1)

            def root(p, c):
                act.wait_ge(p["dv"], c * p["steps"] + p["varied"])
                act.activation(stat[:, 2, :], stat[:, 1, :], ACT.Sqrt).then_inc(p["sq"], 1)

            def keep(p, c):
                act.wait_ge(p["xn"], c + 1)
                pass_waits(act)
                act.copy(X[:, bass.ds(c * CW, CW)], xn[:, :]).then_inc(p["xs"], 1)

            def norm_steps(p, c):
                squares(p, c)
                root(p, c)
                keep(p, c)

            def stage_acc(p, c):
                act.copy(stT[:, :], acc[:, bass.ds(c * CW, CW)]).then_inc(p["st"], 1)

            def transposed(p, c):
                act.wait_ge(p["t2"], c + 1)
                act.copy(xTs[:, :], psA[:, 0:CW]).then_inc(p["xT"], 1)

            def summed(R):
                for b in range(2):
                    act.wait_ge(r_acc[b], (R.g0 + NIT) * nwin + 1)

            with act.Fori(0, NCH) as c:
                transposed(N0, c)

            with act.Fori(0, NIT) as it:
                for b in range(2):
                    stage_idx(b, it, r_seg, it * nwin, r_idx, srci)
                for b in range(2):
                    act.wait_ge(s_attrp[b], it + 2)
                    act.copy(attrT[:, b, :], psA[:, b * 512:b * 512 + P]).then_inc(s_attrT[b], 1)

            summed(R0)
            def evacuate(c, blocks_):
                for k in blocks_:
                    n = c * CB + k
                    act.wait_ge(N1["tb"], n + 1)
                    act.wait_ge(N1["stored"], n + 1)
                    act.copy(n1stage[k % 4], ps4[:, (k % 2) * 1024:(k % 2 + 1) * 1024]).then_inc(N1["eva"], 1)
            stage_acc(N1, 0)
            norm_steps(N1, 0)
            transposed(N1, 0)
            with act.Fori(0, NCH - 1) as c:
                stage_acc(N1, c + 1)
                evacuate(c, (0, 1, 2))
                squares(N1, c + 1)
                evacuate(c, (3,))
                root(N1, c + 1)
                evacuate(c, (4, 5))
                keep(N1, c + 1)
                evacuate(c, (6,))
                transposed(N1, c + 1)
            evacuate(NCH - 1, range(CB))

            index_and_stage_round(R1, reli, R1N)

            summed(R1)
            def evacuate_products(c):
                act.wait_ge(N2["tb"], c + 1)
                act.wait_ge(N2["ev"], c + 2)
                act.wait_ge(N2["stored"], c + 1)
                rows = ps4[:, 0:CB * 256].rearrange("p (b n) -> p b n", n=256)
                act.copy(blocks(msg[:, 0, 0:CW])[:, :, HID:], rows[:, :, HID:2 * HID]).then_inc(N2["eva"], 1)
                act.copy(blocks(XT2[:, bass.ds(c * CW, CW)]), rows[:, :, 2 * HID:]).then_inc(N2["eva2"], 1)
            stage_acc(N2, 0)
            norm_steps(N2, 0)
            transposed(N2, 0)
            with act.Fori(0, NCH - 1) as c:
                stage_acc(N2, c + 1)
                squares(N2, c + 1)
                evacuate_products(c)
                root(N2, c + 1)
                keep(N2, c + 1)
                transposed(N2, c + 1)
            evacuate_products(NCH - 1)

            def turned_onehots(b, q):
                act.wait_ge(m_tp[b], q + 2)
                act.copy(msg[:, b, :], ps4[:, b * GE:(b + 1) * GE]).then_inc(m_ohT[b], 1)
            act.wait_ge(N2["stored"], NCH + 1)
            act.wait_ge(s_half, 1)
            for b in range(2):
                act.copy(idx[:, b, :], srci[:, b * TPG:(b + 1) * TPG]).then_inc(m_idx[b], 1)
            def edge_weights_step(it, last):
                for b in range(2):
                    with act.If(more > 0):
                        if not (last and b):
                            turned_onehots(1 - b, (it + b) * nwin)
                        with act.Fori(1, more + 1) as w:
                            turned_onehots(b, it * nwin + w)
                    if not last:
                        stage_idx(b, it + 1, m_h, it * nwin + 1, m_idx, srci)
                    act.wait_ge(m_h[b], it * nwin + nwin + 1)
                    act.activation(hid[:, b, :], hid[:, b, :], ACT.Gelu).then_inc(m_gelu[b], 1)
                    act.wait_ge(m_dot[b], it * 2 + 2)
                    act.activation(tanhz[:, b, :], zed[:, b, :], ACT.Tanh, bias=mb2r[:, :], scale=0.5).then_inc(m_tanh[b], 1)
                    if not (last and b):
                        with act.If(more < 1):
                            turned_onehots(1 - b, (it + b) * nwin)
            turned_onehots(0, 0)
            with act.Fori(0, NIT - 1) as it:
                edge_weights_step(it, False)
            edge_weights_step(NIT - 1, True)
            act.wait_ge(d_t, 1)
            act.activation(droot[:, :], ps4[:, 0:NB], ACT.Sqrt, bias=onec[:, :]).then_inc(d_sq, 1)

            index_and_stage_round(R2b, srci, R2N)

            summed(R2b)
            with act.Fori(0, NCH) as c:
                stage_acc(N3, c)
                norm_steps(N3, c)
                act.wait_ge(N3["t2"], c + 1)
                pass_waits(act)
                act.copy(acc[:, bass.ds(c * CW, CW)], psA[:, 0:CW]).then_inc(N3["eva"], 1)

            dense = dense_flag(act)
            with act.Fori(0, LAYERS) as l:
                act.dma_start(WA[:, :], L3W1[bass.ds(l, 1)].rearrange("a i o -> (a i) o")).then_inc(l_w, 16)
                act.dma_start(WB[:, :], L3W2[bass.ds(l, 1)].rearrange("a i o -> (a i) o")).then_inc(l_w, 16)
                act.dma_start(l3b2r[:, :], L3b2[bass.ds(l, 1), :].broadcast_to([P, D])).then_inc(l_w, 16)
                act.dma_start(l3b1c[:, :], L3b1[bass.ds(l, 1), :].rearrange("a f -> f a")).then_inc(l_w, 16)
                act.dma_start(l3b2c[:, :], L3b2[bass.ds(l, 1), :].rearrange("a f -> f a")).then_inc(l_w, 16)
                with act.If(dense < 1):
                    index_round(R3, srci, l)
                for c in range(NCH):
                    act.wait_ge(l_h, l * NCH + c + 1)
                    act.activation(xTs[:, :], psA[:, 0:CW], ACT.Relu, bias=l3b1c[:, :]).then_inc(l_relu, 1)
                    act.wait_ge(l_o, l * NCH + c + 1)
                    act.activation(acc[:, c * CW:(c + 1) * CW], ps4[:, 1024:1024 + CW], ACT.Identity,
                                   bias=l3b2c[:, :]).then_inc(l_acc, 1)
                act.wait_ge(l_acc, l * NCH + NCH)
                act.wait_ge(l_xo, l * NCH + NCH)
                pass_waits(act)

            act.wait_ge(s_xload, 48)
            with act.Fori(0, NCH) as c:
                norm_steps(NF, c)

        @block.tensor
        def _(pe):
            pe.wait_ge(s_ident, 1)
            for r in range(4):
                pe.wait_ge(s_prep, r + 1)
                if r >= 1:
                    pe.wait_ge(s_pe, r)
                v = raw[r].rearrange("g (p j) -> g j p", j=TPG)
                for j in range(TPG):
                    m = pe.transpose(ps4[:, j * P:j * P + NG], v[0:NG, j, :], ident[0:NG, 0:NG])
                m.then_inc(s_pt, 1)
            pe.wait_ge(s_prep, 5)
            pe.transpose(psA[0:1, 0:NG], small[0:NG, 0:1], ident[0:NG, 0:NG])
            pe.transpose(psA[0:1, P:P + NG], small[0:NG, 1:2], ident[0:NG, 0:NG])
            pe.transpose(psA[0:1, 2 * P:2 * P + NG], small[0:NG, 2:3], ident[0:NG, 0:NG]).then_inc(s_pt, 1)
            pe.wait_ge(s_plan, 1)
            nwin, more = window_count(pe)
            pe.wait_ge(s_wload, ALLW)

            def turn_chunk(source, done):
                for k in range(CB):
                    m = pe.transpose(psA[:, k * P:(k + 1) * P], source[:, k * P:(k + 1) * P], ident[:, :])
                m.then_inc(done, 1)

            def window_sums(rows, b, q):
                pe.wait_ge(r_oh[b], q + 1)
                pe.wait_ge(r_acc[b], q + 1)
                for j in range(TPG):
                    m = pe.matmul(psS[b][:, 0:P], rows[:, b, j * P:(j + 1) * P], onehot[:, b, j * P:(j + 1) * P],
                                  start=(j == 0), stop=(j == TPG - 1))
                m.then_inc(r_seg[b], 1)

            def segment_sums(rows, b, q0):
                window_sums(rows, b, q0)
                with pe.If(more > 0):
                    with pe.Fori(1, more + 1) as w:
                        window_sums(rows, b, q0 + w)

            def plain_round(R, l=0):
                with pe.Fori(0, NIT) as it:
                    for b in range(2):
                        pe.wait_ge(R.gathered[b], (l * NIT + it + R.d0) * (16 * TPG) + 16 * TPG)
                        segment_sums(G, b, (l * NIT + it + R.g0) * nwin)

            def block_counts(u, n):
                m = n * 2 + u
                pe.wait_ge(b_oh[u], n + 2)
                for k in range(KS):
                    pe.wait_ge(b_ev, m * KS + k + 1)
                    for j in range(BT):
                        mm = pe.matmul(ps4[:, k * 512:k * 512 + BN], ohS[:, u, (j * KS + k) * P:(j * KS + k + 1) * P],
                                       ohB[:, u, j * BN:(j + 1) * BN], start=(j == 0), stop=(j == BT - 1))
                    mm.then_inc(b_bank, 1)

            def counting_round(R, n0):
                with pe.Fori(0, NIT) as it:
                    for b in range(2):
                        block_counts(b, it + n0)
                        pe.wait_ge(R.gathered[b], (it + R.d0) * (16 * TPG) + 16 * TPG)
                        segment_sums(G, b, (it + R.g0) * nwin)

            pe.sem_inc(b_bank, 2 * KS)
            for b in range(2):
                pe.sem_inc(a_done[b], 1)
                pe.sem_inc(r_seg[b], 1)
                pe.sem_inc(s_attrp[b], 1)
                pe.sem_inc(m_tp[b], 1)
                pe.sem_inc(m_exp[b], 1)

            with pe.Fori(0, NCH) as c:
                pe.wait_ge(N0["xn"], c + 1)
                turn_chunk(xn, N0["t2"])
                pe.wait_ge(N0["xT"], c + 1)
                pe.wait_ge(N0["ev"], c + 1)
                for k in range(CB):
                    m = pe.matmul(ps4[:, k * P:(k + 1) * P], xTs[:, k * P:(k + 1) * P], W0s[:, :], start=True, stop=True)
                m.then_inc(N0["tb"], 1)

            pe.wait_ge(N0["ev"], NCH + 1)
            with pe.Fori(0, NIT) as it:
                for b in range(2):
                    pe.wait_ge(s_attr[b], 16 * it + 16)
                    pe.transpose(psA[:, b * 512:b * 512 + P], attr[:, b, :], ident[:, :]).then_inc(s_attrp[b], 1)
                for b in range(2):
                    pe.wait_ge(s_attrT[b], it + 1)
                    pe.wait_ge(s_msg[b], it + 1)
                    for h in range(2):
                        m = pe.matmul(ps4[:, b * GE + h * 512:b * GE + (h + 1) * 512], attrT[:, b, :],
                                      EWb[:, 4 * h:4 * h + 4, :].rearrange("p j f -> p (j f)"), start=True, stop=True)
                    m.then_inc(s_ew[b], 1)
                for b in range(2):
                    pe.wait_ge(s_msg[b], it + 2)
                    segment_sums(msg, b, it * nwin)

            pe.wait_ge(c_cnt, NT + 1)
            pe.wait_ge(r_acc[0], NIT * nwin + 1)
            pe.matmul(psS[0][0:1, 0:NT], onec[0:NG, :], counts[0:NG, :], start=True, stop=True).then_inc(s_pt, 1)

            def turn_sums(p, c):
                pe.wait_ge(p["st"], c + 1)
                turn_chunk(stT, p["t1"])

            def turn_x(p, c):
                pe.wait_ge(p["xn"], c + 1)
                turn_chunk(xn, p["t2"])

            def relation_rows(c):
                for k in range(CB):
                    pe.wait_ge(N1["eva"], c * CB + k + (0 if k else 1))
                    for h in range(2):
                        m = pe.matmul(ps4[:, (k % 2) * 1024 + h * 512:(k % 2) * 1024 + (h + 1) * 512], xTs[:, k * P:(k + 1) * P],
                                      W1s[:, 4 * h:4 * h + 4, :].rearrange("p r f -> p (r f)"), start=True, stop=True)
                    m.then_inc(N1["tb"], 1)
            turn_sums(N1, 0)
            turn_x(N1, 0)
            with pe.Fori(0, NCH - 1) as c:
                pe.wait_ge(N1["xT"], c + 1)
                turn_sums(N1, c + 1)
                relation_rows(c)
                turn_x(N1, c + 1)
            pe.wait_ge(N1["xT"], NCH)
            relation_rows(NCH - 1)

            pe.wait_ge(N1["eva"], NCH * CB + 1)
            pe.wait_ge(c_start, 1)
            counting_round(R1, R1N)
            pe.wait_ge(b_ev, 2 * NIT * KS + KS)

            def products(c):
                pe.wait_ge(N2["ev"], c + 1)
                pe.wait_ge(N2["eva2"], c + 1)
                for k in range(CB):
                    m = pe.matmul(ps4[:, k * 256:(k + 1) * 256], xTs[:, k * P:(k + 1) * P], W2s[:, :], start=True, stop=True)
                m.then_inc(N2["tb"], 1)
            turn_sums(N2, 0)
            turn_x(N2, 0)
            with pe.Fori(0, NCH - 1) as c:
                pe.wait_ge(N2["xT"], c + 1)
                turn_sums(N2, c + 1)
                products(c)
                turn_x(N2, c + 1)
            pe.wait_ge(N2["xT"], NCH)
            products(NCH - 1)

            pe.wait_ge(N2["ev"], NCH + 1)
            pe.wait_ge(N2["eva2"], NCH + 1)

            def expand(b, q):
                pe.wait_ge(m_oh[b], q + 1)
                for j in range(TPG):
                    m = pe.transpose(ps4[:, b * GE + j * P:b * GE + (j + 1) * P], onehot[:, b, j * P:(j + 1) * P], ident[:, :])
                m.then_inc(m_tp[b], 1)
                pe.wait_ge(m_ohT[b], q + 1)
                pe.wait_ge(m_bwin[b], 16 * q + 16)
                pe.wait_ge(m_h[b], q + 1)
                for j in range(TPG):
                    m = pe.matmul(psA[:, b * 512 + j * HID:b * 512 + (j + 1) * HID], msg[:, b, j * P:(j + 1) * P],
                                  bwin[:, b, :], start=True, stop=True)
                m.then_inc(m_exp[b], 1)

            def degrees(b, q):
                pe.wait_ge(m_dacc[b], q + 1)
                for j in range(TPG):
                    m = pe.matmul(psS[b][0:1, 0:P], ews[:, b, j:j + 1], onehot[:, b, j * P:(j + 1) * P],
                                  start=(j == 0), stop=(j == TPG - 1))
                m.then_inc(m_deg[b], 1)
            def expansion_step(it, last):
                for b in range(2):
                    if not (last and b):
                        expand(1 - b, (it + b) * nwin)
                    with pe.If(more > 0):
                        with pe.Fori(1, more + 1) as w:
                            expand(b, it * nwin + w)
                    pe.wait_ge(m_ew[b], it + 1)
                    degrees(b, it * nwin)
                    with pe.If(more > 0):
                        with pe.Fori(0, more) as w:
                            pe.wait_ge(m_oh2[b], it * more + w + 1)
                            degrees(b, it * nwin + w + 1)
            expand(0, 0)
            with pe.Fori(0, NIT - 1) as it:
                expansion_step(it, False)
            expansion_step(NIT - 1, True)
            for b in range(2):
                pe.wait_ge(m_dacc[b], NIT * nwin + 1)
            for k in range(NB):
                m = pe.matmul(ps4[:, k:k + 1], acc[0:1, k * P:(k + 1) * P], one11[:, :], start=True, stop=True)
            m.then_inc(d_t, 1)

            pe.wait_ge(d_sq, 1)
            counting_round(R2b, R2N)

            with pe.Fori(0, NCH) as c:
                pe.wait_ge(N3["st"], c + 1)
                turn_chunk(stT, N3["t1"])
                pe.wait_ge(N3["xn"], c + 1)
                turn_chunk(xn, N3["t2"])

            pe.wait_ge(N3["eva"], NCH)
            pe.wait_ge(b_ev, 4 * NIT * KS + KS)
            dense = dense_flag(pe)
            with pe.Fori(0, LAYERS) as l:
                with pe.If(dense < 1):
                    plain_round(R3, l)
                    for b in range(2):
                        pe.wait_ge(r_acc[b], (l * NIT + NIT + R3.g0) * nwin + 1)
                    pass_waits(pe)
                with pe.If(dense > 0):
                    with pe.Fori(0, NCI) as i:
                        for r in range(2):
                            pe.wait_ge(a_ready[r], (l * NCI + i) * 32 + 32)
                            pe.wait_ge(a_add[r], l * NCI + i + 1)
                            for t in range(NB):
                                if r == 0 and t % CB == 0:
                                    pe.wait_ge(x_s, l * (4 * NCH) + t // CB * 4 + 4)
                                for k in range(3):
                                    m = pe.matmul(psS[r][:, 0:CC], xs[:, t, k, :], Aring[:, r, :, t, :],
                                                  start=(t == 0 and k == 0), stop=(t == NB - 1 and k == 2))
                            m.then_inc(a_done[r], 1)
                    for r in range(2):
                        pe.wait_ge(a_add[r], l * NCI + NCI + 1)
                    pass_waits(pe)
                pe.wait_ge(l_w, l * 80 + 80)
                pass_waits(pe)
                for c in range(NCH):
                    for lo, hi in ((0, 512), (512, CW)):
                        m = pe.matmul(psA[:, lo:hi], WA[:, :], acc[:, c * CW + lo:c * CW + hi], start=True, stop=True)
                    m.then_inc(l_h, 1)
                    pe.wait_ge(l_relu, l * NCH + c + 1)
                    if c:
                        pe.wait_ge(l_acc, l * NCH + c)
                        pe.wait_ge(l_xo, l * NCH + c)
                    for k in range(CB):
                        pe.matmul(ps4[:, k * P:(k + 1) * P], xTs[:, k * P:(k + 1) * P], WB[:, :], start=True, stop=True)
                    for lo, hi in ((0, 512), (512, CW)):
                        m = pe.matmul(ps4[:, 1024 + lo:1024 + hi], WB[:, :], xTs[:, lo:hi], start=True, stop=True)
                    m.then_inc(l_o, 1)
                pe.wait_ge(l_acc, l * NCH + NCH)
                pe.wait_ge(l_xo, l * NCH + NCH)
                pass_waits(pe)

        @block.vector
        def _(dve):
            chain = [0]

            def link(ins):
                chain[0] += 1
                ins.then_inc(s_chain, 1)
                dve.wait_ge(s_chain, chain[0])

            for r in range(4):
                if r == RDST:
                    dve.memset(raw[r].bitcast(I32), -1)
                else:
                    dve.memset(raw[r], 0.0)
            for v in (next1, nextx):
                dve.memset(v.bitcast(I32), 2 * NPAD)
            dve.memset(starts[:, :, :], 0.0)
            dve.memset(starti[:, :], 0)
            dve.memset(EWb[:, :, :], 0.0)
            dve.memset(attr[:, :, :], 0.0)
            dve.memset(srci[:, NG * TPG:], 0)
            dve.memset(one11[:, :], 1.0)
            dve.memset(onec[:, :], 1.0)
            dve.memset(X[:, (NB - 1) * P:NPAD], 0.0).then_inc(s_fill, 1)
            for b in range(2):
                dve.sem_inc(r_acc[b], 1)
                dve.sem_inc(s_msg[b], 1)
                dve.sem_inc(m_h[b], 1)
                dve.sem_inc(m_dacc[b], 1)
                dve.sem_inc(b_oh[b], 1)
                dve.sem_inc(a_add[b], 1)
            dve.sem_inc(c_cnt, 1)
            for p in (N0, N2):
                dve.sem_inc(p["ev"], 1)
            dve.wait_ge(s_iota, 2)
            dve.tensor_scalar(ident[:, :], iota[:, 0:P], pcol[:, 0:1], None, ALU.is_equal).then_inc(s_ident, 1)
            dve.tensor_copy(iotaS[:, :], iota[:, 0:KS * P])
            dve.tensor_copy(iotaB[:, :], iota[:, 1:BN + 1])
            dve.wait_ge(s_load, 16 * 12)
            srcn, dstn = raw[RSRC].bitcast(I32), raw[RDST].bitcast(I32)
            ka, kb = G[:, 0, :].bitcast(I32), G[:, 1, :].bitcast(I32)
            shift_s, shift_t = (KS * P).bit_length() - 1, TB.bit_length() - 1
            link(dve.tensor_scalar(ka, srcn, KS * P - 1, None, ALU.bitwise_and))
            link(dve.tensor_copy(keyraw[:, :, 0], ka))
            link(dve.tensor_scalar(ka, srcn, shift_s - shift_t, 15 * TB, ALU.logical_shift_right, ALU.bitwise_and))
            link(dve.tensor_scalar(kb, dstn, TB - 1, None, ALU.bitwise_and))
            link(dve.scalar_tensor_tensor(keyraw[:, :, 1], ka, 1.0, kb, ALU.add, ALU.add))
            link(dve.tensor_scalar(ka, dstn, shift_t, None, ALU.logical_shift_right))
            link(dve.tensor_copy(keyraw[:, :, 2], ka))
            dve.sem_inc(c_keys, 1)
            unsorted, many = G[:, 0, :], G[:, 1, :]
            link(dve.tensor_tensor(unsorted, dstn, next1.bitcast(I32), ALU.is_gt))
            link(dve.tensor_tensor(many, dstn, nextx.bitcast(I32), ALU.is_equal))
            link(dve.tensor_tensor(many, many, unsorted, ALU.max))
            link(dve.tensor_reduce(small[:, 2:3], many, AXX, ALU.max))
            link(dve.tensor_copy(raw[RSRC], raw[RSRC].bitcast(I32)))
            dve.sem_inc(s_prep, 1)
            link(dve.tensor_copy(raw[RDST], raw[RDST].bitcast(I32)))
            dve.sem_inc(s_prep, 1)
            link(dve.tensor_copy(raw[RTYP], raw[RTYP].bitcast(I32)))
            link(dve.scalar_tensor_tensor(raw[RTYP], raw[RSRC], float(RELS), raw[RTYP], ALU.mult, ALU.add))
            dve.sem_inc(s_prep, 2)
            link(dve.tensor_scalar(msg[0:NG, 0, :], raw[RDST][0:NG, :], 0.0, float(NPAD), ALU.is_lt, ALU.mult))
            link(dve.tensor_tensor(msg[0:NG, 0, :], msg[0:NG, 0, :], raw[RDST][0:NG, :], ALU.add))
            link(dve.tensor_reduce(small[0:NG, 0:1], msg[0:NG, 0, :], AXX, ALU.min))
            link(dve.tensor_reduce(small[0:NG, 1:2], raw[RDST][0:NG, :], AXX, ALU.max))
            dve.sem_inc(s_prep, 1)
            lists = ((RSRC, srci), (RDST, dstf), (RTYP, reli), (RWGT, wedge))
            for r, to in lists:
                dve.wait_ge(s_pt, r + 1)
                link(dve.tensor_copy(to[:, 0:NG * TPG].rearrange("p (g j) -> p j g", j=TPG),
                                     ps4[:, 0:GE].rearrange("p (j g) -> p j g", j=TPG)[:, :, 0:NG]))
                dve.sem_inc(s_pe, 1)
            dve.wait_ge(s_pt, 5)
            lo, hi, span, base = (rowf[:, k, :] for k in range(4))
            link(dve.tensor_copy(lo, psA[0:1, 0:NG]))
            link(dve.tensor_tensor(span, psA[0:1, P:P + NG], lo, ALU.subtract))
            link(dve.tensor_reduce(badrow[:, 0:1], psA[0:1, 2 * P:2 * P + NG], AXX, ALU.max))
            link(dve.tensor_reduce(hi[:, 0:1], span, AXX, ALU.max))
            link(dve.tensor_scalar(hi[:, 1:2], hi[:, 0:1], float(P), None, ALU.is_lt))
            link(dve.tensor_scalar(base, lo, float(MAXBASE), hi[:, 1:2], ALU.min, ALU.mult))
            link(dve.tensor_copy(basei[:, :], base))
            link(dve.tensor_scalar(hi[:, 2:3], hi[:, 1:2], float(1 - NB), float(NB), ALU.mult, ALU.add))
            link(dve.tensor_scalar(hi[:, 3:4], hi[:, 2:3], -1.0, None, ALU.add))
            link(dve.tensor_copy(nwini[:, :], hi[:, 2:4]))
            dve.sem_inc(s_plan, 1)
            nwin, more = window_count(dve)
            dve.wait_ge(s_wload, ALLW)
            dve.tensor_scalar(mb2r[:, :], mb2r[:, :], 0.5, None, ALU.mult).then_inc(s_half, 1)

            def load_base(it, b):
                return dve.value_load(basei[0:1, bass.ds(it * 2 + b, 1)], min_val=0, max_val=MAXBASE)

            def tiles(ap):
                return ap.rearrange("p (j n) -> p j n", j=TPG)

            def columns(table, it, b):
                return table[:, bass.ds(it * (2 * TPG) + b * TPG, TPG)].unsqueeze(2).broadcast_to([P, TPG, P])

            def compare(b, base, w, it):
                return dve.tensor_tensor(tiles(onehot[:, b, :]), iota[:, window(base, w)].unsqueeze(1).broadcast_to([P, TPG, P]),
                                         columns(dstf, it, b), ALU.is_equal)

            def make_onehots(b, base, w, it, raw_count, weights):
                if weights is None:
                    compare(b, base, w, it).then_inc(r_oh[b], 1)
                else:
                    compare(b, base, w, it).then_inc(r_ohraw[b], 1)
                    dve.wait_ge(r_ohraw[b], raw_count + 1)
                    dve.tensor_tensor(tiles(onehot[:, b, :]), tiles(onehot[:, b, :]), columns(weights, it, b),
                                      ALU.mult).then_inc(r_oh[b], 1)

            def last_add(done, b, w, q, steps):
                if not isinstance(w, int):
                    dve.wait_ge(done[b], q + 1)
                elif b:
                    dve.wait_ge(done[0], steps + nwin + 1)
                else:
                    dve.wait_ge(done[1], steps + 1)

            def add_sums(b, base, w, q, q0):
                last_add(r_acc, b, w, q, q0)
                dve.wait_ge(r_seg[b], q + 2)
                at = acc[:, window(base, w)]
                dve.tensor_tensor(at, at, psS[b][:, 0:P], ALU.add).then_inc(r_acc[b], 1)

            def block_onehots(u, n):
                dve.wait_ge(b_keys[u], n * 16 + 16)
                dve.scalar_tensor_tensor(kk[:, u, :], keys[:, u, :, 2], iota[:, bass.ds(n * 2 + u, 1)], keys[:, u, :, 1],
                                         ALU.is_equal, ALU.mult).then_inc(b_kk, 1)
                dve.wait_ge(b_bank, n * (2 * KS) + (u + 1) * KS)
                for j in range(BT):
                    dve.tensor_scalar(ohS[:, u, j * KS * P:(j + 1) * KS * P], iotaS[:, :], keys[:, u, j, 0:1], None, ALU.is_equal)
                dve.wait_ge(b_kk, n * 2 + u + 1)
                for j in range(BT):
                    last = dve.tensor_scalar(ohB[:, u, j * BN:(j + 1) * BN], iotaB[:, :], kk[:, u, j:j + 1], None, ALU.is_equal)
                last.then_inc(b_oh[u], 1)

            def count_edges(it, half):
                for k in range(2 * half, 2 * half + 2):
                    m = it * 4 + k
                    dve.wait_ge(c_cnt, m + 1)
                    dve.tensor_tensor(atmost, iota[:, bass.ds(m * TB + (TB - 1), 1)].broadcast_to([P, GE]), raw[RDST],
                                      ALU.is_ge).then_inc(c_ge, 1)
                    dve.wait_ge(c_ge, m + 1)
                    dve.tensor_reduce(counts[:, bass.ds(m, 1)], atmost, AXX, ALU.add).then_inc(c_cnt, 1)

            def round_(R, weights, l=0, messages=False, n0=None):
                with dve.Fori(0, NIT) as it:
                    bases = []
                    q = (l * NIT + it + R.g0) * nwin
                    qw = (it + R.w0) * nwin
                    for b in range(2):
                        if n0 is not None:
                            block_onehots(b, it + n0)
                        bases.append(load_base(it, b))
                        make_onehots(b, bases[b], 0, it, qw, weights)
                    for b in range(2):
                        if messages:
                            dve.wait_ge(R.gathered[b], it * (16 * TPG) + 16 * TPG)
                            dve.wait_ge(s_ew[b], it + 1)
                            dve.tensor_tensor(msg[:, b, :], G[:, b, :], ps4[:, b * GE:(b + 1) * GE], ALU.mult).then_inc(s_msg[b], 1)
                            count_edges(it, b)
                        add_sums(b, bases[b], 0, q, q)
                        with dve.If(more > 0):
                            with dve.Fori(1, more + 1) as w:
                                make_onehots(b, bases[b], w, it, qw + w, weights)
                                add_sums(b, bases[b], w, q + w, q)

            def spread(ap):
                return ap.unsqueeze(1).broadcast_to([P, CB, D])

            def per_node(ap):
                return ap.unsqueeze(2).broadcast_to([P, CB, D])

            def stepper(p, c):
                k = [0]

                def step(ins):
                    k[0] += 1
                    ins.then_inc(p["dv"], 1)
                    dve.wait_ge(p["dv"], c * p["steps"] + k[0])
                return step, k

            def normalise(p, c, step, k, between=None):
                y3 = blocks(y[:, :])
                step(dve.tensor_reduce(stat[:, 0, :], y3, AXX, ALU.add))
                step(dve.tensor_scalar(stat[:, 0, :], stat[:, 0, :], -1.0 / D, None, ALU.mult))
                step(dve.tensor_tensor(y3, y3, per_node(stat[:, 0, :]), ALU.add))
                assert k[0] == p["centred"]
                if between is not None:
                    between()
                dve.wait_ge(p["sq"], c * 2 + 1)
                step(dve.tensor_reduce(stat[:, 1, :], blocks(sq[:, :]), AXX, ALU.add))
                step(dve.tensor_scalar(stat[:, 1, :], stat[:, 1, :], 1.0 / D, EPS, ALU.mult, ALU.add))
                assert k[0] == p["varied"]
                dve.wait_ge(p["sq"], c * 2 + 2)
                step(dve.reciprocal(stat[:, 3, :], stat[:, 2, :]))
                assert k[0] == p["steps"]
                if p is N3:
                    dve.wait_ge(N3["stored"], c + 1)
                dve.tensor_tensor(blocks(xn[:, :]), y3, per_node(stat[:, 3, :]), ALU.mult).then_inc(p["xn"], 1)

            def chunk(table, c):
                return table[:, bass.ds(c * CW, CW)]

            dve.wait_ge(s_xload, 32)
            with dve.Fori(0, NCH) as c:
                dve.tensor_copy(xn[:, :], chunk(X, c)).then_inc(N0["xn"], 1)
                dve.wait_ge(N0["tb"], c + 1)
                dve.wait_ge(N0["stored"], c + 1)
                dve.tensor_copy(msg[:, 0, 0:CW], ps4[:, 0:CW]).then_inc(N0["ev"], 1)

            dve.wait_ge(N0["stored"], NCH + 1)
            dve.wait_ge(s_zero, 1)
            round_(R0, None, messages=True)

            dve.wait_ge(s_pt, 6)
            first, size = starts[:, 0, :], starts[:, 1, :]
            link(dve.tensor_scalar(first[:, 1:NT + 1], psS[0][0:1, 0:NT], -float(PADDED), None, ALU.add))
            link(dve.tensor_tensor(size[:, 0:NT], first[:, 1:NT + 1], first[:, 0:NT], ALU.subtract))
            link(dve.tensor_reduce(badrow[:, 1:2], size[:, 0:NT], AXX, ALU.max))
            link(dve.tensor_scalar(badrow[:, 1:2], badrow[:, 1:2], float(BE), None, ALU.is_gt))
            link(dve.tensor_tensor(badrow[:, 0:1], badrow[:, 0:1], badrow[:, 1:2], ALU.max))
            link(dve.tensor_scalar(badrow[:, 0:1], badrow[:, 0:1], 0.0, None, ALU.is_equal))
            link(dve.tensor_copy(densei[:, :], badrow[:, 0:1]))
            link(dve.tensor_scalar(first[:, 0:NT], first[:, 0:NT], float(E - BE), None, ALU.min))
            link(dve.tensor_copy(starti[:, 0:NT], first[:, 0:NT]))
            dve.sem_inc(c_start, 1)

            with dve.Fori(0, NCH) as c:
                step, k = stepper(N1, c)
                dve.wait_ge(N1["t1"], c + 1)
                step(dve.tensor_tensor(y[:, :], psA[:, 0:CW], chunk(X, c), ALU.add))
                step(dve.tensor_tensor(blocks(y[:, :]), blocks(y[:, :]), spread(b0r[:, :]), ALU.add))
                normalise(N1, c, step, k)

            dve.wait_ge(s_zero, 2)
            dve.wait_ge(N1["stored"], NCH * CB + 3)
            round_(R1, wedge, n0=R1N)

            def update(c, between=None):
                step, k = stepper(N2, c)
                dve.wait_ge(N2["t1"], c + 1)
                step(dve.tensor_tensor(blocks(y[:, :]), blocks(psA[:, 0:CW]), spread(b1r[:, :]), ALU.add))
                step(dve.scalar_tensor_tensor(y[:, :], y[:, :], 0.0, chunk(X, c), ALU.max, ALU.add))
                normalise(N2, c, step, k, between)

            def evacuate_rows(c):
                dve.wait_ge(N2["tb"], c + 1)
                dve.wait_ge(N2["stored"], c + 1)
                dve.tensor_tensor(blocks(msg[:, 0, 0:CW])[:, :, 0:HID],
                                  ps4[:, 0:CB * 256].rearrange("p (b n) -> p b n", n=256)[:, :, 0:HID],
                                  mb1r[:, :].unsqueeze(1).broadcast_to([P, CB, HID]), ALU.add).then_inc(N2["ev"], 1)
            update(0)
            with dve.Fori(0, NCH - 1) as c:
                update(c + 1, lambda: evacuate_rows(c))
            evacuate_rows(NCH - 1)

            dve.wait_ge(s_zero, 3)

            def add_expanded(b, q, first):
                dve.wait_ge(m_exp[b], q + 2)
                h = hid[:, b, :].rearrange("p (j n) -> p j n", n=HID)
                dve.tensor_tensor(h, blocks(G[:, b, :])[:, :, 0:HID] if first else h, psA[:, b * 512:b * 512 + TPG * HID].rearrange("p (j n) -> p j n", n=HID), ALU.add).then_inc(m_h[b], 1)

            def add_degrees(b, base, w, q, q0, first):
                last_add(m_dacc, b, 0 if first else w, q, q0)
                dve.wait_ge(m_deg[b], q + 1)
                at = acc[0:1, window(base, w)]
                dve.tensor_tensor(at, at, psS[b][0:1, 0:P], ALU.add).then_inc(m_dacc[b], 1)

            def times(it, count):
                return 0 if isinstance(it, int) and it == 0 else it * count

            def finish_degrees(b, it):
                base, q = load_base(it, b), times(it, nwin)
                add_degrees(b, base, more, q, q, True)
                with dve.If(more > 0):
                    with dve.Fori(0, more) as w:
                        compare(b, base, w, it).then_inc(m_oh2[b], 1)
                        add_degrees(b, base, w, q + w + 1, q, False)

            def edge_mlp_step(it, first, last):
                q = times(it, nwin)
                for b in range(2):
                    dve.wait_ge(m_gath[b], it * (16 * TPG) + 16 * TPG)
                    add_expanded(b, q, True)
                    if not (first and b == 0):
                        finish_degrees(1 - b, it - (1 - b))
                    if not (last and b):
                        compare(1 - b, load_base(it + b, 1 - b), 0, it + b).then_inc(m_oh[1 - b], 1)
                    with dve.If(more > 0):
                        base = load_base(it, b)
                        with dve.Fori(1, more + 1) as w:
                            compare(b, base, w, it).then_inc(m_oh[b], 1)
                            dve.wait_ge(m_h[b], q + w + 1)
                            add_expanded(b, q + w, False)
                    dve.wait_ge(m_gelu[b], it + 1)
                    e3 = tiles(hid[:, b, :])
                    dve.tensor_tensor(e3, e3, w2r[:, :].unsqueeze(1).broadcast_to([P, TPG, HID]), ALU.mult).then_inc(m_dot[b], 1)
                    dve.wait_ge(m_dot[b], it * 2 + 1)
                    dve.tensor_reduce(zed[:, b, :], e3, AXX, ALU.add).then_inc(m_dot[b], 1)
                    dve.wait_ge(m_tanh[b], it + 1)
                    dve.tensor_scalar(ews[:, b, :], tanhz[:, b, :], 0.5, 0.5, ALU.mult, ALU.add).then_inc(m_ew[b], 1)
                    dve.tensor_scalar(ewt[:, bass.ds(it * (2 * TPG) + b * TPG, TPG)], tanhz[:, b, :], 0.5, 0.5,
                                      ALU.mult, ALU.add).then_inc(m_ewt, 1)
            compare(0, load_base(0, 0), 0, 0).then_inc(m_oh[0], 1)
            edge_mlp_step(0, True, False)
            with dve.Fori(1, NIT - 1) as it:
                edge_mlp_step(it, False, False)
            edge_mlp_step(NIT - 1, False, True)
            finish_degrees(1, NIT - 1)

            dve.wait_ge(d_sq, 1)
            dve.reciprocal(dinv[:, :], droot[:, :]).then_inc(d_v, 1)
            dve.wait_ge(d_v, 1)
            dve.tensor_tensor(blocks(XT2[:, :]), blocks(XT2[:, :]), dinv[:, :].unsqueeze(2).broadcast_to([P, NB, D]),
                              ALU.mult).then_inc(d_v, 1)
            dve.wait_ge(m_ewt, NG)
            dve.wait_ge(s_zero, 4)
            round_(R2b, ewt, n0=R2N)

            def split(v, c, count):
                hi, mid, lo = (xs[:, bass.ds(c * CB, CB), k, :] for k in range(3))
                rest = blocks(sq[:, :])
                for s, ins in enumerate((lambda: dve.tensor_copy(hi, v),
                                         lambda: dve.tensor_tensor(rest, v, hi, ALU.subtract),
                                         lambda: dve.tensor_copy(mid, rest),
                                         lambda: dve.tensor_tensor(lo, rest, mid, ALU.subtract))):
                    ins().then_inc(x_s, 1)
                    dve.wait_ge(x_s, count * 4 + s + 1)

            dve.wait_ge(d_v, 2)
            for u in range(2):
                dve.wait_ge(b_free[u], NSTEP + 1)
            with dve.Fori(0, NCH) as c:
                step, k = stepper(N3, c)
                dve.wait_ge(N3["t1"], c + 1)
                step(dve.tensor_tensor(y[:, :], psA[:, 0:CW], chunk(XT2, c), ALU.add))
                step(dve.tensor_tensor(blocks(y[:, :]), blocks(y[:, :]), per_node(dinv[:, bass.ds(c * CB, CB)]), ALU.mult))
                step(dve.tensor_tensor(blocks(y[:, :]), blocks(y[:, :]), spread(cbr[:, :]), ALU.add))
                step(dve.tensor_tensor(y[:, :], y[:, :], chunk(X, c), ALU.add))
                normalise(N3, c, step, k)
                dve.wait_ge(N3["xn"], c + 1)
                split(blocks(xn[:, :]), c, c)

            dve.wait_ge(N3["eva"], NCH)
            dve.wait_ge(N3["stored"], NCH + 1)
            dense = dense_flag(dve)
            with dve.Fori(0, LAYERS) as l:
                with dve.If(dense < 1):
                    round_(R3, None, l=l)
                with dve.If(dense > 0):
                    with dve.Fori(0, NCI) as i:
                        for r in range(2):
                            dve.wait_ge(a_done[r], l * NCI + i + 2)
                            at = acc[:, bass.ds(i * (2 * CC) + r * CC, CC)]
                            dve.tensor_tensor(at, at, psS[r][:, 0:CC], ALU.add).then_inc(a_add[r], 1)
                dve.wait_ge(l_w, l * 80 + 80)
                pass_waits(dve)
                for c in range(NCH):
                    lc = l * NCH + c
                    stage = blocks(l3stage[c % 2][:, :])
                    dve.wait_ge(l_o, lc + 1)
                    dve.wait_ge(l_stored, lc + (0 if c else 1))
                    dve.tensor_tensor(stage, blocks(ps4[:, 0:CW]), spread(l3b2r[:, :]), ALU.add).then_inc(l_xo, 1)
                    dve.wait_ge(l_xo, lc + 1)
                    split(stage, c, lc + NCH)
                dve.wait_ge(l_acc, l * NCH + NCH)
                pass_waits(dve)

            dve.wait_ge(l_stored, LAYERS * NCH + 1)
            dve.wait_ge(s_xload, 48)
            with dve.Fori(0, NCH) as c:
                step, k = stepper(NF, c)
                dve.wait_ge(f_part, c + 1)
                step(dve.tensor_tensor(y[:, :], chunk(XT2, c), chunk(X, c), ALU.add))
                normalise(NF, c, step, k)
                dve.wait_ge(NF["xn"], c + 1)
                pass_waits(dve)


_INS = ['x', 'src', 'dst', 'edge_attr_16', 'edge_type_8', 'edge_weight', 'L0_gnn_W', 'L0_gnn_edge_w', 'L0_gnn_b',
        'L1_gnn_weight', 'L1_gnn_bias', 'L2_gnn_mlp_w1', 'L2_gnn_mlp_b1', 'L2_gnn_mlp_w2', 'L2_gnn_mlp_b2',
        'L2_gnn_conv_w', 'L2_gnn_conv_b', 'L3_gnn_W1', 'L3_gnn_b1', 'L3_gnn_W2', 'L3_gnn_b2']
_OUTS = [((6250, 128), 'float32')]


def kernel(**inputs):
    import numpy as _np
    import concourse.bacc as _bacc
    from concourse import mybir as _mybir
    from concourse.bass_utils import run_bass_kernel_spmd as _run

    nc = _bacc.Bacc("TRN2", target_bir_lowering=False, num_devices=1)
    arrays, args = {}, []
    for name in _INS:
        a = _np.ascontiguousarray(inputs[name])
        arrays[f"in_{name}_dram"] = a
        args.append(nc.dram_tensor(f"in_{name}_dram", a.shape, _mybir.dt.from_np(a.dtype), kind="ExternalInput").ap())
    for i, (shape, dtype) in enumerate(_OUTS):
        dt = _mybir.dt.from_np(_np.dtype(dtype))
        args.append(nc.dram_tensor(f"out_{i}_dram", shape, dt, kind="ExternalOutput").ap())
    gnn_program(nc, *args)
    r = _run(nc, [arrays], core_ids=[0])
    got = tuple(r.results[0][f"out_{i}_dram"] for i in range(len(_OUTS)))
    return got[0]
```
